# Optimizing a Trainium2 kernel written in Bass

```python
import numpy as np
import jax
import jax.numpy as jnp

def _softmax(x, axis=-1):
    return jax.nn.softmax(x, axis=axis)

def _gelu(x):
    return jax.nn.gelu(x, approximate=True)

def _silu(x):
    return jax.nn.silu(x)

def _sigmoid(x):
    return jax.nn.sigmoid(x)

def _layernorm(x, axis=-1, eps=1e-05):
    m = jnp.mean(x, axis=axis, keepdims=True)
    v = jnp.var(x, axis=axis, keepdims=True)
    return (x - m) / jnp.sqrt(v + eps)

def _scatter_add(tgt, idx, src, axis=0):
    return tgt.at[idx].add(src)

def _segment_sum(src, seg, n):
    return jax.ops.segment_sum(src, seg, n)
kernel_name = 'mk_decoder_preln_d2_seqx_r4_6f22cf'

def setup_inputs(seed: int=0):
    np.random.seed(seed)
    _w = jnp.asarray

    def _rec_inputs():
        import jax
        import jax.numpy as jnp
        _rk = jax.random.key(seed)
        x = -0.0003929 + 0.9999 * jax.random.normal(jax.random.fold_in(_rk, 1), (2, 512, 512), jnp.float32)
        _lenS = 512 - jax.random.randint(jax.random.fold_in(_rk, 7), (2,), 0, max(1, 512 // 4) + 1, jnp.int32)
        _lenS2 = 1024 - jax.random.randint(jax.random.fold_in(_rk, 8), (2,), 0, max(1, 1024 // 4) + 1, jnp.int32)
        _ctx_2048P = jax.random.normal(jax.random.fold_in(_rk, 11), (2, 16, 512), jnp.float32)
        _ctx_2048c = jax.random.dirichlet(jax.random.fold_in(_rk, 511), 0.3 * jnp.ones((16,), jnp.float32), (2, 1024))
        _ctx_2048t = jnp.einsum('bsk,bkd->bsd', _ctx_2048c, _ctx_2048P)
        _ctx_2048t = _ctx_2048t * jax.lax.rsqrt(jnp.mean(jnp.square(_ctx_2048t)) + 1e-12) * 0.953939
        ctx_2048 = -0.000514642 + 1.00011 * (_ctx_2048t + 0.3 * jax.random.normal(jax.random.fold_in(_rk, 611), (2, 1024, 512), jnp.float32))
        return (x, ctx_2048)
    x, ctx_2048 = _rec_inputs()

    def _L0_attn_setup():
        import jax, jax.numpy as jnp
        import numpy as np
        HIDDEN = 512
        INTER = 1024
        KCONV = 1024
        DT_RANK = 128
        SSM_N = 16
        B_SZ, SEQ = (2, 1024)
        key = jax.random.key(seed)
        ks = jax.random.split(key, 8)
        s = 0.02
        return {'hidden_states': jax.random.normal(ks[0], (B_SZ, SEQ, HIDDEN), jnp.float32), 'W_in': jax.random.normal(ks[1], (2 * INTER, HIDDEN), jnp.float32) * s, 'conv_w': jax.random.normal(ks[2], (INTER, KCONV), jnp.float32) * s, 'W_x': jax.random.normal(ks[3], (DT_RANK + 2 * SSM_N, INTER), jnp.float32) * s, 'W_dt': jax.random.normal(ks[4], (INTER, DT_RANK), jnp.float32) * s, 'b_dt': jax.random.normal(ks[5], (INTER,), jnp.float32) * s, 'D': jnp.ones((INTER,), jnp.float32), 'W_out': jax.random.normal(ks[6], (HIDDEN, INTER), jnp.float32) * s}
    _L0_attn_all = _L0_attn_setup()
    _L0_attn_in = {k: v for k, v in _L0_attn_all.items() if k in ('W_in', 'conv_w', 'W_x', 'W_dt', 'b_dt', 'D', 'W_out')}
    del _L0_attn_all

    def _L0_xattn_setup():
        import jax, jax.numpy as jnp
        import numpy as np
        NUM_HEADS = 16

        def _qdq(x):
            s = jnp.maximum(jnp.max(jnp.abs(x), axis=-1, keepdims=True) / 127.0, 1e-08)
            return jnp.clip(jnp.round(x / s), -127.0, 127.0) * s
        key = jax.random.key(seed)
        ks = jax.random.split(key, 8)
        B, N, M, D = (2, 1024, 128, 512)
        w_std = 0.02
        return {'x': jax.random.normal(ks[0], (B, N, D), jnp.float32), 'cond': jax.random.normal(ks[1], (B, M, D), jnp.float32), 'wq': jax.random.normal(ks[2], (D, D), jnp.float32) * w_std, 'bq': jax.random.normal(ks[3], (D,), jnp.float32) * w_std, 'wkv': jax.random.normal(ks[4], (2 * D, D), jnp.float32) * w_std, 'bkv': jax.random.normal(ks[5], (2 * D,), jnp.float32) * w_std, 'wp': jax.random.normal(ks[6], (D, D), jnp.float32) * w_std, 'bp': jax.random.normal(ks[7], (D,), jnp.float32) * w_std}
    _L0_xattn_all = _L0_xattn_setup()
    _L0_xattn_in = {k: v for k, v in _L0_xattn_all.items() if k in ('wq', 'bq', 'wkv', 'bkv', 'wp', 'bp')}
    del _L0_xattn_all

    def _L0_ffn_setup():
        import jax, jax.numpy as jnp
        import numpy as np
        B, S, EMB = (4, 512, 512)
        LAT, HID = (128, 256)
        E, K = (16, 8)
        SCALE = 2.5

        def _w(key, shape, fan_in):
            return jax.random.normal(key, shape, jnp.float32) * fan_in ** (-0.5)

        def _sqrelu(x):
            return jnp.square(jax.nn.relu(x))
        key = jax.random.key(seed)
        ks = jax.random.split(key, 11)
        return {'x': jax.random.normal(ks[0], (B, S, EMB), jnp.float32), 'sw1': _w(ks[1], (HID, EMB), EMB), 'swg': _w(ks[2], (HID, EMB), EMB), 'sw2': _w(ks[3], (EMB, HID), HID), 'rw1': _w(ks[4], (E, HID, LAT), LAT), 'rwg': _w(ks[5], (E, HID, LAT), LAT), 'rw2': _w(ks[6], (E, LAT, HID), HID), 'Wg': _w(ks[7], (E, EMB), EMB), 'Wdown': _w(ks[8], (LAT, EMB), EMB), 'Wup': _w(ks[9], (EMB, LAT), LAT), 'biases': jnp.zeros((E,), jnp.float32)}
    _L0_ffn_all = _L0_ffn_setup()
    _L0_ffn_in = {k: v for k, v in _L0_ffn_all.items() if k in ('sw1', 'swg', 'sw2', 'rw1', 'rwg', 'rw2', 'Wg', 'Wdown', 'Wup', 'biases')}
    del _L0_ffn_all

    def _L1_attn_setup():
        import jax, jax.numpy as jnp
        import numpy as np
        H = 32
        D = 64
        BS = 64
        LAYER_IDX = 0
        NUM_LAYERS = 32
        EPS = 1e-05

        def _decay_buffers():
            base = 1.0 / 2.0 ** (8.0 / H)
            rate = base ** (jnp.arange(H, dtype=jnp.float32) + 1.0)
            factor = 1.0 - LAYER_IDX / (NUM_LAYERS - 1 + 1e-05) + 1e-05
            slope = (rate * factor)[:, None, None]
            r = jnp.arange(BS, dtype=jnp.float32) + 1.0
            query_decay = jnp.exp(-slope * r[:, None])
            key_decay = jnp.exp(-slope * (BS - r[:, None]))
            dd = r[:, None] - r[None, :]
            dd = slope * dd[None, :, :]
            dd = jnp.where(dd >= 0, -dd, -jnp.inf)
            diagonal_decay = jnp.exp(dd)[None]
            block_decay = jnp.exp(-slope * BS)
            return (slope, query_decay, key_decay, diagonal_decay, block_decay)

        def _rmsnorm(x, w):
            v = jnp.mean(x.astype(jnp.float32) ** 2, axis=-1, keepdims=True)
            return (x * jax.lax.rsqrt(v + EPS)).astype(x.dtype) * w
        key = jax.random.key(seed)
        ks = jax.random.split(key, 4)
        b, s, hid = (2, 1024, 512)
        return {'hidden_states': jax.random.normal(ks[0], (b, s, hid), jnp.float32), 'qkv_w': jax.random.normal(ks[1], (3 * H * D, hid), jnp.float32) * 0.02, 'out_w': jax.random.normal(ks[2], (hid, H * D), jnp.float32) * 0.02, 'gate_w': jax.random.normal(ks[3], (H * D, hid), jnp.float32) * 0.02, 'norm_w': jnp.ones((H * D,), jnp.float32)}
    _L1_attn_all = _L1_attn_setup()
    _L1_attn_in = {k: v for k, v in _L1_attn_all.items() if k in ('qkv_w', 'out_w', 'gate_w', 'norm_w')}
    del _L1_attn_all

    def _L1_xattn_setup():
        import jax, jax.numpy as jnp
        import numpy as np
        EPS = 1e-06
        NUM_HEADS = 16

        def _feature_map(x):
            return jnp.where(x > 0, x + 1.0, jnp.exp(x))
        key = jax.random.key(seed)
        ks = jax.random.split(key, 7)
        B, L, S, D = (4, 1024, 1024, 512)
        sc = 1.0 / np.sqrt(D)
        return {'query': jax.random.normal(ks[0], (B, L, D), jnp.float32), 'kv': jax.random.normal(ks[1], (B, S, D), jnp.float32), 'Wq': jax.random.normal(ks[2], (D, D), jnp.float32) * sc, 'Wg': jax.random.normal(ks[3], (D, D), jnp.float32) * sc, 'bg': jnp.ones((D,), jnp.float32), 'Wkv': jax.random.normal(ks[4], (2 * D, D), jnp.float32) * sc, 'Wo': jax.random.normal(ks[5], (D, D), jnp.float32) * sc}
    _L1_xattn_all = _L1_xattn_setup()
    _L1_xattn_in = {k: v for k, v in _L1_xattn_all.items() if k in ('Wq', 'Wg', 'bg', 'Wkv', 'Wo')}
    del _L1_xattn_all

    def _L1_ffn_setup():
        import jax, jax.numpy as jnp
        import numpy as np
        _FP8_MAX = 448.0
        _BLOCK = 32
        _EPS = 1e-30

        def _mx_dequant(t):
            rows, feat = t.shape
            blocks = t.reshape(rows, feat // _BLOCK, _BLOCK)
            max_abs = jnp.max(jnp.abs(blocks), axis=-1)
            scales = jnp.maximum(max_abs / _FP8_MAX, _EPS)
            q = (blocks / scales[..., None]).astype(jnp.float8_e4m3fn).astype(jnp.float32)
            return (q * scales[..., None]).reshape(rows, feat)

        def _mx_linear(x2d, w):
            return _mx_dequant(x2d) @ _mx_dequant(w).T
        key = jax.random.key(seed)
        k1, k2, k3, k4 = jax.random.split(key, 4)
        B, S, H, I = (2, 256, 512, 2048)
        return {'x': jax.random.normal(k1, (B, S, H), dtype=jnp.float32), 'gate_w': jax.random.normal(k2, (I, H), dtype=jnp.float32) * 0.02, 'up_w': jax.random.normal(k3, (I, H), dtype=jnp.float32) * 0.02, 'down_w': jax.random.normal(k4, (H, I), dtype=jnp.float32) * 0.02}
    _L1_ffn_all = _L1_ffn_setup()
    _L1_ffn_in = {k: v for k, v in _L1_ffn_all.items() if k in ('gate_w', 'up_w', 'down_w')}
    del _L1_ffn_all
    return {'x': x, 'ctx_2048': ctx_2048, 'L0_attn_W_in': _L0_attn_in['W_in'], 'L0_attn_conv_w': _L0_attn_in['conv_w'], 'L0_attn_W_x': _L0_attn_in['W_x'], 'L0_attn_W_dt': _L0_attn_in['W_dt'], 'L0_attn_b_dt': _L0_attn_in['b_dt'], 'L0_attn_D': _L0_attn_in['D'], 'L0_attn_W_out': _L0_attn_in['W_out'], 'L0_xattn_wq': _L0_xattn_in['wq'], 'L0_xattn_bq': _L0_xattn_in['bq'], 'L0_xattn_wkv': _L0_xattn_in['wkv'], 'L0_xattn_bkv': _L0_xattn_in['bkv'], 'L0_xattn_wp': _L0_xattn_in['wp'], 'L0_xattn_bp': _L0_xattn_in['bp'], 'L0_ffn_sw1': _L0_ffn_in['sw1'], 'L0_ffn_swg': _L0_ffn_in['swg'], 'L0_ffn_sw2': _L0_ffn_in['sw2'], 'L0_ffn_rw1': _L0_ffn_in['rw1'], 'L0_ffn_rwg': _L0_ffn_in['rwg'], 'L0_ffn_rw2': _L0_ffn_in['rw2'], 'L0_ffn_Wg': _L0_ffn_in['Wg'], 'L0_ffn_Wdown': _L0_ffn_in['Wdown'], 'L0_ffn_Wup': _L0_ffn_in['Wup'], 'L0_ffn_biases': _L0_ffn_in['biases'], 'L1_attn_qkv_w': _L1_attn_in['qkv_w'], 'L1_attn_out_w': _L1_attn_in['out_w'], 'L1_attn_gate_w': _L1_attn_in['gate_w'], 'L1_attn_norm_w': _L1_attn_in['norm_w'], 'L1_xattn_Wq': _L1_xattn_in['Wq'], 'L1_xattn_Wg': _L1_xattn_in['Wg'], 'L1_xattn_bg': _L1_xattn_in['bg'], 'L1_xattn_Wkv': _L1_xattn_in['Wkv'], 'L1_xattn_Wo': _L1_xattn_in['Wo'], 'L1_ffn_gate_w': _L1_ffn_in['gate_w'], 'L1_ffn_up_w': _L1_ffn_in['up_w'], 'L1_ffn_down_w': _L1_ffn_in['down_w']}

def reference(x, ctx_2048, L0_attn_W_in, L0_attn_conv_w, L0_attn_W_x, L0_attn_W_dt, L0_attn_b_dt, L0_attn_D, L0_attn_W_out, L0_xattn_wq, L0_xattn_bq, L0_xattn_wkv, L0_xattn_bkv, L0_xattn_wp, L0_xattn_bp, L0_ffn_sw1, L0_ffn_swg, L0_ffn_sw2, L0_ffn_rw1, L0_ffn_rwg, L0_ffn_rw2, L0_ffn_Wg, L0_ffn_Wdown, L0_ffn_Wup, L0_ffn_biases, L1_attn_qkv_w, L1_attn_out_w, L1_attn_gate_w, L1_attn_norm_w, L1_xattn_Wq, L1_xattn_Wg, L1_xattn_bg, L1_xattn_Wkv, L1_xattn_Wo, L1_ffn_gate_w, L1_ffn_up_w, L1_ffn_down_w):
    import jax
    import jax.numpy as jnp

    def _L0_attn_ref(hidden_states, W_in, conv_w, W_x, W_dt, b_dt, D, W_out):
        import jax, jax.numpy as jnp
        import numpy as np
        HIDDEN = 512
        INTER = 1024
        KCONV = 1024
        DT_RANK = 128
        SSM_N = 16
        B_SZ, SEQ = (2, 1024)
        xz = jnp.einsum('bsh,ih->bsi', hidden_states, W_in)
        x, z = jnp.split(xz, 2, axis=-1)
        x = jnp.einsum('bsk,ik->bsi', x, conv_w)
        x_proj = jnp.einsum('bsi,pi->bsp', x, W_x)
        delta_raw = x_proj[..., :DT_RANK]
        B = x_proj[..., DT_RANK:DT_RANK + SSM_N]
        C = x_proj[..., DT_RANK + SSM_N:]
        delta = jax.nn.softplus(jnp.einsum('bsr,ir->bsi', delta_raw, W_dt))
        y = x * D
        z = jax.nn.silu(z)
        return jnp.einsum('bsi,hi->bsh', y * z, W_out)

    def _L0_xattn_ref(x, cond, wq, bq, wkv, bkv, wp, bp):
        import jax, jax.numpy as jnp
        import numpy as np
        NUM_HEADS = 16

        def _qdq(x):
            s = jnp.maximum(jnp.max(jnp.abs(x), axis=-1, keepdims=True) / 127.0, 1e-08)
            return jnp.clip(jnp.round(x / s), -127.0, 127.0) * s
        B, N, C = x.shape
        M = cond.shape[1]
        H = NUM_HEADS
        Dh = C // H
        q = _qdq(x) @ _qdq(wq).T + bq
        kv = cond @ wkv.T + bkv
        k, v = jnp.split(kv, 2, axis=-1)
        q = q.reshape(B, N, H, Dh)
        k = k.reshape(B, M, H, Dh)
        v = v.reshape(B, M, H, Dh)
        scale = 1.0 / np.sqrt(Dh)
        attn = jax.nn.softmax(jnp.einsum('bnhd,bmhd->bhnm', q, k) * scale, axis=-1)
        o = jnp.einsum('bhnm,bmhd->bnhd', attn, v).reshape(B, N, C)
        out = _qdq(o) @ _qdq(wp).T + bp
        return out

    def _L0_ffn_ref(x, sw1, swg, sw2, rw1, rwg, rw2, Wg, Wdown, Wup, biases):
        import jax, jax.numpy as jnp
        import numpy as np
        B, S, EMB = (4, 512, 512)
        LAT, HID = (128, 256)
        E, K = (16, 8)
        SCALE = 2.5

        def _w(key, shape, fan_in):
            return jax.random.normal(key, shape, jnp.float32) * fan_in ** (-0.5)

        def _sqrelu(x):
            return jnp.square(jax.nn.relu(x))
        b, s, d = x.shape
        x2 = x.reshape(-1, d)
        shared = x2 @ sw1.T * _sqrelu(x2 @ swg.T) @ sw2.T
        xl = x2 @ Wdown.T
        probas = jax.nn.sigmoid(x2 @ Wg.T)
        _, idx = jax.lax.top_k(probas + biases, K)
        p = jnp.take_along_axis(probas, idx, axis=-1)
        p = p / p.sum(-1, keepdims=True) * SCALE
        T = x2.shape[0]
        w_dense = jnp.zeros((T, E), x2.dtype).at[jnp.arange(T)[:, None], idx].add(p)
        acc = jnp.zeros_like(xl)
        for e in range(E):
            ye = xl @ rw1[e].T * _sqrelu(xl @ rwg[e].T) @ rw2[e].T
            acc = acc + w_dense[:, e:e + 1] * ye
        out = shared + acc @ Wup.T
        return out.reshape(b, s, d)

    def _L1_attn_ref(hidden_states, qkv_w, out_w, gate_w, norm_w):
        import jax, jax.numpy as jnp
        import numpy as np
        H = 32
        D = 64
        BS = 64
        LAYER_IDX = 0
        NUM_LAYERS = 32
        EPS = 1e-05

        def _decay_buffers():
            base = 1.0 / 2.0 ** (8.0 / H)
            rate = base ** (jnp.arange(H, dtype=jnp.float32) + 1.0)
            factor = 1.0 - LAYER_IDX / (NUM_LAYERS - 1 + 1e-05) + 1e-05
            slope = (rate * factor)[:, None, None]
            r = jnp.arange(BS, dtype=jnp.float32) + 1.0
            query_decay = jnp.exp(-slope * r[:, None])
            key_decay = jnp.exp(-slope * (BS - r[:, None]))
            dd = r[:, None] - r[None, :]
            dd = slope * dd[None, :, :]
            dd = jnp.where(dd >= 0, -dd, -jnp.inf)
            diagonal_decay = jnp.exp(dd)[None]
            block_decay = jnp.exp(-slope * BS)
            return (slope, query_decay, key_decay, diagonal_decay, block_decay)

        def _rmsnorm(x, w):
            v = jnp.mean(x.astype(jnp.float32) ** 2, axis=-1, keepdims=True)
            return (x * jax.lax.rsqrt(v + EPS)).astype(x.dtype) * w
        b, s, hid = hidden_states.shape
        nb = s // BS
        _, qd, kd, dd, bd = _decay_buffers()
        qkv = jax.nn.silu(hidden_states @ qkv_w.T)
        qkv = qkv.reshape(b, s, H, 3 * D)
        q, k, v = jnp.split(qkv, 3, axis=-1)

        def to_blocks(t):
            return t.transpose(0, 2, 1, 3).reshape(b, H, nb, BS, D).transpose(2, 0, 1, 3, 4)
        qb, kb, vb = (to_blocks(q), to_blocks(k), to_blocks(v))
        qd_ = qd[None]
        kd_ = kd[None]
        bd_ = bd[None]

        def step(state, blk):
            qi, ki, vi = blk
            aw = jnp.einsum('bhid,bhjd->bhij', qi, ki) * dd
            intra = jnp.einsum('bhij,bhjd->bhid', aw, vi)
            inter = jnp.einsum('bhid,bhde->bhie', qi * qd_, state)
            new_state = state * bd_ + jnp.einsum('bhsd,bhse->bhde', ki * kd_, vi)
            return (new_state, intra + inter)
        state0 = jnp.zeros((b, H, D, D), hidden_states.dtype)
        _, ys = jax.lax.scan(step, state0, (qb, kb, vb))
        attn = ys.transpose(1, 2, 0, 3, 4).reshape(b, H, s, D)
        attn = attn.transpose(0, 2, 1, 3).reshape(b, s, H * D)
        attn = _rmsnorm(attn, norm_w)
        gate = jax.nn.sigmoid(hidden_states @ gate_w.T)
        return gate * attn @ out_w.T

    def _L1_xattn_ref(query, kv, Wq, Wg, bg, Wkv, Wo):
        import jax, jax.numpy as jnp
        import numpy as np
        EPS = 1e-06
        NUM_HEADS = 16

        def _feature_map(x):
            return jnp.where(x > 0, x + 1.0, jnp.exp(x))
        B, L, D = query.shape
        S = kv.shape[1]
        H = NUM_HEADS
        hd = D // H
        q = query @ Wq.T
        gate = jax.nn.sigmoid(query @ Wg.T + bg)
        kvp = kv @ Wkv.T
        k, v = jnp.split(kvp, 2, axis=-1)
        q = _feature_map(q.reshape(B, L, H, hd).transpose(0, 2, 1, 3))
        k = _feature_map(k.reshape(B, S, H, hd).transpose(0, 2, 1, 3))
        v = v.reshape(B, S, H, hd).transpose(0, 2, 1, 3)
        kv_summary = jnp.einsum('bhsd,bhse->bhde', k, v)
        k_sum = k.sum(axis=-2)
        z = 1.0 / (jnp.einsum('bhld,bhd->bhl', q, k_sum)[..., None] + EPS)
        attn = jnp.einsum('bhld,bhde->bhle', q, kv_summary) * z
        attn = attn.transpose(0, 2, 1, 3).reshape(B, L, D)
        out = attn * gate @ Wo.T
        return out

    def _L1_ffn_ref(x, gate_w, up_w, down_w):
        import jax, jax.numpy as jnp
        import numpy as np
        _FP8_MAX = 448.0
        _BLOCK = 32
        _EPS = 1e-30

        def _mx_dequant(t):
            rows, feat = t.shape
            blocks = t.reshape(rows, feat // _BLOCK, _BLOCK)
            max_abs = jnp.max(jnp.abs(blocks), axis=-1)
            scales = jnp.maximum(max_abs / _FP8_MAX, _EPS)
            q = (blocks / scales[..., None]).astype(jnp.float8_e4m3fn).astype(jnp.float32)
            return (q * scales[..., None]).reshape(rows, feat)

        def _mx_linear(x2d, w):
            return _mx_dequant(x2d) @ _mx_dequant(w).T
        B, S, H = x.shape
        x2d = x.reshape(B * S, H)
        gate = _mx_linear(x2d, gate_w)
        up = _mx_linear(x2d, up_w)
        h = jax.nn.silu(gate) * up
        out = _mx_linear(h, down_w)
        return out.reshape(B, S, H)
    x = x + _L0_attn_ref(_layernorm(x, axis=-1), L0_attn_W_in, L0_attn_conv_w, L0_attn_W_x, L0_attn_W_dt, L0_attn_b_dt, L0_attn_D, L0_attn_W_out)
    x = x + _L0_xattn_ref(_layernorm(x, axis=-1), ctx_2048, L0_xattn_wq, L0_xattn_bq, L0_xattn_wkv, L0_xattn_bkv, L0_xattn_wp, L0_xattn_bp)
    x = x + _L0_ffn_ref(_layernorm(x, axis=-1), L0_ffn_sw1, L0_ffn_swg, L0_ffn_sw2, L0_ffn_rw1, L0_ffn_rwg, L0_ffn_rw2, L0_ffn_Wg, L0_ffn_Wdown, L0_ffn_Wup, L0_ffn_biases)
    x = x + _L1_attn_ref(_layernorm(x, axis=-1), L1_attn_qkv_w, L1_attn_out_w, L1_attn_gate_w, L1_attn_norm_w)
    x = x + _L1_xattn_ref(_layernorm(x, axis=-1), ctx_2048, L1_xattn_Wq, L1_xattn_Wg, L1_xattn_bg, L1_xattn_Wkv, L1_xattn_Wo)
    x = x + _L1_ffn_ref(_layernorm(x, axis=-1), L1_ffn_gate_w, L1_ffn_up_w, L1_ffn_down_w)
    return x

_drawn_inputs = setup_inputs


def setup_inputs(seed=0):
    import zlib

    import numpy as np

    out = dict(_drawn_inputs(seed))
    spreads = {'L0_attn_D': (1.0, 0.2),
     'L0_ffn_biases': (0.0, 0.1),
     'L1_attn_norm_w': (1.0, 0.2),
     'L1_xattn_bg': (1.0, 0.6)}
    factors = {'L0_xattn_bq': 24.664, 'L1_xattn_Wq': 44.585}
    for name, (base, spread) in spreads.items():
        noise = np.random.default_rng([zlib.crc32(name.encode()), seed]).standard_normal(out[name].shape)
        drawn = base * np.exp(spread * noise) if base else spread * noise
        out[name] = jnp.asarray(drawn.astype(out[name].dtype))
    for name, factor in factors.items():
        out[name] = (out[name] * factor).astype(out[name].dtype)
    return out
```

```python
import numpy as np
import concourse.bass as bass
from concourse import mybir

F32 = mybir.dt.float32
BF16 = mybir.dt.bfloat16
U32 = mybir.dt.uint32
ALU = mybir.AluOpType
ACT = mybir.ActivationFunctionType
AX = mybir.AxisListType

P = 128
TOK, DM = 1024, 512
TT, KD = TOK // P, DM // P
BANK = 512
CTX = 2048


class Core:

    def __init__(self, nc, dram, out):
        self.nc, self.dram, self.out = nc, dram, out
        self.base = -(-nc.sbuf_base // 64) * 64
        self.x = self.at("x", [P, TT, DM], F32, 0)
        self.xF = self.at("xF", [P, KD, TOK], F32, 16)
        self.xn = self.at("xn", [P, TT, DM], F32, 32)
        self.ident = self.at("ident", [P, P], F32, 48)
        self.identb = self.at("identb", [P, P], BF16, 48.5)
        self.stats = self.at("stats", [P, TT, 6], F32, 48.75)
        self.mv = self.at("mv", [P, TT, 2], F32, 49)
        self.rstd = self.at("rstd", [P, TT], F32, 49.125)
        self.var_eps = self.at("var_eps", [P, TT], F32, 49.25)
        self.neg_half = self.at("neg_half", [P, TT], F32, 49.375)
        self.stored = nc.alloc_semaphore("stored")
        self.ps = nc.alloc_psum_tensor("ps", [P, 8, BANK], F32)

    def at(self, name, shape, dt, kb):
        off = self.base + int(kb * 1024)
        return self.nc.alloc_sbuf_tensor_at(name, shape, dt, offset=off)

    def sem(self, name):
        s = self.nc.alloc_semaphore(name)
        self.stage_sems.append(s)
        return s


def tiled(ap):
    return ap.rearrange("(k p) n -> p k n", p=P)


def load_constants(c):
    nc = c.nc
    loaded = c.sem("const_loaded")
    identb_ready = c.sem("identb_ready")
    with nc.Block() as block:
        @block.sync
        def _(sp):
            sp.dma_start(c.x[:], tiled(c.dram["x"])).then_inc(loaded, 16)
            sp.dma_start(c.ident[:], c.dram["c_ident"]).then_inc(loaded, 16)
            sp.wait_ge(loaded, 32)

        @block.gpsimd
        def _(pool):
            nc.gpsimd.memset(c.neg_half[:], -0.5)

        @block.vector
        def _(dve):
            dve.wait_ge(loaded, 32)
            nc.vector.tensor_copy(c.identb[:], c.ident[:]).then_inc(identb_ready, 1)
            dve.wait_ge(identb_ready, 1)


def rstd_pool(c, aggr_done, rstd_done):
    c.nc.gpsimd.wait_ge(aggr_done, TT + 1)
    c.nc.gpsimd.tensor_tensor(c.rstd[:], c.var_eps[:], c.neg_half[:], ALU.pow).then_inc(rstd_done, 1)


def layernorm_dve(c, tag, aggr_done, rstd_done, normed):
    nc, dve = c.nc, c.nc.vector
    stats_done = c.sem(f"{tag}_stats_done")
    for t in range(TT):
        nc.vector.bn_stats(c.stats[:, t, :], c.x[:, t, :]).then_inc(stats_done, 1)
    for t in range(TT):
        dve.wait_ge(stats_done, t + 1)
        nc.vector.bn_aggr(c.mv[:, t, :], c.stats[:, t, :]).then_inc(aggr_done, 1)
    dve.wait_ge(aggr_done, TT)
    nc.vector.tensor_scalar(c.var_eps[:], c.mv[:, :, 1], 1e-5, None, ALU.add).then_inc(aggr_done, 1)
    dve.wait_ge(rstd_done, 1)
    for t in range(TT):
        nc.vector.tensor_scalar(c.xn[:, t, :], c.x[:, t, :], c.mv[:, t, 0:1], c.rstd[:, t:t + 1],
                                ALU.subtract, ALU.mult).then_inc(normed, 1)


def norm_and_transpose(c, tag, extra_pe=None, extra_act=None):
    nc = c.nc
    normed, turned = c.sem(f"{tag}_normed"), c.sem(f"{tag}_turned")
    moved_act, moved_dve = c.sem(f"{tag}_moved_act"), c.sem(f"{tag}_moved_dve")
    aggr_done, rstd_done = c.sem(f"{tag}_aggr_done"), c.sem(f"{tag}_rstd_done")
    with nc.Block() as block:
        @block.gpsimd
        def _(pool):
            rstd_pool(c, aggr_done, rstd_done)

        @block.vector
        def _(dve):
            layernorm_dve(c, tag, aggr_done, rstd_done, normed)
            for t in range(1, TT, 2):
                dve.wait_ge(turned, t + 1)
                nc.vector.tensor_copy(c.xF[:, :, t * P:(t + 1) * P],
                                      c.ps[:, t, :].rearrange("p (k t) -> p k t", k=KD)).then_inc(moved_dve, 1)
            dve.wait_ge(moved_dve, TT // 2)

        @block.scalar
        def _(act):
            for t in range(0, TT, 2):
                act.wait_ge(turned, t + 1)
                nc.scalar.activation(c.xF[:, :, t * P:(t + 1) * P],
                                     c.ps[:, t, :].rearrange("p (k t) -> p k t", k=KD), ACT.Copy).then_inc(moved_act, 1)
            act.wait_ge(moved_act, TT // 2)

        @block.tensor
        def _(pe):
            for t in range(TT):
                pe.wait_ge(normed, t + 1)
                for k in range(KD):
                    last = nc.tensor.transpose(c.ps[:, t, k * P:(k + 1) * P], c.xn[:, t, k * P:(k + 1) * P], c.ident[:])
                last.then_inc(turned, 1)


def turn_normed(c, tag):
    nc = c.nc
    turned = c.sem(f"{tag}_turned")
    moved_act, moved_dve = c.sem(f"{tag}_moved_act"), c.sem(f"{tag}_moved_dve")
    with nc.Block() as block:
        @block.vector
        def _(dve):
            for t in range(1, TT, 2):
                dve.wait_ge(turned, t + 1)
                nc.vector.tensor_copy(c.xF[:, :, t * P:(t + 1) * P],
                                      c.ps[:, t, :].rearrange("p (k t) -> p k t", k=KD)).then_inc(moved_dve, 1)

        @block.scalar
        def _(act):
            for t in range(0, TT, 2):
                act.wait_ge(turned, t + 1)
                nc.scalar.activation(c.xF[:, :, t * P:(t + 1) * P],
                                     c.ps[:, t, :].rearrange("p (k t) -> p k t", k=KD), ACT.Copy).then_inc(moved_act, 1)

        @block.tensor
        def _(pe):
            for t in range(TT):
                for k in range(KD):
                    last = nc.tensor.transpose(c.ps[:, t, k * P:(k + 1) * P], c.xn[:, t, k * P:(k + 1) * P], c.ident[:])
                last.then_inc(turned, 1)



def mixer(c):
    nc = c.nc
    INTER = 1024
    KI = INTER // P
    winx = c.at("a_winx", [P, KI, DM], F32, 52)
    convT = c.at("a_convT", [P, KI, INTER], F32, 68)
    winzT = c.at("a_winzT", [P, KD, INTER], F32, 100)
    wpT = c.at("a_wpT", [P, KD, INTER], F32, 116)
    woutT = c.at("a_woutT", [P, KI, DM], F32, 132)
    g = c.at("a_g", [P, KI, TOK], F32, 148)
    sz = c.at("a_sz", [P, 2, BANK], F32, 180)
    Dv = c.at("a_D", [P, KI], F32, 50)
    in_x, in_rest = c.sem("a_in_x"), c.sem("a_in_rest")
    in_conv = [c.sem(f"a_in_conv{h}") for h in range(2)]

    with nc.Block() as block:
        @block.sync
        def _(sp):
            sp.dma_start(winx[:], tiled(c.dram["winx"])).then_inc(in_x, 16)
            for h in range(2):
                sp.dma_start(convT[:, :, h * BANK:(h + 1) * BANK],
                             tiled(c.dram["convT"])[:, :, h * BANK:(h + 1) * BANK]).then_inc(in_conv[h], 16)
            sp.dma_start(winzT[:], tiled(c.dram["winzT"])).then_inc(in_rest, 16)
            sp.dma_start(woutT[:], tiled(c.dram["woutT"])).then_inc(in_rest, 16)
            sp.dma_start(Dv[:], c.dram["Dv"]).then_inc(in_rest, 16)

    fused, fused_moved = c.sem("a_fused"), c.sem("a_fused_moved")
    with nc.Block() as block:
        @block.tensor
        def _(pe):
            pe.wait_ge(in_x, 16)
            for n in range(2):
                pe.wait_ge(in_conv[n], 16)
                for m in range(KD):
                    for k in range(KI):
                        last = nc.tensor.matmul(c.ps[:, n * KD + m, :], winx[:, k, m * P:(m + 1) * P],
                                                convT[:, k, n * BANK:(n + 1) * BANK], start=k == 0, stop=k == KI - 1)
                    last.then_inc(fused, 1)

        @block.scalar
        def _(act):
            for j in range(2 * KD):
                n, m = j // KD, j % KD
                act.wait_ge(fused, j + 1)
                nc.scalar.activation(wpT[:, m, n * BANK:(n + 1) * BANK], c.ps[:, j, :], ACT.Copy).then_inc(fused_moved, 1)
            act.wait_ge(fused_moved, 2 * KD)

    norm_and_transpose(c, "a_ln")

    z_done, y_done, silu_done, g_done = (c.sem(f"a_{n}") for n in ("z_done", "y_done", "silu_done", "g_done"))
    out_done, added = c.sem("a_out_done"), c.sem("a_added")
    JOBS = [(n, m) for n in range(2) for m in range(KI)]
    with nc.Block() as block:
        @block.tensor
        def _(pe):
            pe.wait_ge(in_rest, 48)
            for j, (n, m) in enumerate(JOBS):
                tok = slice(n * BANK, (n + 1) * BANK)
                if j >= 2:
                    pe.wait_ge(silu_done, j - 1)
                for k in range(KD):
                    last = nc.tensor.matmul(c.ps[:, j % 2, :], winzT[:, k, m * P:(m + 1) * P], c.xF[:, k, tok],
                                            start=k == 0, stop=k == KD - 1)
                last.then_inc(z_done, 1)
                if j >= 2:
                    pe.wait_ge(g_done, j - 1)
                for k in range(KD):
                    last = nc.tensor.matmul(c.ps[:, 2 + j % 2, :], wpT[:, k, m * P:(m + 1) * P], c.xF[:, k, tok],
                                            start=k == 0, stop=k == KD - 1)
                last.then_inc(y_done, 1)
            for t in range(TT):
                pe.wait_ge(g_done, KI * (1 + t // (TT // 2)))
                if t >= 4:
                    pe.wait_ge(added, t - 3)
                for k in range(KI):
                    last = nc.tensor.matmul(c.ps[:, 4 + t % 4, :], g[:, k, t * P:(t + 1) * P], woutT[:, k, :],
                                            start=k == 0, stop=k == KI - 1)
                last.then_inc(out_done, 1)

        @block.scalar
        def _(act):
            for j, (n, m) in enumerate(JOBS):
                act.wait_ge(z_done, j + 1)
                if j >= 2:
                    act.wait_ge(g_done, j - 1)
                nc.scalar.activation(sz[:, j % 2, :], c.ps[:, j % 2, :], ACT.Silu).then_inc(silu_done, 1)

        @block.vector
        def _(dve):
            for j, (n, m) in enumerate(JOBS):
                dve.wait_ge(y_done, j + 1)
                dve.wait_ge(silu_done, j + 1)
                nc.vector.scalar_tensor_tensor(g[:, m, n * BANK:(n + 1) * BANK], c.ps[:, 2 + j % 2, :], Dv[:, m:m + 1],
                                               sz[:, j % 2, :], ALU.mult, ALU.mult).then_inc(g_done, 1)
            for t in range(TT):
                dve.wait_ge(out_done, t + 1)
                nc.vector.tensor_tensor(c.x[:, t, :], c.ps[:, 4 + t % 4, :], c.x[:, t, :], ALU.add).then_inc(added, 1)
            dve.wait_ge(added, TT)



ROUND = 1.5 * 2.0 ** 23


def int8_rows(c, tag, src, ints, scale, n, start=None):
    nc, dve = c.nc, c.nc.vector
    step = c.sem(f"{tag}_step")
    inv = c.at(f"{tag}_inv", [P, n], F32, 50.5)
    nc.vector.tensor_reduce(scale[:], src[:], AX.X, ALU.max, apply_absolute_value=True).then_inc(step, 1)
    dve.wait_ge(step, 1)
    nc.vector.tensor_scalar(scale[:], scale[:], 1.0 / 127.0, 1e-8, ALU.mult, ALU.max).then_inc(step, 1)
    dve.wait_ge(step, 2)
    nc.vector.reciprocal(inv[:], scale[:]).then_inc(step, 1)
    dve.wait_ge(step, 3)
    for j in range(n):
        nc.vector.tensor_scalar(src[:, j, :], src[:, j, :], inv[:, j:j + 1], ROUND, ALU.mult, ALU.add).then_inc(step, 1)
    for j in range(n):
        dve.wait_ge(step, 4 + j)
        last = nc.vector.tensor_scalar(ints[:, j, :], src[:, j, :], -ROUND, None, ALU.add)
    return last


def cross_attention(c):
    nc = c.nc
    H, DH, KEYS = 16, 32, 1024
    KT = KEYS // P
    ctxT = c.at("b_ctxT", [P, KD, CTX], F32, 52)
    KF = c.at("b_KF", [P, KD, CTX], F32, 84)
    V = c.at("b_V", [P, CTX // P, DM], F32, 116)
    wq = c.at("b_wq", [P, KD, DM], F32, 148)
    wp = c.at("b_wp", [P, KD, DM], F32, 156)
    qF = c.at("b_qF", [P, KD, TOK], F32, 148)
    o = c.at("b_o", [P, TT, DM], F32, 164)
    wkT = c.at("b_wkT", [P, KD, DM], F32, 180)
    wvT = c.at("b_wvT", [P, KD, DM], F32, 188)
    wqT = c.at("b_wqT", [P, KD, DM], BF16, 196)
    wpT = c.at("b_wpT", [P, KD, DM], BF16, 200)
    bv = c.at("b_bv", [P, DM], F32, 204)
    wq_int = c.at("b_wq_int", [P, KD, DM], BF16, 164)
    wp_int = c.at("b_wp_int", [P, KD, DM], BF16, 168)
    xq = c.at("b_xq", [P, TT, DM], BF16, 172)
    xqF = c.at("b_xqF", [P, KD, TOK], BF16, 16)
    sx_row = c.at("b_sx_row", [P, TOK], F32, 24)
    swp_row = c.at("b_swp_row", [P, DM], F32, 28)
    q_raw = c.at("b_q_raw", [P, 2, BANK], F32, 52)
    pr = c.at("b_pr", [P, 2, KEYS], F32, 56)
    prT = c.at("b_prT", [P, 2, KT, P], F32, 64)
    oq = c.at("b_oq", [P, TT, DM], BF16, 52)
    oqF = c.at("b_oqF", [P, KD, TOK], BF16, 60)
    bq = c.at("b_bq", [P, KD], F32, 50.0625)
    bk = c.at("b_bk", [P, KD], F32, 50.125)
    sx = c.at("b_sx", [P, TT], F32, 50.1875)
    swq = c.at("b_swq", [P, KD], F32, 50.25)
    swp = c.at("b_swp", [P, KD], F32, 50.3125)
    so = c.at("b_so", [P, TT], F32, 50.375)
    nmax = c.at("b_nmax", [P, 2], F32, 50.4375)
    rsum = c.at("b_rsum", [P, 2, H], F32, 50.625)
    rinv = c.at("b_rinv", [P, 2, H], F32, 50.75)
    bp = c.at("b_bp", [P, DM], F32, 30)

    in_k, in_v, in_wq, in_b = c.sem("b_in_k"), c.sem("b_in_v"), c.sem("b_in_wq"), c.sem("b_in_b")
    in_ctx = [c.sem(f"b_in_ctx{n}") for n in range(4)]
    with nc.Block() as block:
        @block.sync
        def _(sp):
            sp.dma_start(wkT[:], tiled(c.dram["b_wkT"])).then_inc(in_k, 16)
            for n in range(4):
                sp.dma_start(ctxT[:, :, n * BANK:(n + 1) * BANK],
                             tiled(c.dram["ctxT"])[:, :, n * BANK:(n + 1) * BANK]).then_inc(in_ctx[n], 16)
            sp.dma_start(wvT[:], tiled(c.dram["b_wvT"])).then_inc(in_v, 16)
            sp.dma_start(wq[:], tiled(c.dram["b_wq"])).then_inc(in_wq, 16)
            sp.dma_start(wp[:], tiled(c.dram["b_wp"])).then_inc(in_wq, 16)
            sp.dma_start(bq[:], c.dram["b_bq"]).then_inc(in_b, 16)
            sp.dma_start(bk[:], c.dram["b_bk"]).then_inc(in_b, 16)
            sp.dma_start(bv[:], c.dram["b_bv"].partition_broadcast(P)).then_inc(in_b, 16)
            sp.dma_start(bp[:], c.dram["b_bp"].partition_broadcast(P)).then_inc(in_b, 16)

    k_done, k_moved, v_done, v_moved = (c.sem(f"b_{n}") for n in ("k_done", "k_moved", "v_done", "v_moved"))
    normed, aggr_done, rstd_done = c.sem("b_normed"), c.sem("b_aggr_done"), c.sem("b_rstd_done")
    with nc.Block() as block:
        @block.tensor
        def _(pe):
            pe.wait_ge(in_k, 16)
            for n in range(4):
                pe.wait_ge(in_ctx[n], 16)
                for m in range(KD):
                    j = n * KD + m
                    if j >= 4:
                        pe.wait_ge(k_moved, j - 3)
                    for k in range(KD):
                        last = nc.tensor.matmul(c.ps[:, j % 4, :], wkT[:, k, m * P:(m + 1) * P],
                                                ctxT[:, k, n * BANK:(n + 1) * BANK], start=k == 0, stop=k == KD - 1)
                    last.then_inc(k_done, 1)
            pe.wait_ge(in_v, 16)
            for j in range(CTX // P):
                if j >= 4:
                    pe.wait_ge(v_moved, j - 3)
                for k in range(KD):
                    last = nc.tensor.matmul(c.ps[:, 4 + j % 4, :], ctxT[:, k, j * P:(j + 1) * P], wvT[:, k, :],
                                            start=k == 0, stop=k == KD - 1)
                last.then_inc(v_done, 1)

        @block.scalar
        def _(act):
            act.wait_ge(in_b, 64)
            for j in range(4 * KD):
                n, m = j // KD, j % KD
                act.wait_ge(k_done, j + 1)
                nc.scalar.activation(KF[:, m, n * BANK:(n + 1) * BANK], c.ps[:, j % 4, :], ACT.Identity,
                                     bias=bk[:, m:m + 1]).then_inc(k_moved, 1)

        @block.gpsimd
        def _(pool):
            rstd_pool(c, aggr_done, rstd_done)

        @block.vector
        def _(dve):
            layernorm_dve(c, "b", aggr_done, rstd_done, normed)
            dve.wait_ge(normed, TT)
            int8_rows(c, "b_x8", c.xn, xq, sx, TT)
            dve.wait_ge(in_wq, 32)
            int8_rows(c, "b_wq8", wq, wq_int, swq, KD)
            int8_rows(c, "b_wp8", wp, wp_int, swp, KD)
            dve.wait_ge(in_b, 64)
            for t in range(TT):
                nc.vector.tensor_tensor(c.x[:, t, :], c.x[:, t, :], bp[:], ALU.add)
            for j in range(CTX // P):
                dve.wait_ge(v_done, j + 1)
                nc.vector.tensor_tensor(V[:, j, :], c.ps[:, 4 + j % 4, :], bv[:], ALU.add).then_inc(v_moved, 1)

    turned, turned_act, turned_dve = c.sem("b_turned"), c.sem("b_turned_act"), c.sem("b_turned_dve")
    spread, spread_moved = c.sem("b_spread"), c.sem("b_spread_moved")
    SOURCES = ([(wq_int, wqT, m) for m in range(KD)] + [(wp_int, wpT, m) for m in range(KD)]
               + [(xq, xqF, t) for t in range(TT)])

    def turn_target(j):
        _, dst, m = SOURCES[j]
        return dst[:, :, m * P:(m + 1) * P]

    def turned_bank(j):
        return c.ps[:, j % 4, 0:BANK // 2].bitcast(BF16).rearrange("p (k t) -> p k t", k=KD)

    with nc.Block() as block:
        @block.tensor
        def _(pe):
            for j, (src, _, m) in enumerate(SOURCES):
                if j >= 4 and j % 2 == 0:
                    pe.wait_ge(turned_act, (j - 4) // 2 + 1)
                elif j >= 4:
                    pe.wait_ge(turned_dve, (j - 4) // 2 + 1)
                for k in range(KD):
                    last = nc.tensor.transpose(turned_bank(j)[:, k, :], src[:, m, k * P:(k + 1) * P], c.identb[:])
                last.then_inc(turned, 1)
            for t in range(TT):
                last = nc.tensor.matmul(c.ps[:, 4 + t // 4, t % 4 * P:(t % 4 + 1) * P],
                                        sx[:, t:t + 1].to_broadcast([P, P]), c.ident[:], start=True, stop=True)
            last.then_inc(spread, 1)
            for m in range(KD):
                last = nc.tensor.matmul(c.ps[:, 6, m * P:(m + 1) * P],
                                        swp[:, m:m + 1].to_broadcast([P, P]), c.ident[:], start=True, stop=True)
            last.then_inc(spread, 1)

        @block.scalar
        def _(act):
            for j in range(0, len(SOURCES), 2):
                act.wait_ge(turned, j + 1)
                nc.scalar.activation(turn_target(j), turned_bank(j), ACT.Copy).then_inc(turned_act, 1)
            act.wait_ge(spread, 1)
            nc.scalar.activation(sx_row[:].rearrange("p (a n) -> p a n", a=2), c.ps[:, 4:6, :], ACT.Copy)
            act.wait_ge(spread, 2)
            nc.scalar.activation(swp_row[:], c.ps[:, 6, :], ACT.Copy).then_inc(spread_moved, 1)

        @block.vector
        def _(dve):
            for j in range(1, len(SOURCES), 2):
                dve.wait_ge(turned, j + 1)
                nc.vector.tensor_copy(turn_target(j), turned_bank(j)).then_inc(turned_dve, 1)

    q_done, q_scaled, q_ready = c.sem("b_q_done"), c.sem("b_q_scaled"), c.sem("b_q_ready")
    with nc.Block() as block:
        @block.tensor
        def _(pe):
            for j in range(2 * KD):
                n, m = j // KD, j % KD
                for k in range(KD):
                    last = nc.tensor.matmul(c.ps[:, j, :], wqT[:, k, m * P:(m + 1) * P],
                                            xqF[:, k, n * BANK:(n + 1) * BANK], start=k == 0, stop=k == KD - 1)
                last.then_inc(q_done, 1)

        @block.vector
        def _(dve):
            for j in range(2 * KD):
                n, m = j // KD, j % KD
                dve.wait_ge(q_done, j + 1)
                if j >= 2:
                    dve.wait_ge(q_ready, j - 1)
                nc.vector.scalar_tensor_tensor(q_raw[:, j % 2, :], c.ps[:, j, :], swq[:, m:m + 1],
                                               sx_row[:, n * BANK:(n + 1) * BANK], ALU.mult, ALU.mult).then_inc(q_scaled, 1)

        @block.gpsimd
        def _(pool):
            for j in range(2 * KD):
                n, m = j // KD, j % KD
                pool.wait_ge(q_scaled, j + 1)
                nc.gpsimd.tensor_scalar(qF[:, m, n * BANK:(n + 1) * BANK], q_raw[:, j % 2, :], bq[:, m:m + 1],
                                        DH ** -0.5, ALU.add, ALU.mult).then_inc(q_ready, 1)

    UNITS = [(b, t, h) for b in range(2) for t in range(TT // 2) for h in range(H)]
    s_done, max_done, exp_done = c.sem("b_s_done"), c.sem("b_max_done"), c.sem("b_exp_done")
    t_done = [c.sem(f"b_t_done{i}") for i in range(2)]
    t_moved = [c.sem(f"b_t_moved{i}") for i in range(2)]
    pv_done, o_ready, inv_done = c.sem("b_pv_done"), c.sem("b_o_ready"), c.sem("b_inv_done")

    with nc.Block() as block:
        @block.tensor
        def _(pe):
            def scores(u):
                b, t, h = UNITS[u]
                rows, tok = slice(h % 4 * DH, (h % 4 + 1) * DH), slice((4 * b + t) * P, (4 * b + t + 1) * P)
                if u >= 2:
                    pe.wait_ge(exp_done, u - 1)
                for n in range(2):
                    keys = slice(b * KEYS + n * BANK, b * KEYS + (n + 1) * BANK)
                    last = nc.tensor.matmul(c.ps[:, 2 * (u % 2) + n, :], qF[rows, h // 4, tok], KF[rows, h // 4, keys],
                                            start=True, stop=True)
                last.then_inc(s_done, 1)

            def turn(u):
                pe.wait_ge(exp_done, u + 1)
                for half in range(2):
                    if u >= 1:
                        pe.wait_ge(t_moved[half], u)
                    for i in range(4):
                        last = nc.tensor.transpose(c.ps[:, 4 + half, i * P:(i + 1) * P],
                                                   pr[:, u % 2, (4 * half + i) * P:(4 * half + i + 1) * P], c.ident[:])
                    last.then_inc(t_done[half], 1)

            def weigh(u):
                b, t, h = UNITS[u]
                group = u // H
                for half in range(2):
                    pe.wait_ge(t_moved[half], u + 1)
                if h == 0 and group >= 2:
                    pe.wait_ge(o_ready, group - 1)
                for k in range(KT):
                    last = nc.tensor.matmul(c.ps[:, 6 + group % 2, h * DH:(h + 1) * DH], prT[:, u % 2, k, :],
                                            V[:, b * KT + k, h * DH:(h + 1) * DH], start=k == 0, stop=k == KT - 1)
                last.then_inc(pv_done, 1)

            n = len(UNITS)
            scores(0)
            for u in range(n + 1):
                if u + 1 < n:
                    scores(u + 1)
                if u >= 1:
                    weigh(u - 1)
                if u < n:
                    turn(u)

        @block.scalar
        def _(act):
            for u, (b, t, h) in enumerate(UNITS):
                act.wait_ge(max_done, u + 1)
                if u >= 2:
                    act.wait_ge(t_done[1], u - 1)
                if u >= 2 * H and h == 0:
                    act.wait_ge(inv_done, u // H - 1)
                nc.scalar.activation(pr[:, u % 2, :].rearrange("p (a n) -> p a n", a=2),
                                     c.ps[:, 2 * (u % 2):2 * (u % 2) + 2, :], ACT.Exp, bias=nmax[:, u % 2:u % 2 + 1],
                                     accum_out=rsum[:, u // H % 2, h:h + 1]).then_inc(exp_done, 1)
                act.wait_ge(t_done[0], u + 1)
                if u >= 2:
                    act.wait_ge(pv_done, u - 1)
                nc.scalar.activation(prT[:, u % 2, 0:4, :].rearrange("p a n -> p (a n)"), c.ps[:, 4, :],
                                     ACT.Copy).then_inc(t_moved[0], 1)

        @block.vector
        def _(dve):
            def row_max(u):
                dve.wait_ge(s_done, u + 1)
                if u >= 2:
                    dve.wait_ge(exp_done, u - 1)
                nc.vector.tensor_reduce(nmax[:, u % 2:u % 2 + 1], c.ps[:, 2 * (u % 2):2 * (u % 2) + 2, :], AX.XY, ALU.max,
                                        negate=True).then_inc(max_done, 1)

            row_max(0)
            for u, (b, t, h) in enumerate(UNITS):
                if u + 1 < len(UNITS):
                    row_max(u + 1)
                dve.wait_ge(t_done[1], u + 1)
                if u >= 2:
                    dve.wait_ge(pv_done, u - 1)
                nc.vector.tensor_copy(prT[:, u % 2, 4:8, :].rearrange("p a n -> p (a n)"), c.ps[:, 5, :]).then_inc(t_moved[1], 1)
                if h == H - 1:
                    group = u // H
                    dve.wait_ge(exp_done, u + 1)
                    nc.vector.reciprocal(rinv[:, group % 2, :], rsum[:, group % 2, :]).then_inc(inv_done, 1)
                    dve.wait_ge(inv_done, group + 1)
                    dve.wait_ge(pv_done, u + 1)
                    nc.vector.tensor_tensor(o[:, 4 * b + t, :].rearrange("p (h d) -> p h d", h=H),
                                            c.ps[:, 6 + group % 2, :].rearrange("p (h d) -> p h d", h=H),
                                            rinv[:, group % 2, :].unsqueeze(2).to_broadcast([P, H, DH]),
                                            ALU.mult).then_inc(o_ready, 1)
            dve.wait_ge(o_ready, TT)
            int8_rows(c, "b_o8", o, oq, so, TT)

    oturned, oturned_moved, out_done, out_scaled = (c.sem(f"b_{n}") for n in ("oturned", "oturned_moved", "out_done", "out_scaled"))
    added = c.sem("b_added")
    tmp = c.at("b_tmp", [P, 2, DM], F32, 76)
    with nc.Block() as block:
        def obank(t):
            return c.ps[:, t % 4, 0:BANK // 2].bitcast(BF16).rearrange("p (k t) -> p k t", k=KD)

        @block.tensor
        def _(pe):
            for t in range(TT + 1):
                if t < TT:
                    if t >= 4:
                        pe.wait_ge(oturned_moved, t - 3)
                    for k in range(KD):
                        last = nc.tensor.transpose(obank(t)[:, k, :], oq[:, t, k * P:(k + 1) * P], c.identb[:])
                    last.then_inc(oturned, 1)
                if t >= 1:
                    t0 = t - 1
                    pe.wait_ge(oturned_moved, t0 + 1)
                    if t0 >= 4:
                        pe.wait_ge(out_scaled, t0 - 3)
                    for k in range(KD):
                        last = nc.tensor.matmul(c.ps[:, 4 + t0 % 4, :], oqF[:, k, t0 * P:(t0 + 1) * P], wpT[:, k, :],
                                                start=k == 0, stop=k == KD - 1)
                    last.then_inc(out_done, 1)

        @block.scalar
        def _(act):
            for t in range(TT):
                act.wait_ge(oturned, t + 1)
                nc.scalar.activation(oqF[:, :, t * P:(t + 1) * P], obank(t), ACT.Copy).then_inc(oturned_moved, 1)

        @block.vector
        def _(dve):
            for t in range(TT):
                dve.wait_ge(out_done, t + 1)
                if t >= 2:
                    dve.wait_ge(added, t - 1)
                nc.vector.scalar_tensor_tensor(tmp[:, t % 2, :], c.ps[:, 4 + t % 4, :], so[:, t:t + 1], swp_row[:],
                                               ALU.mult, ALU.mult).then_inc(out_scaled, 1)

        @block.gpsimd
        def _(pool):
            for t in range(TT):
                pool.wait_ge(out_scaled, t + 1)
                nc.gpsimd.tensor_tensor(c.x[:, t, :], c.x[:, t, :], tmp[:, t % 2, :], ALU.add).then_inc(added, 1)



def experts(c):
    nc = c.nc
    E, LAT, HID, SCALE = 16, 128, 256, 2.5
    KH = HID // P
    s1T = c.at("c_s1T", [P, KD, HID], F32, 52)
    sgT = c.at("c_sgT", [P, KD, HID], F32, 56)
    s2T = c.at("c_s2T", [P, KH, DM], F32, 60)
    wdT = c.at("c_wdT", [P, KD, LAT], F32, 64)
    wupT = c.at("c_wupT", [P, DM], F32, 66)
    wgT = c.at("c_wgT", [P, KD, E], F32, 68)
    bias = c.at("c_bias", [P, E], F32, 68.5)
    r1T = c.at("c_r1T", [P, E, HID], F32, 72)
    rgT = c.at("c_rgT", [P, E, HID], F32, 88)
    r2T = c.at("c_r2T", [P, E, KH, LAT], F32, 104)
    sF = c.at("c_sF", [P, KH, TOK], F32, 120)
    xlF = c.at("c_xlF", [P, TOK], F32, 128)
    acc = c.at("c_acc", [P, TT, LAT], F32, 132)
    accF = c.at("c_accF", [P, TOK], F32, 136)
    hF = c.at("c_hF", [P, 2, KH, TOK], F32, 140)
    relu = c.at("c_relu", [P, 2, BANK], F32, 156)
    sq = c.at("c_sq", [P, 2, BANK], F32, 160)
    prob = c.at("c_prob", [P, TT, E], F32, 164)
    sel = c.at("c_sel", [P, TT, E], F32, 164.5)
    rest = c.at("c_rest", [P, TT, E], F32, 165)
    top = c.at("c_top", [P, TT, 8], F32, 165.5)
    w = c.at("c_w", [P, TT, E], F32, 166)
    total = c.at("c_total", [P, TT], F32, 166.5)

    in_s, in_r1, in_r2 = c.sem("c_in_s"), c.sem("c_in_r1"), c.sem("c_in_r2")
    with nc.Block() as block:
        @block.sync
        def _(sp):
            sp.dma_start(wdT[:], tiled(c.dram["c_wdT"])).then_inc(in_s, 16)
            sp.dma_start(wgT[:], tiled(c.dram["c_wgT"])).then_inc(in_s, 16)
            sp.dma_start(s1T[:], tiled(c.dram["c_s1T"])).then_inc(in_s, 16)
            sp.dma_start(sgT[:], tiled(c.dram["c_sgT"])).then_inc(in_s, 16)
            sp.dma_start(s2T[:], tiled(c.dram["c_s2T"])).then_inc(in_s, 16)
            sp.dma_start(wupT[:], c.dram["c_wupT"]).then_inc(in_s, 16)
            sp.dma_start(bias[:], c.dram["c_bias"].partition_broadcast(P)).then_inc(in_s, 16)
            sp.dma_start(r1T[:], c.dram["c_r1T"].rearrange("e p n -> p e n")).then_inc(in_r1, 16)
            sp.dma_start(rgT[:], c.dram["c_rgT"].rearrange("e p n -> p e n")).then_inc(in_r1, 16)
            sp.dma_start(r2T[:], c.dram["c_r2T"].rearrange("e (k p) n -> p e k n", p=P)).then_inc(in_r2, 16)

    norm_and_transpose(c, "c_ln")

    lat_done, lat_moved, logit_done, prob_done = (c.sem(f"c_{n}") for n in ("lat_done", "lat_moved", "logit_done", "prob_done"))
    sg_done, s1_done, relu_done, sq_done, sh_done = (c.sem(f"c_{n}") for n in ("sg_done", "s1_done", "relu_done", "sq_done", "sh_done"))
    step = c.sem("c_step")
    JOBS = [(n, m) for n in range(2) for m in range(KH)]
    with nc.Block() as block:
        @block.tensor
        def _(pe):
            pe.wait_ge(in_s, 112)
            for t in range(TT):
                for k in range(KD):
                    last = nc.tensor.matmul(c.ps[:, 6, t * E:(t + 1) * E], c.xF[:, k, t * P:(t + 1) * P], wgT[:, k, :],
                                            start=k == 0, stop=k == KD - 1)
            last.then_inc(logit_done, 1)
            for n in range(2):
                for k in range(KD):
                    last = nc.tensor.matmul(c.ps[:, 4 + n, :], wdT[:, k, :], c.xF[:, k, n * BANK:(n + 1) * BANK],
                                            start=k == 0, stop=k == KD - 1)
                last.then_inc(lat_done, 1)
            for j, (n, m) in enumerate(JOBS):
                for bank, wT, freed, done in ((j % 2, sgT, relu_done, sg_done), (2 + j % 2, s1T, sh_done, s1_done)):
                    if j >= 2:
                        pe.wait_ge(freed, j - 1)
                    for k in range(KD):
                        last = nc.tensor.matmul(c.ps[:, bank, :], wT[:, k, m * P:(m + 1) * P],
                                                c.xF[:, k, n * BANK:(n + 1) * BANK], start=k == 0, stop=k == KD - 1)
                    last.then_inc(done, 1)

        @block.scalar
        def _(act):
            act.wait_ge(logit_done, 1)
            nc.scalar.activation(prob[:].rearrange("p t e -> p (t e)"), c.ps[:, 6, 0:TT * E], ACT.Sigmoid).then_inc(prob_done, 1)
            for n in range(2):
                act.wait_ge(lat_done, n + 1)
                nc.scalar.activation(xlF[:, n * BANK:(n + 1) * BANK], c.ps[:, 4 + n, :], ACT.Copy).then_inc(lat_moved, 1)
            for j, (n, m) in enumerate(JOBS):
                act.wait_ge(sg_done, j + 1)
                nc.scalar.activation(relu[:, j % 2, :], c.ps[:, j % 2, :], ACT.Relu).then_inc(relu_done, 1)
                act.wait_ge(relu_done, j + 1)
                if j >= 2:
                    act.wait_ge(sh_done, j - 1)
                nc.scalar.activation(sq[:, j % 2, :], relu[:, j % 2, :], ACT.Square).then_inc(sq_done, 1)

        @block.vector
        def _(dve):
            done = [0]

            def chained(ins):
                done[0] += 1
                ins.then_inc(step, 1)
                dve.wait_ge(step, done[0])

            dve.wait_ge(prob_done, 1)
            chained(nc.vector.tensor_tensor(sel[:], prob[:], bias[:].unsqueeze(1).to_broadcast([P, TT, E]), ALU.add))
            for t in range(TT):
                last = nc.vector.max(top[:, t, :], sel[:, t, :])
            chained(last)
            for t in range(TT):
                last = nc.vector.match_replace(rest[:, t, :], top[:, t, :], sel[:, t, :], -3e38)
            chained(last)
            chained(nc.vector.tensor_tensor(sel[:], sel[:], rest[:], ALU.not_equal))
            chained(nc.vector.tensor_tensor(sel[:], sel[:], prob[:], ALU.mult))
            chained(nc.vector.tensor_reduce(total[:], sel[:], AX.X, ALU.add))
            chained(nc.vector.reciprocal(total[:], total[:]))
            chained(nc.vector.tensor_scalar(total[:], total[:], SCALE, None, ALU.mult))
            chained(nc.vector.tensor_tensor(w[:], sel[:], total[:].unsqueeze(2).to_broadcast([P, TT, E]), ALU.mult))
            for j, (n, m) in enumerate(JOBS):
                dve.wait_ge(sq_done, j + 1)
                dve.wait_ge(s1_done, j + 1)
                nc.vector.tensor_tensor(sF[:, m, n * BANK:(n + 1) * BANK], c.ps[:, 2 + j % 2, :], sq[:, j % 2, :],
                                        ALU.mult).then_inc(sh_done, 1)

    UP = [(e, n, m) for e in range(E) for n in range(2) for m in range(KH)]
    g_done, a_done, r_done, q_done, h_done = (c.sem(f"c_e_{n}") for n in ("g_done", "a_done", "r_done", "q_done", "h_done"))
    y_done, y_added = c.sem("c_y_done"), c.sem("c_y_added")
    PER = 2 * KH
    with nc.Block() as block:
        @block.tensor
        def _(pe):
            pe.wait_ge(in_r1, 32)
            pe.wait_ge(in_r2, 16)

            def up(e):
                for i in range(PER):
                    j = e * PER + i
                    _, n, m = UP[j]
                    for bank, wT, freed, done in ((j % 2, rgT, r_done, g_done), (2 + j % 2, r1T, h_done, a_done)):
                        if j >= 2:
                            pe.wait_ge(freed, j - 1)
                        nc.tensor.matmul(c.ps[:, bank, :], wT[:, e, m * P:(m + 1) * P], xlF[:, n * BANK:(n + 1) * BANK],
                                         start=True, stop=True).then_inc(done, 1)

            def down(e):
                pe.wait_ge(h_done, (e + 1) * PER)
                for n in range(2):
                    if e >= 1:
                        pe.wait_ge(y_added, 2 * (e - 1) + n + 1)
                    for i in range(4):
                        t = 4 * n + i
                        for k in range(KH):
                            last = nc.tensor.matmul(c.ps[:, 4 + n, i * LAT:(i + 1) * LAT], hF[:, e % 2, k, t * P:(t + 1) * P],
                                                    r2T[:, e, k, :], start=k == 0, stop=k == KH - 1)
                    last.then_inc(y_done, 1)

            up(0)
            for e in range(E):
                if e + 1 < E:
                    up(e + 1)
                down(e)

        @block.scalar
        def _(act):
            for j, (e, n, m) in enumerate(UP):
                act.wait_ge(g_done, j + 1)
                nc.scalar.activation(relu[:, j % 2, :], c.ps[:, j % 2, :], ACT.Relu).then_inc(r_done, 1)
                act.wait_ge(r_done, j + 1)
                if j >= 2:
                    act.wait_ge(h_done, j - 1)
                nc.scalar.activation(sq[:, j % 2, :], relu[:, j % 2, :], ACT.Square).then_inc(q_done, 1)

        @block.vector
        def _(dve):
            def hidden(e):
                if e >= 2:
                    dve.wait_ge(y_done, 2 * (e - 1))
                for i in range(PER):
                    j = e * PER + i
                    _, n, m = UP[j]
                    dve.wait_ge(a_done, j + 1)
                    dve.wait_ge(q_done, j + 1)
                    nc.vector.tensor_tensor(hF[:, e % 2, m, n * BANK:(n + 1) * BANK], c.ps[:, 2 + j % 2, :], sq[:, j % 2, :],
                                            ALU.mult).then_inc(h_done, 1)

            hidden(0)
            for e in range(E):
                if e + 1 < E:
                    hidden(e + 1)
                for n in range(2):
                    dve.wait_ge(y_done, 2 * e + n + 1)
                    if e >= 1:
                        dve.wait_ge(y_added, 2 * (e - 1) + n + 1)
                    for i in range(4):
                        t = 4 * n + i
                        src = c.ps[:, 4 + n, i * LAT:(i + 1) * LAT]
                        if e == 0:
                            last = nc.vector.tensor_scalar(acc[:, t, :], src, w[:, t, e:e + 1], None, ALU.mult)
                        else:
                            last = nc.vector.scalar_tensor_tensor(acc[:, t, :], src, w[:, t, e:e + 1], acc[:, t, :],
                                                                  ALU.mult, ALU.add)
                    last.then_inc(y_added, 1)

    a_turned, a_moved, out_done, added = (c.sem(f"c_{n}") for n in ("a_turned", "a_moved", "out_done", "added"))
    with nc.Block() as block:
        @block.tensor
        def _(pe):
            for n in range(2):
                for i in range(4):
                    last = nc.tensor.transpose(c.ps[:, n, i * P:(i + 1) * P], acc[:, 4 * n + i, :], c.ident[:])
                last.then_inc(a_turned, 1)
            for t in range(TT):
                pe.wait_ge(a_moved, 1 + t // 4)
                if t >= 4:
                    pe.wait_ge(added, t - 3)
                for k in range(KH):
                    nc.tensor.matmul(c.ps[:, 4 + t % 4, :], sF[:, k, t * P:(t + 1) * P], s2T[:, k, :],
                                     start=k == 0, stop=False)
                nc.tensor.matmul(c.ps[:, 4 + t % 4, :], accF[:, t * P:(t + 1) * P], wupT[:], start=False,
                                 stop=True).then_inc(out_done, 1)

        @block.scalar
        def _(act):
            for n in range(2):
                act.wait_ge(a_turned, n + 1)
                nc.scalar.activation(accF[:, n * BANK:(n + 1) * BANK], c.ps[:, n, :], ACT.Copy).then_inc(a_moved, 1)

        @block.vector
        def _(dve):
            for t in range(TT):
                dve.wait_ge(out_done, t + 1)
                nc.vector.tensor_tensor(c.x[:, t, :], c.ps[:, 4 + t % 4, :], c.x[:, t, :], ALU.add).then_inc(added, 1)



def linear_attention(c):
    nc = c.nc
    H, D = 32, 64
    PAIRS, GP = H // 2, 4
    G, CH = PAIRS // GP, TT // 2
    F = H * D
    at = 52.0

    def take(name, shape, dt, kb):
        nonlocal at
        at += kb
        return c.at(f"d_{name}", shape, dt, at - kb)

    mask = take("mask", [P, 2, 2 * GP, P], F32, 8)
    qdec = take("qdec", [P, 2, GP, P], F32, 4)
    wv = take("wv", [P, 2, KD, DM], F32, 16)
    wq = take("wq", [P, 2, KD, P], F32, 4)
    wk = take("wk", [P, 2, KD, P], F32, 4)
    wg = take("wg", [P, 2, KD, P], F32, 4)
    wo = take("wo", [P, 2, GP, DM], F32, 16)
    v = take("v", [P, TT, DM], F32, 16)
    qF = take("qF", [P, 2, TOK], F32, 8)
    qD = take("qD", [P, 2, TOK], F32, 8)
    kF = take("kF", [P, 2, TOK], F32, 8)
    kT = take("kT", [P, 2, TT, P], F32, 8)
    ga = take("ga", [P, 2 * GP, TOK], F32, 32)
    A = take("A", [P, 2, 2, CH, P], F32, 8)
    S = take("S", [P, CH - 1, 2, P], F32, 3)
    sq = take("sq", [P, 2, BANK], F32, 4)
    sqsum = take("sqsum", [P, TOK], F32, 4)
    y = c.at("d_y", [P, TT, DM], F32, 32)
    kdec = c.at("d_kdec", [P, H], F32, 50.5)
    bdec = c.at("d_bdec", [P, PAIRS], F32, 50.75)
    nw = c.at("d_nw", [P, PAIRS], F32, 51)
    ones = c.at("d_ones", [P, 1], F32, 51.125)
    ms = c.at("d_ms", [P, TT], F32, 51.25)

    in_c = c.sem("d_in_c")
    in_p = [c.sem(f"d_in_p{i}") for i in range(2)]
    in_g = [c.sem(f"d_in_g{i}") for i in range(2)]
    normed, turned = c.sem("d_ln_n"), None
    a_done, a_moved = c.sem("d_a_done"), c.sem("d_a_moved")
    proj_done, proj_moved = c.sem("d_proj_done"), c.sem("d_proj_moved")
    t_done, t_moved = c.sem("d_t_done"), c.sem("d_t_moved")
    u_done, s_ready = c.sem("d_u_done"), c.sem("d_s_ready")
    o_done, sq_done, ga_done = c.sem("d_o_done"), c.sem("d_sq_done"), c.sem("d_ga_done")
    qd_done, sqsum_done = c.sem("d_qd_done"), c.sem("d_sqsum_done")
    step, zeroed = c.sem("d_step"), c.sem("d_zeroed")

    def first_job(p):
        return 6 * p + (0 if p == 0 else TT * (1 + (p - 1) // GP))

    def a_jobs(p):
        return 4 * p + TT * (p // GP)

    with nc.Block() as block:
        @block.sync
        def _(sp):
            sp.dma_start(kdec[:], c.dram["d_kdec"]).then_inc(in_c, 16)
            sp.dma_start(bdec[:], c.dram["d_bdec"]).then_inc(in_c, 16)
            sp.dma_start(nw[:], c.dram["d_nw"]).then_inc(in_c, 16)

    norm_and_transpose(c, "d_ln")

    with nc.Block() as block:
        @block.sync
        def _(sp):
            for p in range(PAIRS):
                if p >= 2:
                    sp.wait_ge(proj_done, first_job(p - 2) + 6)
                for w, name in ((wq, "d_wq"), (wk, "d_wk"), (wg, "d_wg")):
                    sp.dma_start(w[:, p % 2, :, :], c.dram[name][p, :, :, :]).then_inc(in_p[p % 2], 16)
                if p % GP == 0:
                    g = p // GP
                    if g >= 2:
                        sp.wait_ge(a_moved, a_jobs(GP * (g - 1)))
                        sp.wait_ge(qd_done, 2 * GP * (g - 1))
                    sp.dma_start(wv[:, g % 2, :, :], tiled(c.dram["d_wvT"])[:, :, g * DM:(g + 1) * DM]).then_inc(in_g[g % 2], 16)
                    sp.dma_start(mask[:, g % 2, :, :], c.dram["d_mask"][:, g * 2 * GP:(g + 1) * 2 * GP, :]).then_inc(in_g[g % 2], 16)
                    sp.dma_start(qdec[:, g % 2, :, :], c.dram["d_qdec"][:, g * GP:(g + 1) * GP, :]).then_inc(in_g[g % 2], 16)
                    sp.dma_start(wo[:, g % 2, :, :], tiled(c.dram["d_woT"])[:, g * GP:(g + 1) * GP, :]).then_inc(in_g[g % 2], 16)

        @block.tensor
        def _(pe):
            def project(j, w, n):
                if j >= 2:
                    pe.wait_ge(proj_moved, j - 1)
                for k in range(KD):
                    last = nc.tensor.matmul(c.ps[:, j % 2, :], w[:, k, :], c.xF[:, k, n * BANK:(n + 1) * BANK],
                                            start=k == 0, stop=k == KD - 1)
                last.then_inc(proj_done, 1)

            def queries_keys(p):
                pe.wait_ge(in_p[p % 2], 48 * (p // 2 + 1))
                for i in range(4):
                    project(first_job(p) + i, (wq, wk)[i // 2][:, p % 2, :, :], i % 2)

            def gates(p):
                for n in range(2):
                    project(first_job(p) + 4 + n, wg[:, p % 2, :, :], n)

            def values(g):
                pe.wait_ge(in_g[g % 2], 64 * (g // 2 + 1))
                for t in range(TT):
                    j = first_job(GP * g) + 6 + t
                    pe.wait_ge(proj_moved, j - 1)
                    for k in range(KD):
                        last = nc.tensor.matmul(c.ps[:, j % 2, :], c.xF[:, k, t * P:(t + 1) * P], wv[:, g % 2, k, :],
                                                start=k == 0, stop=k == KD - 1)
                    last.then_inc(proj_done, 1)

            def products(p):
                pe.wait_ge(proj_moved, first_job(p) + 4)
                for i in range(4):
                    b, hh = i // 2, i % 2
                    j, rows = a_jobs(p) + i, slice(hh * D, (hh + 1) * D)
                    if j >= 2:
                        pe.wait_ge(a_moved, j - 1)
                    for ch in range(CH):
                        tok = slice((b * CH + ch) * P, (b * CH + ch + 1) * P)
                        last = nc.tensor.matmul(c.ps[:, 2 + j % 2, ch * P:(ch + 1) * P], kF[rows, p % 2, tok], qF[rows, p % 2, tok],
                                                start=True, stop=True)
                    last.then_inc(a_done, 1)

            def turn_keys(p):
                for b in range(2):
                    if p >= 1:
                        pe.wait_ge(s_ready, 3 * p)
                    for ch in range(CH):
                        t = b * CH + ch
                        last = nc.tensor.transpose(c.ps[:, 4 + b, ch * P:(ch + 1) * P], kF[:, p % 2, t * P:(t + 1) * P], c.ident[:])
                    last.then_inc(t_done, 1)

            def updates(p):
                pe.wait_ge(t_moved, 2 * (p + 1))
                if p % GP == 0:
                    pe.wait_ge(proj_moved, first_job(p) + 6 + TT)
                for b in range(2):
                    for ch in range(CH - 1):
                        t = b * CH + ch
                        last = nc.tensor.matmul(c.ps[:, 4 + b, ch * P:(ch + 1) * P], kT[:, p % 2, t, :],
                                                v[:, t, p % GP * P:(p % GP + 1) * P], start=True, stop=True)
                last.then_inc(u_done, 1)

            def outputs(p):
                pe.wait_ge(s_ready, 3 * (p + 1))
                pe.wait_ge(qd_done, 2 * (p + 1))
                pe.wait_ge(a_moved, a_jobs(p) + 4)
                for b in range(2):
                    if p >= 1:
                        pe.wait_ge(ga_done, 2 * (p - 1) + b + 1)
                    for ch in range(CH):
                        t = b * CH + ch
                        col = slice(ch * P, (ch + 1) * P)
                        if ch > 0:
                            nc.tensor.matmul(c.ps[:, 6 + b, col], S[:, ch - 1, b, :], qD[:, p % 2, t * P:(t + 1) * P],
                                             start=True, stop=False, skip_group_check=True)
                        for hh in range(2):
                            h = p % GP * 2 + hh
                            last = nc.tensor.matmul(c.ps[hh * D:(hh + 1) * D, 6 + b, col], v[:, t, h * D:(h + 1) * D],
                                                    A[:, b, hh, ch, :], start=ch == 0, stop=True, skip_group_check=True)
                    last.then_inc(o_done, 1)

            def sum_outputs(g):
                pe.wait_ge(ga_done, 2 * GP * (g + 1))
                for t in range(TT):
                    j = a_jobs(GP * (g + 1)) - TT + t
                    pe.wait_ge(a_moved, j - 1)
                    for k in range(GP):
                        last = nc.tensor.matmul(c.ps[:, 2 + j % 2, :], ga[:, g % 2 * GP + k, t * P:(t + 1) * P], wo[:, g % 2, k, :],
                                                start=k == 0, stop=k == GP - 1)
                    last.then_inc(a_done, 1)

            queries_keys(0)
            gates(0)
            values(0)
            for p in range(PAIRS):
                products(p)
                turn_keys(p)
                if p + 1 < PAIRS:
                    queries_keys(p + 1)
                updates(p)
                if p + 1 < PAIRS:
                    gates(p + 1)
                outputs(p)
                if p + 1 < PAIRS and (p + 1) % GP == 0:
                    values((p + 1) // GP)
                if p % GP == GP - 1:
                    sum_outputs(p // GP)

        @block.scalar
        def _(act):
            def pair(p):
                j = first_job(p)
                for i in range(6):
                    act.wait_ge(proj_done, j + i + 1)
                    tok = slice(i % 2 * BANK, (i % 2 + 1) * BANK)
                    src = c.ps[:, (j + i) % 2, :]
                    if i == 0 and p >= 2:
                        act.wait_ge(a_done, a_jobs(p - 2) + 4)
                        act.wait_ge(qd_done, 2 * (p - 1))
                    if i == 2 and p >= 2:
                        act.wait_ge(t_done, 2 * (p - 1))
                    if i == 4 and p >= 2 * GP and p % GP == 0:
                        act.wait_ge(a_done, a_jobs(p - GP))
                    if i < 4:
                        dst = (qF, kF)[i // 2][:, p % 2, tok]
                        nc.scalar.activation(dst, src, ACT.Silu).then_inc(proj_moved, 1)
                    else:
                        nc.scalar.activation(ga[:, p % (2 * GP), tok], src, ACT.Sigmoid).then_inc(proj_moved, 1)

            def values(g):
                j = first_job(GP * g) + 6
                if g >= 1:
                    act.wait_ge(o_done, 2 * GP * g)
                for t in range(TT):
                    act.wait_ge(proj_done, j + t + 1)
                    nc.scalar.activation(v[:, t, :], c.ps[:, (j + t) % 2, :], ACT.Silu).then_inc(proj_moved, 1)

            def squares(p):
                for b in range(2):
                    act.wait_ge(o_done, 2 * p + b + 1)
                    if p >= 1:
                        act.wait_ge(sqsum_done, 2 * (p - 1) + b + 1)
                    nc.scalar.activation(sq[:, b, :], c.ps[:, 6 + b, :], ACT.Square).then_inc(sq_done, 1)

            pair(0)
            values(0)
            for p in range(PAIRS):
                if p + 1 < PAIRS:
                    pair(p + 1)
                squares(p)
                if p + 1 < PAIRS and (p + 1) % GP == 0:
                    values((p + 1) // GP)

        @block.gpsimd
        def _(pool):
            nc.gpsimd.memset(sqsum[:], 0.0).then_inc(zeroed, 1)
            pool.wait_ge(zeroed, 1)
            for p in range(PAIRS):
                g = p // GP
                if p % GP == 0:
                    pool.wait_ge(in_g[g % 2], 64 * (g // 2 + 1))
                if p >= 2:
                    pool.wait_ge(o_done, 2 * (p - 1))
                for n in range(2):
                    pool.wait_ge(proj_moved, first_job(p) + n + 1)
                    tok = slice(n * BANK, (n + 1) * BANK)
                    nc.gpsimd.tensor_tensor(qD[:, p % 2, tok].rearrange("p (c i) -> p c i", i=P),
                                            qF[:, p % 2, tok].rearrange("p (c i) -> p c i", i=P),
                                            qdec[:, g % 2, p % GP, :].unsqueeze(1).to_broadcast([P, CH, P]),
                                            ALU.mult).then_inc(qd_done, 1)
                for b in range(2):
                    pool.wait_ge(sq_done, 2 * p + b + 1)
                    if p >= 1:
                        pool.wait_ge(sqsum_done, 2 * (p - 1) + b + 1)
                    tok = slice(b * BANK, (b + 1) * BANK)
                    nc.gpsimd.tensor_tensor(sqsum[:, tok], sqsum[:, tok], sq[:, b, :], ALU.add).then_inc(sqsum_done, 1)

        @block.vector
        def _(dve):
            nc.vector.memset(S[:], 0.0).then_inc(step, 1)
            nc.vector.memset(ones[:], 1.0)
            dve.wait_ge(step, 1)
            dve.wait_ge(in_c, 48)
            steps = [1]

            def mask_products(p):
                g = p // GP
                if p % GP == 0:
                    dve.wait_ge(in_g[g % 2], 64 * (g // 2 + 1))
                for i in range(4):
                    b, hh = i // 2, i % 2
                    j, h = a_jobs(p) + i, p % GP * 2 + hh
                    dve.wait_ge(a_done, j + 1)
                    if p >= 1:
                        dve.wait_ge(o_done, 2 * (p - 1) + b + 1)
                    nc.vector.tensor_tensor(A[:, b, hh, :, :], c.ps[:, 2 + j % 2, :].rearrange("p (c i) -> p c i", i=P),
                                            mask[:, g % 2, h, :].unsqueeze(1).to_broadcast([P, CH, P]),
                                            ALU.mult).then_inc(a_moved, 1)

            def decay_keys(p):
                if p >= 2:
                    dve.wait_ge(u_done, p - 1)
                for b in range(2):
                    dve.wait_ge(t_done, 2 * p + b + 1)
                    nc.vector.tensor_tensor(kT[:, p % 2, b * CH:(b + 1) * CH, :].rearrange("p c (h d) -> p c h d", h=2),
                                            c.ps[:, 4 + b, :].rearrange("p (c h d) -> p c h d", c=CH, h=2),
                                            kdec[:, 2 * p:2 * p + 2].unsqueeze(1).unsqueeze(3).to_broadcast([P, CH, 2, D]),
                                            ALU.mult).then_inc(t_moved, 1)

            def states(p):
                dve.wait_ge(u_done, p + 1)
                if p >= 1:
                    dve.wait_ge(o_done, 2 * p)
                for ch in range(CH - 1):
                    for hh in range(2):
                        rows, cols = slice(hh * D, (hh + 1) * D), slice(hh * D, (hh + 1) * D)
                        new = c.ps[rows, 4:6, ch * P + hh * D:ch * P + (hh + 1) * D]
                        if ch == 0:
                            last = nc.vector.tensor_copy(S[rows, 0, :, cols], new)
                        else:
                            last = nc.vector.scalar_tensor_tensor(S[rows, ch, :, cols], S[rows, ch - 1, :, cols],
                                                                  bdec[rows, p:p + 1], new, ALU.mult, ALU.add)
                        if hh == 0:
                            last.then_inc(step, 1)
                            steps[0] += 1
                    last.then_inc(s_ready, 1)
                    dve.wait_ge(step, steps[0])
                    dve.wait_ge(s_ready, 3 * p + ch + 1)

            def gate(p):
                for b in range(2):
                    tok = slice(b * BANK, (b + 1) * BANK)
                    dve.wait_ge(sq_done, 2 * p + b + 1)
                    nc.vector.scalar_tensor_tensor(ga[:, p % (2 * GP), tok], c.ps[:, 6 + b, :], nw[:, p:p + 1],
                                                   ga[:, p % (2 * GP), tok], ALU.mult, ALU.mult).then_inc(ga_done, 1)

            def add_outputs(g):
                for t in range(TT):
                    j = a_jobs(GP * (g + 1)) - TT + t
                    dve.wait_ge(a_done, j + 1)
                    if g == 0:
                        nc.vector.tensor_copy(y[:, t, :], c.ps[:, 2 + j % 2, :]).then_inc(a_moved, 1)
                    else:
                        nc.vector.tensor_tensor(y[:, t, :], c.ps[:, 2 + j % 2, :], y[:, t, :], ALU.add).then_inc(a_moved, 1)

            for p in range(PAIRS):
                mask_products(p)
                decay_keys(p)
                states(p)
                gate(p)
                if p % GP == GP - 1:
                    add_outputs(p // GP)

    sum_done, ms_done, rs_done = c.sem("d_sum_done"), c.sem("d_ms_done"), c.sem("d_rs_done")
    with nc.Block() as block:
        @block.tensor
        def _(pe):
            for t in range(TT):
                last = nc.tensor.matmul(c.ps[:, 0, t:t + 1], sqsum[:, t * P:(t + 1) * P], ones[:], start=True, stop=True)
            last.then_inc(sum_done, 1)

        @block.vector
        def _(dve):
            dve.wait_ge(sum_done, 1)
            nc.vector.tensor_scalar(c.var_eps[:], c.ps[:, 0, 0:TT], 1.0 / F, 1e-5, ALU.mult, ALU.add).then_inc(ms_done, 1)
            dve.wait_ge(rs_done, 1)
            for t in range(TT):
                nc.vector.scalar_tensor_tensor(c.x[:, t, :], y[:, t, :], ms[:, t:t + 1], c.x[:, t, :], ALU.mult, ALU.add)

        @block.gpsimd
        def _(pool):
            pool.wait_ge(ms_done, 1)
            nc.gpsimd.tensor_tensor(ms[:], c.var_eps[:], c.neg_half[:], ALU.pow).then_inc(rs_done, 1)



def gated_cross_attention(c):
    nc = c.nc
    H, DH, KEYS = 16, 32, 1024
    ST = CTX // P
    W = P + 1
    ctxT = c.at("e_ctxT", [P, KD, CTX], F32, 52)
    qF = c.at("e_qF", [P, KD, TOK], F32, 52)
    gF = c.at("e_gF", [P, KD, TOK], F32, 68)
    kf = c.at("e_kf", [P, ST, DM], F32, 84)
    v = c.at("e_v", [P, ST, KD, W], F32, 116)
    wkT = c.at("e_wkT", [P, KD, DM], F32, 149)
    wvT = c.at("e_wvT", [P, KD, DM], F32, 157)
    wqT = c.at("e_wqT", [P, KD, DM], F32, 165)
    wgT = c.at("e_wgT", [P, KD, DM], F32, 173)
    woT = c.at("e_woT", [P, KD, DM], F32, 181)
    ex = c.at("e_ex", [P, 2, BANK], F32, 189)
    kv = c.at("e_kv", [P, 2, KD, P], F32, 193)
    gz = c.at("e_gz", [P, 2, BANK], F32, 197)
    z = c.at("e_z", [H, TOK], F32, 201)
    ksum = c.at("e_ksum", [P, 2, KD, H], F32, 205)
    blocks = c.at("e_blocks", [P, P], F32, 205.5)
    heads = c.at("e_heads", [P, KD, H], F32, 206)
    headsT = c.at("e_headsT", [H, KD, P], F32, 46)
    bg = c.at("e_bg", [P, KD], F32, 50.5)

    in_k, in_v, in_w, in_b, in_h = (c.sem(f"e_{n}") for n in ("in_k", "in_v", "in_w", "in_b", "in_h"))
    in_ctx = [c.sem(f"e_in_ctx{n}") for n in range(4)]
    with nc.Block() as block:
        @block.sync
        def _(sp):
            sp.dma_start(wkT[:], tiled(c.dram["e_wkT"])).then_inc(in_k, 16)
            for n in range(4):
                sp.dma_start(ctxT[:, :, n * BANK:(n + 1) * BANK],
                             tiled(c.dram["ctxT"])[:, :, n * BANK:(n + 1) * BANK]).then_inc(in_ctx[n], 16)
                if n == 0:
                    sp.dma_start(wvT[:], tiled(c.dram["e_wvT"])).then_inc(in_v, 16)
            for w, name in ((wqT, "e_wqT"), (wgT, "e_wgT"), (woT, "e_woT")):
                sp.dma_start(w[:], tiled(c.dram[name])).then_inc(in_w, 16)
            sp.dma_start(bg[:], c.dram["e_bg"]).then_inc(in_b, 16)
            sp.dma_start(blocks[:], c.dram["e_blocks"]).then_inc(in_b, 16)
            sp.dma_start(heads[:], c.dram["e_heads"]).then_inc(in_b, 16)

    k_done, k_exp, k_min, k_ready = (c.sem(f"e_{n}") for n in ("k_done", "k_exp", "k_min", "k_ready"))
    v_done, v_ready, ones_set = c.sem("e_v_done"), c.sem("e_v_ready"), c.sem("e_ones_set")
    normed, aggr_done, rstd_done = c.sem("e_normed"), c.sem("e_aggr_done"), c.sem("e_rstd_done")
    with nc.Block() as block:
        @block.tensor
        def _(pe):
            pe.wait_ge(in_k, 16)
            pe.wait_ge(in_v, 16)
            for j in range(ST):
                pe.wait_ge(in_ctx[j // 4], 16)
                for bank, wT, freed, done in ((j % 4, wkT, k_ready, k_done), (4 + j % 4, wvT, v_ready, v_done)):
                    if j >= 4:
                        pe.wait_ge(freed, j - 3)
                    for k in range(KD):
                        last = nc.tensor.matmul(c.ps[:, bank, :], ctxT[:, k, j * P:(j + 1) * P], wT[:, k, :],
                                                start=k == 0, stop=k == KD - 1)
                    last.then_inc(done, 1)

        @block.scalar
        def _(act):
            for j in range(ST):
                act.wait_ge(k_done, j + 1)
                if j >= 2:
                    act.wait_ge(k_ready, j - 1)
                nc.scalar.activation(ex[:, j % 2, :], c.ps[:, j % 4, :], ACT.Relu, scale=-1.0).then_inc(k_min, 1)
                act.wait_ge(k_min, j + 1)
                nc.scalar.activation(ex[:, j % 2, :], ex[:, j % 2, :], ACT.Exp, scale=-1.0).then_inc(k_exp, 1)
                act.wait_ge(v_done, j + 1)
                nc.scalar.activation(v[:, j, :, 0:P], c.ps[:, 4 + j % 4, :].rearrange("p (k d) -> p k d", k=KD),
                                     ACT.Copy).then_inc(v_ready, 1)

        @block.gpsimd
        def _(pool):
            nc.gpsimd.memset(v[:, :, :, P:W], 1.0)
            rstd_pool(c, aggr_done, rstd_done)

        @block.vector
        def _(dve):
            layernorm_dve(c, "e", aggr_done, rstd_done, normed)
            for j in range(ST):
                dve.wait_ge(k_exp, j + 1)
                nc.vector.scalar_tensor_tensor(kf[:, j, :], c.ps[:, j % 4, :], 0.0, ex[:, j % 2, :],
                                               ALU.max, ALU.add).then_inc(k_ready, 1)

    turn_normed(c, "e")

    kv_done, kv_ready = c.sem("e_kv_done"), c.sem("e_kv_ready")
    q_done, q_exp, q_min, q_ready = (c.sem(f"e_{n}") for n in ("q_done", "q_exp", "q_min", "q_ready"))
    g_done, g_ready = c.sem("e_g_done"), c.sem("e_g_ready")
    JOBS = [(n, m) for n in range(2) for m in range(KD)]
    with nc.Block() as block:
        @block.sync
        def _(sp):
            sp.dma_start(headsT[:], c.dram["e_headsT"]).then_inc(in_h, 16)
            sp.wait_ge(in_h, 16)

        @block.tensor
        def _(pe):
            for b in range(2):
                for m in range(KD):
                    for s in range(ST // 2):
                        t = b * ST // 2 + s
                        last = nc.tensor.matmul(c.ps[:, 2 * b + m // 2, m % 2 * W:(m % 2 + 1) * W],
                                                kf[:, t, m * P:(m + 1) * P], v[:, t, m, :],
                                                start=s == 0, stop=s == ST // 2 - 1)
                last.then_inc(kv_done, 1)
            pe.wait_ge(in_w, 48)
            for j, (n, m) in enumerate(JOBS):
                if j >= 2:
                    pe.wait_ge(q_ready, j - 1)
                for k in range(KD):
                    last = nc.tensor.matmul(c.ps[:, 4 + j % 2, :], wqT[:, k, m * P:(m + 1) * P],
                                            c.xF[:, k, n * BANK:(n + 1) * BANK], start=k == 0, stop=k == KD - 1)
                last.then_inc(q_done, 1)
            for j, (n, m) in enumerate(JOBS):
                if j >= 2:
                    pe.wait_ge(g_ready, j - 1)
                for k in range(KD):
                    last = nc.tensor.matmul(c.ps[:, 6 + j % 2, :], wgT[:, k, m * P:(m + 1) * P],
                                            c.xF[:, k, n * BANK:(n + 1) * BANK], start=k == 0, stop=k == KD - 1)
                last.then_inc(g_done, 1)

        @block.scalar
        def _(act):
            for j, (n, m) in enumerate(JOBS):
                act.wait_ge(q_done, j + 1)
                if j >= 2:
                    act.wait_ge(q_ready, j - 1)
                nc.scalar.activation(ex[:, j % 2, :], c.ps[:, 4 + j % 2, :], ACT.Relu, scale=-1.0).then_inc(q_min, 1)
                act.wait_ge(q_min, j + 1)
                nc.scalar.activation(ex[:, j % 2, :], ex[:, j % 2, :], ACT.Exp, scale=-1.0).then_inc(q_exp, 1)
            act.wait_ge(in_b, 48)
            for j, (n, m) in enumerate(JOBS):
                act.wait_ge(g_done, j + 1)
                nc.scalar.activation(gF[:, m, n * BANK:(n + 1) * BANK], c.ps[:, 6 + j % 2, :], ACT.Sigmoid,
                                     bias=bg[:, m:m + 1]).then_inc(g_ready, 1)

        @block.vector
        def _(dve):
            dve.wait_ge(in_b, 48)
            for b in range(2):
                dve.wait_ge(kv_done, b + 1)
                for m in range(KD):
                    col = m % 2 * W
                    nc.vector.tensor_tensor(kv[:, b, m, :], c.ps[:, 2 * b + m // 2, col:col + P], blocks[:], ALU.mult)
                    nc.vector.tensor_scalar(ksum[:, b, m, :], heads[:, m, :], c.ps[:, 2 * b + m // 2, col + P:col + W],
                                            None, ALU.mult)
            for j, (n, m) in enumerate(JOBS):
                dve.wait_ge(q_exp, j + 1)
                nc.vector.scalar_tensor_tensor(qF[:, m, n * BANK:(n + 1) * BANK], c.ps[:, 4 + j % 2, :], 0.0, ex[:, j % 2, :],
                                               ALU.max, ALU.add).then_inc(q_ready, 1)

    den_done, z_step, zb_done, gz_done, num_done, ag_done = (
        c.sem(f"e_{n}") for n in ("den_done", "z_step", "zb_done", "gz_done", "num_done", "ag_done"))
    out_done, added = c.sem("e_out_done"), c.sem("e_added")
    with nc.Block() as block:
        @block.tensor
        def _(pe):
            for b in range(2):
                for m in range(KD):
                    last = nc.tensor.matmul(c.ps[0:H, b, :], ksum[:, b, m, :], qF[:, m, b * BANK:(b + 1) * BANK],
                                            start=m == 0, stop=m == KD - 1)
                last.then_inc(den_done, 1)
            for j, (b, m) in enumerate(JOBS):
                if j >= 2:
                    pe.wait_ge(ag_done, j - 1)
                nc.tensor.matmul(c.ps[:, 4 + j % 2, :], kv[:, b, m, :], qF[:, m, b * BANK:(b + 1) * BANK],
                                 start=True, stop=True).then_inc(num_done, 1)
                pe.wait_ge(z_step, 2 * (b + 1))
                nc.tensor.matmul(c.ps[:, 2 + j % 2, :], headsT[:, m, :], z[:, b * BANK:(b + 1) * BANK],
                                 start=True, stop=True).then_inc(zb_done, 1)
            for t in range(TT):
                pe.wait_ge(ag_done, KD * (1 + t // 4))
                if t >= 2:
                    pe.wait_ge(added, t - 1)
                for k in range(KD):
                    last = nc.tensor.matmul(c.ps[:, 6 + t % 2, :], gF[:, k, t * P:(t + 1) * P], woT[:, k, :],
                                            start=k == 0, stop=k == KD - 1)
                last.then_inc(out_done, 1)

        @block.vector
        def _(dve):
            for b in range(2):
                dve.wait_ge(den_done, b + 1)
                nc.vector.tensor_scalar(z[:, b * BANK:(b + 1) * BANK], c.ps[0:H, b, :], 1e-6, None, ALU.add).then_inc(z_step, 1)
                dve.wait_ge(z_step, 2 * b + 1)
                nc.vector.reciprocal(z[:, b * BANK:(b + 1) * BANK], z[:, b * BANK:(b + 1) * BANK]).then_inc(z_step, 1)
            for j, (b, m) in enumerate(JOBS):
                tok = slice(b * BANK, (b + 1) * BANK)
                dve.wait_ge(zb_done, j + 1)
                nc.vector.tensor_tensor(gz[:, j % 2, :], c.ps[:, 2 + j % 2, :], gF[:, m, tok], ALU.mult).then_inc(gz_done, 1)
                dve.wait_ge(gz_done, j + 1)
                nc.vector.tensor_tensor(gF[:, m, tok], c.ps[:, 4 + j % 2, :], gz[:, j % 2, :], ALU.mult).then_inc(ag_done, 1)
            for t in range(TT):
                dve.wait_ge(out_done, t + 1)
                nc.vector.tensor_tensor(c.x[:, t, :], c.ps[:, 6 + t % 2, :], c.x[:, t, :], ALU.add).then_inc(added, 1)



MX = 32
FP8_ROUND = 1.5 * 2.0 ** 20
FP8_SMALL = 2.0 ** -6


def mx_rows(c, step, done, src, aux, scale, inv):
    nc, dve = c.nc, c.nc.vector
    blocks = src.rearrange("p (b m) -> p b m", m=MX)
    wide = [P, src.shape[-1] // MX, MX]

    def chained(ins):
        done[0] += 1
        ins.then_inc(step, 1)
        dve.wait_ge(step, done[0])

    chained(nc.vector.tensor_reduce(scale, blocks, AX.X, ALU.max, apply_absolute_value=True))
    chained(nc.vector.tensor_scalar(scale, scale, 1.0 / 448.0, 1e-30, ALU.mult, ALU.max))
    chained(nc.vector.reciprocal(inv, scale))
    chained(nc.vector.tensor_tensor(blocks, blocks, inv.unsqueeze(2).to_broadcast(wide), ALU.mult))
    chained(nc.vector.tensor_scalar(aux.bitcast(U32), src.bitcast(U32), 0x7F800000, None, ALU.bitwise_and))
    chained(nc.vector.tensor_scalar(aux, aux, FP8_SMALL, FP8_ROUND, ALU.max, ALU.mult))
    chained(nc.vector.tensor_tensor(src, src, aux, ALU.add))
    chained(nc.vector.tensor_tensor(src, src, aux, ALU.subtract))
    return nc.vector.tensor_tensor(blocks, blocks, scale.unsqueeze(2).to_broadcast(wide), ALU.mult)


def mx_feed_forward(c):
    nc = c.nc
    INTER = 2048
    KI, NI = INTER // P, INTER // BANK
    gT = c.at("f_gT", [P, KD, INTER], F32, 52)
    uT = c.at("f_uT", [P, KD, INTER], F32, 84)
    dT = c.at("f_dT", [P, KI, DM], F32, 116)
    w = c.at("f_w", [P, 2, INTER], F32, 148)
    h = c.at("f_h", [P, 2, INTER], F32, 164)
    hF = c.at("f_hF", [P, KI, P], F32, 180)
    aux = c.at("f_aux", [P, INTER], F32, 188)
    silu = c.at("f_silu", [P, 2, BANK], F32, 196)
    scale = c.at("f_scale", [P, INTER // MX], F32, 200)
    inv = c.at("f_inv", [P, INTER // MX], F32, 200.5)
    step = c.sem("f_step")
    in_w = [c.sem(f"f_in_w{i}") for i in range(2)]
    w_ready, w_turned, w_moved = c.sem("f_w_ready"), c.sem("f_w_turned"), c.sem("f_w_moved")
    normed, aggr_done, rstd_done = c.sem("f_normed"), c.sem("f_aggr_done"), c.sem("f_rstd_done")
    done = [0]
    WJOBS = [("f_g", gT, i) for i in range(4)] + [("f_u", uT, i) for i in range(4)] + [("f_d", dT, i) for i in range(4)]

    with nc.Block() as block:
        @block.sync
        def _(sp):
            for j, (name, _, i) in enumerate(WJOBS):
                if j >= 2:
                    sp.wait_ge(w_turned, 4 * (j - 1))
                if name == "f_d":
                    sp.dma_start(w[:, j % 2, :], c.dram[name][i * P:(i + 1) * P, :]).then_inc(in_w[j % 2], 16)
                else:
                    sp.dma_start(w[:, j % 2, :].rearrange("p (m n) -> p m n", m=4),
                                 tiled(c.dram[name][i * DM:(i + 1) * DM, :])).then_inc(in_w[j % 2], 16)

        @block.gpsimd
        def _(pool):
            rstd_pool(c, aggr_done, rstd_done)

        @block.vector
        def _(dve):
            for j in range(len(WJOBS)):
                dve.wait_ge(in_w[j % 2], 16 * (j // 2 + 1))
                mx_rows(c, step, done, w[:, j % 2, :], aux[:], scale[:], inv[:]).then_inc(w_ready, 1)
                dve.wait_ge(w_ready, j + 1)
            layernorm_dve(c, "f", aggr_done, rstd_done, normed)
            dve.wait_ge(normed, TT)
            for i in range(2):
                mx_rows(c, step, done, c.xn[:, 4 * i:4 * i + 4, :].rearrange("p t n -> p (t n)"), aux[:], scale[:],
                        inv[:]).then_inc(normed, 1)
                dve.wait_ge(normed, TT + i + 1)

        @block.tensor
        def _(pe):
            for j, (name, _, i) in enumerate(WJOBS):
                pe.wait_ge(w_ready, j + 1)
                for q in range(4):
                    if j >= 1:
                        pe.wait_ge(w_moved, 4 * (j - 1) + q + 1)
                    for r in range(4):
                        block_ = 4 * q + r if name == "f_d" else 4 * r + q
                        last = nc.tensor.transpose(c.ps[:, q, r * P:(r + 1) * P], w[:, j % 2, block_ * P:(block_ + 1) * P], c.ident[:])
                    last.then_inc(w_turned, 1)

        @block.scalar
        def _(act):
            for j, (name, wT, i) in enumerate(WJOBS):
                for q in range(4):
                    act.wait_ge(w_turned, 4 * j + q + 1)
                    if name == "f_d":
                        nc.scalar.activation(wT[:, 4 * q:4 * q + 4, i * P:(i + 1) * P],
                                             c.ps[:, q, :].rearrange("p (k o) -> p k o", k=4), ACT.Copy).then_inc(w_moved, 1)
                    else:
                        nc.scalar.activation(wT[:, q, i * BANK:(i + 1) * BANK], c.ps[:, q, :], ACT.Copy).then_inc(w_moved, 1)

    turn_normed(c, "f")

    g_done, u_done, silu_done, h_done, hq_done = (c.sem(f"f_{n}") for n in ("g_done", "u_done", "silu_done", "h_done", "hq_done"))
    h_turned, h_moved, out_done, added = (c.sem(f"f_{n}") for n in ("h_turned", "h_moved", "out_done", "added"))
    with nc.Block() as block:
        @block.tensor
        def _(pe):
            def up(t):
                for n in range(NI):
                    j = NI * t + n
                    for bank, wT, freed, done_ in ((j % 2, gT, silu_done, g_done), (2 + j % 2, uT, h_done, u_done)):
                        if j >= 2:
                            pe.wait_ge(freed, j - 1)
                        for k in range(KD):
                            last = nc.tensor.matmul(c.ps[:, bank, :], c.xF[:, k, t * P:(t + 1) * P],
                                                    wT[:, k, n * BANK:(n + 1) * BANK], start=k == 0, stop=k == KD - 1)
                        last.then_inc(done_, 1)

            def down(t):
                pe.wait_ge(hq_done, t + 1)
                for q in range(4):
                    if 4 * t + q >= 2:
                        pe.wait_ge(h_moved, 4 * t + q - 1)
                    for r in range(4):
                        k = 4 * q + r
                        last = nc.tensor.transpose(c.ps[:, 4 + q % 2, r * P:(r + 1) * P], h[:, t % 2, k * P:(k + 1) * P], c.ident[:])
                    last.then_inc(h_turned, 1)
                if t >= 2:
                    pe.wait_ge(added, t - 1)
                for k in range(KI):
                    if k % 4 == 0:
                        pe.wait_ge(h_moved, 4 * t + k // 4 + 1)
                    last = nc.tensor.matmul(c.ps[:, 6 + t % 2, :], hF[:, k, :], dT[:, k, :], start=k == 0, stop=k == KI - 1)
                last.then_inc(out_done, 1)

            up(0)
            for t in range(TT):
                if t + 1 < TT:
                    up(t + 1)
                down(t)

        @block.scalar
        def _(act):
            def silus(t):
                for n in range(NI):
                    j = NI * t + n
                    act.wait_ge(g_done, j + 1)
                    if j >= 2:
                        act.wait_ge(h_done, j - 1)
                    nc.scalar.activation(silu[:, j % 2, :], c.ps[:, j % 2, :], ACT.Silu).then_inc(silu_done, 1)

            silus(0)
            for t in range(TT):
                if t + 1 < TT:
                    silus(t + 1)
                if t >= 1:
                    act.wait_ge(out_done, t)
                for q in range(4):
                    act.wait_ge(h_turned, 4 * t + q + 1)
                    nc.scalar.activation(hF[:, 4 * q:4 * q + 4, :].rearrange("p k t -> p (k t)"), c.ps[:, 4 + q % 2, :],
                                         ACT.Copy).then_inc(h_moved, 1)

        @block.vector
        def _(dve):
            def hidden(t):
                if t >= 2:
                    dve.wait_ge(h_turned, 4 * (t - 1))
                for n in range(NI):
                    j = NI * t + n
                    dve.wait_ge(silu_done, j + 1)
                    dve.wait_ge(u_done, j + 1)
                    nc.vector.tensor_tensor(h[:, t % 2, n * BANK:(n + 1) * BANK], c.ps[:, 2 + j % 2, :], silu[:, j % 2, :],
                                            ALU.mult).then_inc(h_done, 1)
                dve.wait_ge(h_done, NI * (t + 1))
                mx_rows(c, step, done, h[:, t % 2, :], aux[:], scale[:], inv[:]).then_inc(hq_done, 1)
                dve.wait_ge(hq_done, t + 1)

            hidden(0)
            for t in range(TT):
                if t + 1 < TT:
                    hidden(t + 1)
                dve.wait_ge(out_done, t + 1)
                nc.vector.tensor_tensor(c.x[:, t, :], c.ps[:, 6 + t % 2, :], c.x[:, t, :], ALU.add).then_inc(added, 1)


def store_result(c):
    nc, stored = c.nc, c.stored
    with nc.Block() as block:
        @block.sync
        def _(sp):
            sp.dma_start(tiled(c.out), c.x[:]).then_inc(stored, 16)
            sp.wait_ge(stored, 16)


STAGES = [mixer, cross_attention, experts, linear_attention, gated_cross_attention, mx_feed_forward]


def build(nc, dram, out, phases=range(6)):
    c = Core(nc, dram, out)
    for stage in (load_constants, *(STAGES[s] for s in phases), store_result):
        c.stage_sems = []
        stage(c)
        nc.clear_and_free_semaphores(c.stage_sems)
        nc.all_engine_barrier()


def _layout(i):
    c = np.ascontiguousarray
    a = {}
    a["x"] = c(i["x"].reshape(TOK, DM))
    a["c_ident"] = np.eye(P, dtype=np.float32)
    w = i["L0_attn_W_in"]
    a["winx"] = c(w[:1024])
    a["winzT"] = c(w[1024:].T)
    a["convT"] = c(i["L0_attn_conv_w"].T)
    a["woutT"] = c(i["L0_attn_W_out"].T)
    a["Dv"] = c(i["L0_attn_D"].reshape(8, P).T)
    a["ctxT"] = c(i["ctx_2048"].reshape(CTX, DM).T)
    wkv = i["L0_xattn_wkv"]
    a["b_wkT"], a["b_wvT"] = c(wkv[:512].T), c(wkv[512:].T)
    a["b_wq"], a["b_wp"] = c(i["L0_xattn_wq"]), c(i["L0_xattn_wp"])
    bkv = i["L0_xattn_bkv"]
    a["b_bq"], a["b_bk"] = c(i["L0_xattn_bq"].reshape(4, P).T), c(bkv[:512].reshape(4, P).T)
    a["b_bv"], a["b_bp"] = c(bkv[512:]), c(i["L0_xattn_bp"])
    a["c_s1T"], a["c_sgT"], a["c_s2T"] = (c(i[f"L0_ffn_{n}"].T) for n in ("sw1", "swg", "sw2"))
    a["c_wdT"], a["c_wupT"], a["c_wgT"] = (c(i[f"L0_ffn_{n}"].T) for n in ("Wdown", "Wup", "Wg"))
    a["c_r1T"], a["c_rgT"], a["c_r2T"] = (c(i[f"L0_ffn_{n}"].transpose(0, 2, 1)) for n in ("rw1", "rwg", "rw2"))
    a["c_bias"] = c(i["L0_ffn_biases"])
    qkv = i["L1_attn_qkv_w"].reshape(32, 3, 64, DM)

    def by_pair(w):
        return c(w.reshape(16, P, KD, P).transpose(0, 3, 2, 1))
    a["d_wq"], a["d_wk"], a["d_wg"] = by_pair(qkv[:, 0]), by_pair(qkv[:, 1]), by_pair(i["L1_attn_gate_w"])
    a["d_wvT"] = c(qkv[:, 2].reshape(2048, DM).T)
    a["d_woT"] = c(i["L1_attn_out_w"].T)
    a["d_nw"] = c(i["L1_attn_norm_w"].reshape(16, P).T)
    slope = (2.0 ** (-8.0 / 32)) ** np.arange(1, 33) * (1 + 1e-5)
    r = np.arange(1, P + 1)
    gap = r[None, :] - r[:, None]
    mask = np.where(gap[:, None, :] >= 0, np.exp(-slope[None, :, None] * np.maximum(gap, 0)[:, None, :]), 0.0)
    a["d_mask"] = c(mask.astype(np.float32))
    a["d_qdec"] = c(np.repeat(np.exp(-slope[:, None] * r), 64, 0).reshape(16, P, P).transpose(1, 0, 2).astype(np.float32))
    a["d_kdec"] = c(np.exp(-slope[None, :] * (P - r)[:, None]).astype(np.float32))
    a["d_bdec"] = c(np.repeat(np.exp(-slope * P), 64).reshape(16, P).T.astype(np.float32))
    wkv = i["L1_xattn_Wkv"]
    a["e_wkT"], a["e_wvT"] = c(wkv[:512].T), c(wkv[512:].T)
    a["e_wqT"], a["e_wgT"], a["e_woT"] = (c(i[f"L1_xattn_{n}"].T) for n in ("Wq", "Wg", "Wo"))
    a["e_bg"] = c(i["L1_xattn_bg"].reshape(4, P).T)
    head = np.arange(DM) // 32
    a["e_blocks"] = (head[:P, None] == head[None, :P]).astype(np.float32)
    belongs = (head[:, None] == np.arange(16)).astype(np.float32).reshape(KD, P, 16)
    a["e_heads"], a["e_headsT"] = c(belongs.transpose(1, 0, 2)), c(belongs.transpose(2, 0, 1))
    a["f_g"], a["f_u"], a["f_d"] = (c(i[f"L1_ffn_{n}_w"]) for n in ("gate", "up", "down"))
    return a


def kernel(**inputs):
    import concourse.bacc as _bacc
    from concourse.bass_utils import run_bass_kernel_spmd as _run

    nc = _bacc.Bacc("TRN2", target_bir_lowering=False, num_devices=1)
    arrays = {f"in_{k}": v for k, v in _layout({k: np.asarray(v) for k, v in inputs.items()}).items()}
    dram = {k[3:]: nc.dram_tensor(k, v.shape, mybir.dt.from_np(v.dtype), kind="ExternalInput").ap()
            for k, v in arrays.items()}
    out = nc.dram_tensor("out_0", (TOK, DM), F32, kind="ExternalOutput").ap()
    build(nc, dram, out)
    r = _run(nc, [arrays], core_ids=[0])
    return r.results[0]["out_0"].reshape(2, 512, 512)
```

```python
import numpy as np
import concourse.bass as bass
from concourse import mybir

F32 = mybir.dt.float32
BF16 = mybir.dt.bfloat16
U32 = mybir.dt.uint32
F32R = mybir.dt.float32r
ALU = mybir.AluOpType
ACT = mybir.ActivationFunctionType
AX = mybir.AxisListType

P = 128
TOK, DM = 1024, 512
TT, KD = TOK // P, DM // P
BANK = 512
CTX = 2048


class Core:

    def __init__(self, nc, dram, out):
        self.nc, self.dram, self.out = nc, dram, out
        self.base = -(-nc.sbuf_base // 64) * 64
        self.x = self.at("x", [P, TT, DM], F32, 0)
        self.xF = self.at("xF", [P, KD, TOK], F32, 16)
        self.xn = self.at("xn", [P, TT, DM], F32, 32)
        self.ident = self.at("ident", [P, P], F32, 48)
        self.identb = self.at("identb", [P, P], BF16, 48.5)
        self.stats = self.at("stats", [P, TT, 6], F32, 48.75)
        self.mv = self.at("mv", [P, TT, 2], F32, 49)
        self.rstd = self.at("rstd", [P, TT], F32, 49.125)
        self.var_eps = self.at("var_eps", [P, TT], F32, 49.25)
        self.neg_half = self.at("neg_half", [P, TT], F32, 49.375)
        self.stored = nc.alloc_semaphore("stored")
        self.ps = nc.alloc_psum_tensor("ps", [P, 8, BANK], F32)

    def at(self, name, shape, dt, kb):
        off = self.base + int(kb * 1024)
        return self.nc.alloc_sbuf_tensor_at(name, shape, dt, offset=off)

    def sem(self, name):
        s = self.nc.alloc_semaphore(name)
        self.stage_sems.append(s)
        return s


def tiled(ap):
    return ap.rearrange("(k p) n -> p k n", p=P)


def load_constants(c):
    nc = c.nc
    loaded = c.sem("const_loaded")
    identb_ready = c.sem("identb_ready")
    with nc.Block() as block:
        @block.sync
        def _(sp):
            sp.dma_start(c.x[:], tiled(c.dram["x"])).then_inc(loaded, 16)
            sp.dma_start(c.ident[:], c.dram["c_ident"]).then_inc(loaded, 16)
            sp.wait_ge(loaded, 32)

        @block.gpsimd
        def _(pool):
            nc.gpsimd.memset(c.neg_half[:], -0.5)

        @block.vector
        def _(dve):
            dve.wait_ge(loaded, 32)
            nc.vector.tensor_copy(c.identb[:], c.ident[:]).then_inc(identb_ready, 1)
            dve.wait_ge(identb_ready, 1)


def rstd_pool(c, aggr_done, rstd_done):
    c.nc.gpsimd.wait_ge(aggr_done, TT + 1)
    c.nc.gpsimd.tensor_tensor(c.rstd[:], c.var_eps[:], c.neg_half[:], ALU.pow).then_inc(rstd_done, 1)


def layernorm_dve(c, tag, aggr_done, rstd_done, normed):
    nc, dve = c.nc, c.nc.vector
    stats_done = c.sem(f"{tag}_stats_done")
    for t in range(TT):
        nc.vector.bn_stats(c.stats[:, t, :], c.x[:, t, :]).then_inc(stats_done, 1)
    for t in range(TT):
        dve.wait_ge(stats_done, t + 1)
        nc.vector.bn_aggr(c.mv[:, t, :], c.stats[:, t, :]).then_inc(aggr_done, 1)
    dve.wait_ge(aggr_done, TT)
    nc.vector.tensor_scalar(c.var_eps[:], c.mv[:, :, 1], 1e-5, None, ALU.add).then_inc(aggr_done, 1)
    dve.wait_ge(rstd_done, 1)
    for t in range(TT):
        nc.vector.tensor_scalar(c.xn[:, t, :], c.x[:, t, :], c.mv[:, t, 0:1], c.rstd[:, t:t + 1],
                                ALU.subtract, ALU.mult).then_inc(normed, 1)


def norm_and_transpose(c, tag, extra_pe=None, extra_act=None):
    nc = c.nc
    normed, turned = c.sem(f"{tag}_normed"), c.sem(f"{tag}_turned")
    moved_act, moved_dve = c.sem(f"{tag}_moved_act"), c.sem(f"{tag}_moved_dve")
    aggr_done, rstd_done = c.sem(f"{tag}_aggr_done"), c.sem(f"{tag}_rstd_done")
    with nc.Block() as block:
        @block.gpsimd
        def _(pool):
            rstd_pool(c, aggr_done, rstd_done)

        @block.vector
        def _(dve):
            layernorm_dve(c, tag, aggr_done, rstd_done, normed)
            for t in range(1, TT, 2):
                dve.wait_ge(turned, t + 1)
                nc.vector.tensor_copy(c.xF[:, :, t * P:(t + 1) * P],
                                      c.ps[:, t, :].rearrange("p (k t) -> p k t", k=KD)).then_inc(moved_dve, 1)
            dve.wait_ge(moved_dve, TT // 2)

        @block.scalar
        def _(act):
            for t in range(0, TT, 2):
                act.wait_ge(turned, t + 1)
                nc.scalar.activation(c.xF[:, :, t * P:(t + 1) * P],
                                     c.ps[:, t, :].rearrange("p (k t) -> p k t", k=KD), ACT.Copy).then_inc(moved_act, 1)
            act.wait_ge(moved_act, TT // 2)

        @block.tensor
        def _(pe):
            for t in range(TT):
                pe.wait_ge(normed, t + 1)
                for k in range(KD):
                    last = nc.tensor.transpose(c.ps[:, t, k * P:(k + 1) * P], c.xn[:, t, k * P:(k + 1) * P], c.ident[:])
                last.then_inc(turned, 1)


def turn_normed(c, tag):
    nc = c.nc
    turned = c.sem(f"{tag}_turned")
    moved_act, moved_dve = c.sem(f"{tag}_moved_act"), c.sem(f"{tag}_moved_dve")
    with nc.Block() as block:
        @block.vector
        def _(dve):
            for t in range(1, TT, 2):
                dve.wait_ge(turned, t + 1)
                nc.vector.tensor_copy(c.xF[:, :, t * P:(t + 1) * P],
                                      c.ps[:, t, :].rearrange("p (k t) -> p k t", k=KD)).then_inc(moved_dve, 1)

        @block.scalar
        def _(act):
            for t in range(0, TT, 2):
                act.wait_ge(turned, t + 1)
                nc.scalar.activation(c.xF[:, :, t * P:(t + 1) * P],
                                     c.ps[:, t, :].rearrange("p (k t) -> p k t", k=KD), ACT.Copy).then_inc(moved_act, 1)

        @block.tensor
        def _(pe):
            for t in range(TT):
                for k in range(KD):
                    last = nc.tensor.transpose(c.ps[:, t, k * P:(k + 1) * P], c.xn[:, t, k * P:(k + 1) * P], c.ident[:])
                last.then_inc(turned, 1)



def mixer(c):
    nc = c.nc
    INTER = 1024
    KI = INTER // P
    winx = c.at("a_winx", [P, KI, DM], F32, 52)
    convT = c.at("a_convT", [P, KI, INTER], F32, 68)
    winzT = c.at("a_winzT", [P, KD, INTER], F32, 100)
    wpT = c.at("a_wpT", [P, KD, INTER], F32, 116)
    woutT = c.at("a_woutT", [P, KI, DM], F32, 132)
    g = c.at("a_g", [P, KI, TOK], F32, 148)
    sz = c.at("a_sz", [P, 2, BANK], F32, 180)
    Dv = c.at("a_D", [P, KI], F32, 50)
    in_x, in_rest = c.sem("a_in_x"), c.sem("a_in_rest")
    in_conv = [c.sem(f"a_in_conv{h}") for h in range(2)]

    with nc.Block() as block:
        @block.sync
        def _(sp):
            sp.dma_start(winx[:], tiled(c.dram["winx"])).then_inc(in_x, 16)
            for h in range(2):
                sp.dma_start(convT[:, :, h * BANK:(h + 1) * BANK],
                             tiled(c.dram["convT"])[:, :, h * BANK:(h + 1) * BANK]).then_inc(in_conv[h], 16)
            sp.dma_start(winzT[:], tiled(c.dram["winzT"])).then_inc(in_rest, 16)
            sp.dma_start(woutT[:], tiled(c.dram["woutT"])).then_inc(in_rest, 16)
            sp.dma_start(Dv[:], c.dram["Dv"]).then_inc(in_rest, 16)

    fused, fused_moved = c.sem("a_fused"), c.sem("a_fused_moved")
    with nc.Block() as block:
        @block.tensor
        def _(pe):
            pe.wait_ge(in_x, 16)
            for n in range(2):
                pe.wait_ge(in_conv[n], 16)
                for m in range(KD):
                    for k in range(KI):
                        last = nc.tensor.matmul(c.ps[:, n * KD + m, :], winx[:, k, m * P:(m + 1) * P],
                                                convT[:, k, n * BANK:(n + 1) * BANK], start=k == 0, stop=k == KI - 1)
                    last.then_inc(fused, 1)

        @block.scalar
        def _(act):
            for j in range(2 * KD):
                n, m = j // KD, j % KD
                act.wait_ge(fused, j + 1)
                nc.scalar.activation(wpT[:, m, n * BANK:(n + 1) * BANK], c.ps[:, j, :], ACT.Copy).then_inc(fused_moved, 1)
            act.wait_ge(fused_moved, 2 * KD)

    norm_and_transpose(c, "a_ln")

    z_done, y_done, silu_done, g_done = (c.sem(f"a_{n}") for n in ("z_done", "y_done", "silu_done", "g_done"))
    out_done, added = c.sem("a_out_done"), c.sem("a_added")
    JOBS = [(n, m) for n in range(2) for m in range(KI)]
    with nc.Block() as block:
        @block.tensor
        def _(pe):
            pe.wait_ge(in_rest, 48)
            for j, (n, m) in enumerate(JOBS):
                tok = slice(n * BANK, (n + 1) * BANK)
                if j >= 2:
                    pe.wait_ge(silu_done, j - 1)
                for k in range(KD):
                    last = nc.tensor.matmul(c.ps[:, j % 2, :], winzT[:, k, m * P:(m + 1) * P], c.xF[:, k, tok],
                                            start=k == 0, stop=k == KD - 1)
                last.then_inc(z_done, 1)
                if j >= 2:
                    pe.wait_ge(g_done, j - 1)
                for k in range(KD):
                    last = nc.tensor.matmul(c.ps[:, 2 + j % 2, :], wpT[:, k, m * P:(m + 1) * P], c.xF[:, k, tok],
                                            start=k == 0, stop=k == KD - 1)
                last.then_inc(y_done, 1)
            for t in range(TT):
                pe.wait_ge(g_done, KI * (1 + t // (TT // 2)))
                if t >= 4:
                    pe.wait_ge(added, t - 3)
                for k in range(KI):
                    last = nc.tensor.matmul(c.ps[:, 4 + t % 4, :], g[:, k, t * P:(t + 1) * P], woutT[:, k, :],
                                            start=k == 0, stop=k == KI - 1)
                last.then_inc(out_done, 1)

        @block.scalar
        def _(act):
            for j, (n, m) in enumerate(JOBS):
                act.wait_ge(z_done, j + 1)
                if j >= 2:
                    act.wait_ge(g_done, j - 1)
                nc.scalar.activation(sz[:, j % 2, :], c.ps[:, j % 2, :], ACT.Silu).then_inc(silu_done, 1)

        @block.vector
        def _(dve):
            for j, (n, m) in enumerate(JOBS):
                dve.wait_ge(y_done, j + 1)
                dve.wait_ge(silu_done, j + 1)
                nc.vector.scalar_tensor_tensor(g[:, m, n * BANK:(n + 1) * BANK], c.ps[:, 2 + j % 2, :], Dv[:, m:m + 1],
                                               sz[:, j % 2, :], ALU.mult, ALU.mult).then_inc(g_done, 1)
            for t in range(TT):
                dve.wait_ge(out_done, t + 1)
                nc.vector.tensor_tensor(c.x[:, t, :], c.ps[:, 4 + t % 4, :], c.x[:, t, :], ALU.add).then_inc(added, 1)
            dve.wait_ge(added, TT)



ROUND = 1.5 * 2.0 ** 23


def int8_rows(c, tag, src, ints, scale, n, start=None):
    nc, dve = c.nc, c.nc.vector
    step = c.sem(f"{tag}_step")
    inv = c.at(f"{tag}_inv", [P, n], F32, 50.5)
    nc.vector.tensor_reduce(scale[:], src[:], AX.X, ALU.max, apply_absolute_value=True).then_inc(step, 1)
    dve.wait_ge(step, 1)
    nc.vector.tensor_scalar(scale[:], scale[:], 1.0 / 127.0, 1e-8, ALU.mult, ALU.max).then_inc(step, 1)
    dve.wait_ge(step, 2)
    nc.vector.reciprocal(inv[:], scale[:]).then_inc(step, 1)
    dve.wait_ge(step, 3)
    for j in range(n):
        nc.vector.tensor_scalar(src[:, j, :], src[:, j, :], inv[:, j:j + 1], ROUND, ALU.mult, ALU.add).then_inc(step, 1)
    for j in range(n):
        dve.wait_ge(step, 4 + j)
        last = nc.vector.tensor_scalar(ints[:, j, :], src[:, j, :], -ROUND, None, ALU.add)
    return last


def cross_attention(c):
    nc = c.nc
    H, DH, KEYS = 16, 32, 1024
    KT = KEYS // P
    KF = c.at("b_KF", [P, KD, CTX], F32, 52)
    V = c.at("b_V", [P, CTX // P, H, DH], F32, 84)
    wpT = c.at("b_wpT", [P, KD, DM], BF16, 117)
    bv = c.at("b_bv", [P, DM], F32, 121)
    swp_row = c.at("b_swp_row", [P, DM], F32, 121)
    wqT = c.at("b_wqT", [P, KD, DM], BF16, 123)
    wq_int = c.at("b_wq_int", [P, KD, DM], BF16, 127)
    wp_int = c.at("b_wp_int", [P, KD, DM], BF16, 131)
    xq = c.at("b_xq", [P, TT, DM], BF16, 135)
    wkT = c.at("b_wkT", [P, KD, DM], F32, 143)
    wvT = c.at("b_wvT", [P, KD, DM], F32, 151)
    wq = c.at("b_wq", [P, KD, DM], F32, 159)
    wp = c.at("b_wp", [P, KD, DM], F32, 167)
    ctxT = c.at("b_ctxT", [P, KD, CTX], F32, 175)
    xqF = c.at("b_xqF", [P, KD, TOK], BF16, 143)
    sx_row = c.at("b_sx_row", [P, TOK], F32, 151)
    q_raw = c.at("b_q_raw", [P, 2, BANK], F32, 155)
    qF = c.at("b_qF", [P, KD, TOK], F32, 16)
    o = c.at("b_o", [P, TT, DM], F32, 32)
    kS = c.at("b_kS", [P, 2, 4, KEYS], F32R, 123)
    qS = c.at("b_qS", [P, 2, 4, BANK], F32R, 155)
    k_parts = c.at("b_k_parts", [P, 2, KEYS], F32R, 171)
    q_parts = c.at("b_q_parts", [P, 2, BANK], F32R, 179)
    pr = c.at("b_pr", [P, 2, BANK], F32, 183)
    pr_hi = c.at("b_pr_hi", [P, 3, BANK], F32R, 187)
    pr_lo = c.at("b_pr_lo", [P, 3, BANK], F32R, 193)
    oT = c.at("b_oT", [2 * DH + 1, BANK], F32, 199)
    VS = c.at("b_VS", [P, 2, KT, 2 * DH + 1], F32R, 201)
    nm_parts = c.at("b_nm_parts", [16, 2, 2, P], F32R, 205.25)
    nm = c.at("b_nm", [P, 2, 16], F32, 207.3125)
    oinv = c.at("b_oinv", [P, 2, 4], F32, 207.4375)
    fold = c.at("b_fold", [2 * DH + 1, DH + 1], F32, 116)
    mark = c.at("b_mark", [1, 1], F32, 116.25)
    oq = c.at("b_oq", [P, TT, DM], BF16, 123)
    oqF = c.at("b_oqF", [P, KD, TOK], BF16, 131)
    bq = c.at("b_bq", [P, KD], F32, 50.0625)
    bk = c.at("b_bk", [P, KD], F32, 50.125)
    sx = c.at("b_sx", [P, TT], F32, 50.1875)
    swq = c.at("b_swq", [P, KD], F32, 50.25)
    swp = c.at("b_swp", [P, KD], F32, 50.3125)
    so = c.at("b_so", [P, TT], F32, 50.375)
    bp = c.at("b_bp", [P, DM], F32, 30)

    in_k, in_v, in_wq, in_b = c.sem("b_in_k"), c.sem("b_in_v"), c.sem("b_in_wq"), c.sem("b_in_b")
    in_ctx = [c.sem(f"b_in_ctx{n}") for n in range(4)]
    with nc.Block() as block:
        @block.sync
        def _(sp):
            sp.dma_start(wkT[:], tiled(c.dram["b_wkT"])).then_inc(in_k, 16)
            for n in range(4):
                sp.dma_start(ctxT[:, :, n * BANK:(n + 1) * BANK],
                             tiled(c.dram["ctxT"])[:, :, n * BANK:(n + 1) * BANK]).then_inc(in_ctx[n], 16)
            sp.dma_start(wvT[:], tiled(c.dram["b_wvT"])).then_inc(in_v, 16)
            sp.dma_start(wq[:], tiled(c.dram["b_wq"])).then_inc(in_wq, 16)
            sp.dma_start(wp[:], tiled(c.dram["b_wp"])).then_inc(in_wq, 16)
            sp.dma_start(bq[:], c.dram["b_bq"]).then_inc(in_b, 16)
            sp.dma_start(bk[:], c.dram["b_bk"]).then_inc(in_b, 16)
            sp.dma_start(bv[:], c.dram["b_bv"].partition_broadcast(P)).then_inc(in_b, 16)
            sp.dma_start(bp[:], c.dram["b_bp"].partition_broadcast(P)).then_inc(in_b, 16)

    k_done, k_moved, v_done, v_moved = (c.sem(f"b_{n}") for n in ("k_done", "k_moved", "v_done", "v_moved"))
    normed, aggr_done, rstd_done = c.sem("b_normed"), c.sem("b_aggr_done"), c.sem("b_rstd_done")
    with nc.Block() as block:
        @block.tensor
        def _(pe):
            pe.wait_ge(in_k, 16)
            for n in range(4):
                pe.wait_ge(in_ctx[n], 16)
                for m in range(KD):
                    j = n * KD + m
                    if j >= 4:
                        pe.wait_ge(k_moved, j - 3)
                    for k in range(KD):
                        last = nc.tensor.matmul(c.ps[:, j % 4, :], wkT[:, k, m * P:(m + 1) * P],
                                                ctxT[:, k, n * BANK:(n + 1) * BANK], start=k == 0, stop=k == KD - 1)
                    last.then_inc(k_done, 1)
            pe.wait_ge(in_v, 16)
            for j in range(CTX // P):
                if j >= 4:
                    pe.wait_ge(v_moved, j - 3)
                for k in range(KD):
                    last = nc.tensor.matmul(c.ps[:, 4 + j % 4, :], ctxT[:, k, j * P:(j + 1) * P], wvT[:, k, :],
                                            start=k == 0, stop=k == KD - 1)
                last.then_inc(v_done, 1)

        @block.scalar
        def _(act):
            act.wait_ge(in_b, 64)
            for j in range(4 * KD):
                n, m = j // KD, j % KD
                act.wait_ge(k_done, j + 1)
                nc.scalar.activation(KF[:, m, n * BANK:(n + 1) * BANK], c.ps[:, j % 4, :], ACT.Identity,
                                     bias=bk[:, m:m + 1]).then_inc(k_moved, 1)

        @block.gpsimd
        def _(pool):
            rstd_pool(c, aggr_done, rstd_done)

        @block.vector
        def _(dve):
            layernorm_dve(c, "b", aggr_done, rstd_done, normed)
            dve.wait_ge(normed, TT)
            int8_rows(c, "b_x8", c.xn, xq, sx, TT)
            dve.wait_ge(in_wq, 32)
            int8_rows(c, "b_wq8", wq, wq_int, swq, KD)
            int8_rows(c, "b_wp8", wp, wp_int, swp, KD)
            dve.wait_ge(in_b, 64)
            for t in range(TT):
                nc.vector.tensor_tensor(c.x[:, t, :], c.x[:, t, :], bp[:], ALU.add)
            for j in range(CTX // P):
                dve.wait_ge(v_done, j + 1)
                nc.vector.tensor_tensor(V[:, j, :, :], c.ps[:, 4 + j % 4, :].rearrange("p (h d) -> p h d", h=H),
                                        bv[:].rearrange("p (h d) -> p h d", h=H), ALU.add).then_inc(v_moved, 1)

    turned, turned_act, turned_dve = c.sem("b_turned"), c.sem("b_turned_act"), c.sem("b_turned_dve")
    spread, spread_moved = c.sem("b_spread"), c.sem("b_spread_moved")
    SOURCES = ([(wq_int, wqT, m) for m in range(KD)] + [(wp_int, wpT, m) for m in range(KD)]
               + [(xq, xqF, t) for t in range(TT)])

    def turn_target(j):
        _, dst, m = SOURCES[j]
        return dst[:, :, m * P:(m + 1) * P]

    def turned_bank(j):
        return c.ps[:, j % 4, 0:BANK // 2].bitcast(BF16).rearrange("p (k t) -> p k t", k=KD)

    with nc.Block() as block:
        @block.tensor
        def _(pe):
            for j, (src, _, m) in enumerate(SOURCES):
                if j >= 4 and j % 2 == 0:
                    pe.wait_ge(turned_act, (j - 4) // 2 + 1)
                elif j >= 4:
                    pe.wait_ge(turned_dve, (j - 4) // 2 + 1)
                for k in range(KD):
                    last = nc.tensor.transpose(turned_bank(j)[:, k, :], src[:, m, k * P:(k + 1) * P], c.identb[:])
                last.then_inc(turned, 1)
            for t in range(TT):
                last = nc.tensor.matmul(c.ps[:, 4 + t // 4, t % 4 * P:(t % 4 + 1) * P],
                                        sx[:, t:t + 1].to_broadcast([P, P]), c.ident[:], start=True, stop=True)
            last.then_inc(spread, 1)
            for m in range(KD):
                last = nc.tensor.matmul(c.ps[:, 6, m * P:(m + 1) * P],
                                        swp[:, m:m + 1].to_broadcast([P, P]), c.ident[:], start=True, stop=True)
            last.then_inc(spread, 1)

        @block.scalar
        def _(act):
            for j in range(0, len(SOURCES), 2):
                act.wait_ge(turned, j + 1)
                nc.scalar.activation(turn_target(j), turned_bank(j), ACT.Copy).then_inc(turned_act, 1)
            act.wait_ge(spread, 1)
            nc.scalar.activation(sx_row[:].rearrange("p (a n) -> p a n", a=2), c.ps[:, 4:6, :], ACT.Copy)
            act.wait_ge(spread, 2)
            nc.scalar.activation(swp_row[:], c.ps[:, 6, :], ACT.Copy).then_inc(spread_moved, 1)

        @block.vector
        def _(dve):
            for j in range(1, len(SOURCES), 2):
                dve.wait_ge(turned, j + 1)
                nc.vector.tensor_copy(turn_target(j), turned_bank(j)).then_inc(turned_dve, 1)

    q_done, q_scaled, q_ready = c.sem("b_q_done"), c.sem("b_q_scaled"), c.sem("b_q_ready")
    with nc.Block() as block:
        @block.tensor
        def _(pe):
            for j in range(2 * KD):
                n, m = j // KD, j % KD
                for k in range(KD):
                    last = nc.tensor.matmul(c.ps[:, j, :], wqT[:, k, m * P:(m + 1) * P],
                                            xqF[:, k, n * BANK:(n + 1) * BANK], start=k == 0, stop=k == KD - 1)
                last.then_inc(q_done, 1)

        @block.vector
        def _(dve):
            for j in range(2 * KD):
                n, m = j // KD, j % KD
                dve.wait_ge(q_done, j + 1)
                if j >= 2:
                    dve.wait_ge(q_ready, j - 1)
                nc.vector.scalar_tensor_tensor(q_raw[:, j % 2, :], c.ps[:, j, :], swq[:, m:m + 1],
                                               sx_row[:, n * BANK:(n + 1) * BANK], ALU.mult, ALU.mult).then_inc(q_scaled, 1)

        @block.gpsimd
        def _(pool):
            for j in range(2 * KD):
                n, m = j // KD, j % KD
                pool.wait_ge(q_scaled, j + 1)
                nc.gpsimd.tensor_scalar(qF[:, m, n * BANK:(n + 1) * BANK], q_raw[:, j % 2, :], bq[:, m:m + 1],
                                        DH ** -0.5, ALU.add, ALU.mult).then_inc(q_ready, 1)

    GROUPS = [(b, f) for b in range(2) for f in range(KD)]
    NG, QT = len(GROUPS), BANK // P
    STEPS, UNITS = 4 * KT, 4 * QT
    HEADS, NS = 4 * NG, NG * STEPS
    LAG = 2
    in_st = [[c.sem(f"b_in_st{i}{h}") for h in range(4)] for i in range(2)]
    in_rows = [c.sem(f"b_in_rows{i}") for i in range(2)]
    split_done, vsplit_done = c.sem("b_split_done"), c.sem("b_vsplit_done")
    job_done, job_read = c.sem("b_job_done"), c.sem("b_job_read")
    nm_split, ones_set, vones_set, fold_set = (c.sem(f"b_{n}") for n in ("nm_split", "ones_set", "vones_set", "fold_set"))
    st_done, exp_done, hi_done, lo_done, av_done = (c.sem(f"b_{n}") for n in ("st_done", "exp_done", "hi_done", "lo_done", "av_done"))
    o_moved, inv_done = c.sem("b_o_moved"), c.sem("b_inv_done")

    JOBS, JOBS_AT = [("max", 0, u) for u in range(UNITS)] + [("turn", 0, 0)], []
    FIRST_JOBS = len(JOBS)
    for n in range(NS + 8):
        g, i, here = n // STEPS, n % STEPS, len(JOBS)
        if g + 1 < NG and i % 4 != 3 and i - i // 4 < UNITS:
            JOBS.append(("max", g + 1, i - i // 4))
        if n >= 12 and (n - 12) % KT == 0 and (n - 12) // KT < HEADS:
            JOBS.append(("head", (n - 12) // KT, 0))
        if g + 1 < NG and i == 3 * KT:
            JOBS.append(("turn", g + 1, 0))
        JOBS_AT.append(range(here, len(JOBS)))

    with nc.Block() as block:
        @block.gpsimd
        def _(pool):
            def split_group(g, part):
                b, f = GROUPS[g]
                k, q = KF[:, f, b * KEYS:(b + 1) * KEYS], qF[:, f, b * BANK:(b + 1) * BANK]
                if part == 0 and g >= 1:
                    for h in range(4):
                        pool.wait_ge(in_st[(g - 1) % 2][h], 96 * ((g - 1) // 2 + 1))
                src, parts = ((k, k_parts), (q, q_parts))[part % 2]
                if part < 2:
                    nc.gpsimd.tensor_copy(parts[:, 0, :], src).then_inc(split_done, 1)
                else:
                    pool.wait_ge(split_done, 4 * g + part - 1)
                    nc.gpsimd.tensor_tensor(parts[:, 1, :], src, parts[:, 0, :].bitcast(F32), ALU.subtract).then_inc(split_done, 1)

            def split_values(q, part):
                (b, f), h = GROUPS[q // 4], q % 4
                src = V[:, b * KT:(b + 1) * KT, 4 * f + h, :]
                if part == 0:
                    if q >= 2:
                        pool.wait_ge(av_done, KT * (q - 1))
                    nc.gpsimd.tensor_copy(VS[:, q % 2, :, 0:DH], src).then_inc(vsplit_done, 1)
                else:
                    pool.wait_ge(vsplit_done, 2 * q + 1)
                    nc.gpsimd.tensor_tensor(VS[:, q % 2, :, DH:2 * DH], src, VS[:, q % 2, :, 0:DH].bitcast(F32),
                                            ALU.subtract).then_inc(vsplit_done, 1)

            for part in range(4):
                split_group(0, part)
            for part in range(2):
                split_values(0, part)
            for part in range(4):
                split_group(1, part)
            for n in range(NS):
                g, i = n // STEPS, n % STEPS
                if i in range(4, 8) and g + 2 < NG:
                    split_group(g + 2, i - 4)
                if i % KT in range(2, 4) and n // KT + 1 < HEADS:
                    split_values(n // KT + 1, i % KT - 2)

        @block.sync
        def _(sp):
            def stack(g, h):
                s_, rows = g % 2, slice(h * DH, (h + 1) * DH)
                sp.wait_ge(split_done, 4 * (g + 1))
                if g >= 2:
                    sp.wait_ge(st_done, STEPS * (g - 2) + KT * (h + 1))
                for place, part in enumerate((0, 0, 1)):
                    sp.dma_start(kS[place * DH:(place + 1) * DH, s_, h, :].bitcast(F32),
                                 k_parts[rows, part, :].bitcast(F32)).then_inc(in_st[s_][h], 16)
                for place, part in enumerate((0, 1, 0)):
                    sp.dma_start(qS[place * DH:(place + 1) * DH, s_, h, :].bitcast(F32),
                                 q_parts[rows, part, :].bitcast(F32)).then_inc(in_st[s_][h], 16)

            def maxima(g):
                s_ = g % 2
                sp.wait_ge(nm_split, 2 * (g + 1))
                for part in range(2):
                    for h in range(4):
                        sp.dma_start(qS[96 + part:97 + part, s_, h, :].bitcast(F32),
                                     nm_parts[h * QT:(h + 1) * QT, s_, part, :].bitcast(F32)).then_inc(in_rows[s_], 16)

            for h in range(4):
                stack(0, h)
            for g in range(NG):
                for h in range(3):
                    if g + 1 < NG:
                        stack(g + 1, h)
                maxima(g)
                if g + 1 < NG:
                    stack(g + 1, 3)

        @block.tensor
        def _(pe):
            def job(j):
                kind, g, u = JOBS[j]
                banks = 2 * (j % 2)
                if j >= 2:
                    pe.wait_ge(job_read, j - 1)
                if kind == "max":
                    h, t, s_ = u // QT, u % QT, g % 2
                    if t == 0:
                        pe.wait_ge(in_st[s_][h], 96 * (g // 2 + 1))
                    for n in range(2):
                        last = nc.tensor.matmul(c.ps[:, banks + n, :], qS[0:96, s_, h, t * P:(t + 1) * P],
                                                kS[0:96, s_, h, n * BANK:(n + 1) * BANK], start=True, stop=True)
                elif kind == "turn":
                    pe.wait_ge(job_read, j)
                    last = nc.tensor.transpose(c.ps[0:16, banks, 0:P], nm[:, g % 2, :], c.ident[:])
                else:
                    pe.wait_ge(o_moved, g + 1)
                    for t in range(QT):
                        last = nc.tensor.matmul(c.ps[:, banks, t * (DH + 1):(t + 1) * (DH + 1)],
                                                oT[:, t * P:(t + 1) * P], fold[:], start=True, stop=True)
                last.then_inc(job_done, 1)

            def scores(n):
                g, h, k = n // STEPS, n % STEPS // KT, n % KT
                if n % STEPS == 0:
                    pe.wait_ge(in_rows[g % 2], 128 * (g // 2 + 1))
                if n >= 2:
                    pe.wait_ge(hi_done, n - 1)
                nc.tensor.matmul(c.ps[:, 4 + n % 2, :], kS[0:98, g % 2, h, k * P:(k + 1) * P], qS[0:98, g % 2, h, :],
                                 start=True, stop=True).then_inc(st_done, 1)

            def weigh(n):
                q, k = n // KT, n % KT
                if k == 0:
                    pe.wait_ge(vsplit_done, 2 * (q + 1))
                    if q >= 2:
                        pe.wait_ge(o_moved, q - 1)
                pe.wait_ge(hi_done, n + 1)
                nc.tensor.matmul(c.ps[0:2 * DH + 1, 6 + q % 2, :], VS[:, q % 2, k, :], pr_hi[:, n % 3, :],
                                 start=k == 0, stop=False)
                pe.wait_ge(lo_done, n + 1)
                nc.tensor.matmul(c.ps[0:2 * DH + 1, 6 + q % 2, :], VS[:, q % 2, k, :], pr_lo[:, n % 3, :],
                                 start=False, stop=k == KT - 1).then_inc(av_done, 1)

            for j in range(FIRST_JOBS):
                job(j)
            pe.wait_ge(ones_set, 1)
            pe.wait_ge(vones_set, 1)
            pe.wait_ge(fold_set, 3)
            for n in range(NS + 8):
                if n < NS:
                    scores(n)
                for j in JOBS_AT[n]:
                    job(j)
                if LAG <= n < NS + LAG:
                    weigh(n - LAG)

        @block.scalar
        def _(act):
            def move_result(q):
                act.wait_ge(av_done, KT * (q + 1))
                if q >= 1:
                    act.wait_ge(job_done, JOBS.index(("head", q - 1, 0)) + 1)
                nc.scalar.activation(oT[:], c.ps[0:2 * DH + 1, 6 + q % 2, :], ACT.Copy).then_inc(o_moved, 1)

            for n in range(NS + 3):
                if n < NS:
                    act.wait_ge(st_done, n + 1)
                    if n >= 2:
                        act.wait_ge(lo_done, n - 1)
                    nc.scalar.activation(pr[:, n % 2, :], c.ps[:, 4 + n % 2, :], ACT.Exp).then_inc(exp_done, 1)
                    if n >= 3:
                        act.wait_ge(av_done, n - 2)
                    nc.scalar.activation(pr_hi[:, n % 3, :], c.ps[:, 4 + n % 2, :], ACT.Exp).then_inc(hi_done, 1)
                if n >= 10 and (n - 10) % KT == 0:
                    move_result((n - 10) // KT)

        @block.vector
        def _(dve):
            def job(j):
                kind, g, u = JOBS[j]
                banks = 2 * (j % 2)
                dve.wait_ge(job_done, j + 1)
                if kind == "max":
                    nc.vector.tensor_reduce(nm[:, g % 2, u:u + 1], c.ps[:, banks:banks + 2, :], AX.XY, ALU.max,
                                            negate=True).then_inc(job_read, 1)
                elif kind == "turn":
                    turned = c.ps[0:16, banks, 0:P]
                    if g >= 2:
                        dve.wait_ge(in_rows[g % 2], 128 * (g // 2))
                    nc.vector.tensor_copy(nm_parts[:, g % 2, 0, :], turned).then_inc(nm_split, 1)
                    dve.wait_ge(nm_split, 2 * g + 1)
                    nc.vector.tensor_tensor(nm_parts[:, g % 2, 1, :], turned, nm_parts[:, g % 2, 0, :].bitcast(F32),
                                            ALU.subtract).then_inc(nm_split, 1)
                    dve.wait_ge(nm_split, 2 * (g + 1))
                    nc.vector.memset(mark[:], 0.0).then_inc(job_read, 1)
                else:
                    (b, f), h = GROUPS[g // 4], g % 4
                    acc = c.ps[:, banks, 0:QT * (DH + 1)].rearrange("p (t d) -> p t d", t=QT)
                    nc.vector.reciprocal(oinv[:, g % 2, :], acc[:, :, DH]).then_inc(inv_done, 1)
                    dve.wait_ge(inv_done, g + 1)
                    nc.vector.tensor_tensor(o[:, QT * b:QT * (b + 1), (4 * f + h) * DH:(4 * f + h + 1) * DH], acc[:, :, 0:DH],
                                            oinv[:, g % 2, :].unsqueeze(2).to_broadcast([P, QT, DH]), ALU.mult).then_inc(job_read, 1)

            nc.vector.memset(kS[96:98, :, :, :].bitcast(F32), 1.0).then_inc(ones_set, 1)
            nc.vector.memset(VS[:, :, :, 2 * DH:].bitcast(F32), 1.0).then_inc(vones_set, 1)
            nc.vector.tensor_copy(fold[0:DH, :], c.ident[0:DH, 0:DH + 1]).then_inc(fold_set, 1)
            nc.vector.tensor_copy(fold[DH:2 * DH, :], c.ident[DH:2 * DH, DH:2 * DH + 1]).then_inc(fold_set, 1)
            nc.vector.tensor_copy(fold[2 * DH:2 * DH + 1, :], c.ident[2 * DH:2 * DH + 1, DH:2 * DH + 1]).then_inc(fold_set, 1)
            for j in range(FIRST_JOBS):
                job(j)
            for n in range(NS + 8):
                for j in JOBS_AT[n]:
                    job(j)
                if n < NS:
                    dve.wait_ge(exp_done, n + 1)
                    dve.wait_ge(hi_done, n + 1)
                    if n >= 3:
                        dve.wait_ge(av_done, n - 2)
                    nc.vector.tensor_tensor(pr_lo[:, n % 3, :], pr[:, n % 2, :], pr_hi[:, n % 3, :].bitcast(F32),
                                            ALU.subtract).then_inc(lo_done, 1)
            dve.wait_ge(job_read, len(JOBS))
            int8_rows(c, "b_o8", o, oq, so, TT)

    oturned, oturned_moved, out_done, out_scaled = (c.sem(f"b_{n}") for n in ("oturned", "oturned_moved", "out_done", "out_scaled"))
    added = c.sem("b_added")
    tmp = c.at("b_tmp", [P, 2, DM], F32, 139)
    with nc.Block() as block:
        def obank(t):
            return c.ps[:, t % 4, 0:BANK // 2].bitcast(BF16).rearrange("p (k t) -> p k t", k=KD)

        @block.tensor
        def _(pe):
            for t in range(TT + 1):
                if t < TT:
                    if t >= 4:
                        pe.wait_ge(oturned_moved, t - 3)
                    for k in range(KD):
                        last = nc.tensor.transpose(obank(t)[:, k, :], oq[:, t, k * P:(k + 1) * P], c.identb[:])
                    last.then_inc(oturned, 1)
                if t >= 1:
                    t0 = t - 1
                    pe.wait_ge(oturned_moved, t0 + 1)
                    if t0 >= 4:
                        pe.wait_ge(out_scaled, t0 - 3)
                    for k in range(KD):
                        last = nc.tensor.matmul(c.ps[:, 4 + t0 % 4, :], oqF[:, k, t0 * P:(t0 + 1) * P], wpT[:, k, :],
                                                start=k == 0, stop=k == KD - 1)
                    last.then_inc(out_done, 1)

        @block.scalar
        def _(act):
            for t in range(TT):
                act.wait_ge(oturned, t + 1)
                nc.scalar.activation(oqF[:, :, t * P:(t + 1) * P], obank(t), ACT.Copy).then_inc(oturned_moved, 1)

        @block.vector
        def _(dve):
            for t in range(TT):
                dve.wait_ge(out_done, t + 1)
                if t >= 2:
                    dve.wait_ge(added, t - 1)
                nc.vector.scalar_tensor_tensor(tmp[:, t % 2, :], c.ps[:, 4 + t % 4, :], so[:, t:t + 1], swp_row[:],
                                               ALU.mult, ALU.mult).then_inc(out_scaled, 1)

        @block.gpsimd
        def _(pool):
            for t in range(TT):
                pool.wait_ge(out_scaled, t + 1)
                nc.gpsimd.tensor_tensor(c.x[:, t, :], c.x[:, t, :], tmp[:, t % 2, :], ALU.add).then_inc(added, 1)



def experts(c):
    nc = c.nc
    E, LAT, HID, SCALE = 16, 128, 256, 2.5
    KH = HID // P
    s1T = c.at("c_s1T", [P, KD, HID], F32, 52)
    sgT = c.at("c_sgT", [P, KD, HID], F32, 56)
    s2T = c.at("c_s2T", [P, KH, DM], F32, 60)
    wdT = c.at("c_wdT", [P, KD, LAT], F32, 64)
    wupT = c.at("c_wupT", [P, DM], F32, 66)
    wgT = c.at("c_wgT", [P, KD, E], F32, 68)
    bias = c.at("c_bias", [P, E], F32, 68.5)
    r1T = c.at("c_r1T", [P, E, HID], F32, 72)
    rgT = c.at("c_rgT", [P, E, HID], F32, 88)
    r2T = c.at("c_r2T", [P, E, KH, LAT], F32, 104)
    sF = c.at("c_sF", [P, KH, TOK], F32, 120)
    xlF = c.at("c_xlF", [P, TOK], F32, 128)
    acc = c.at("c_acc", [P, TT, LAT], F32, 132)
    accF = c.at("c_accF", [P, TOK], F32, 136)
    hF = c.at("c_hF", [P, 2, KH, TOK], F32, 140)
    relu = c.at("c_relu", [P, 2, BANK], F32, 156)
    sq = c.at("c_sq", [P, 2, BANK], F32, 160)
    prob = c.at("c_prob", [P, TT, E], F32, 164)
    sel = c.at("c_sel", [P, TT, E], F32, 164.5)
    rest = c.at("c_rest", [P, TT, E], F32, 165)
    top = c.at("c_top", [P, TT, 8], F32, 165.5)
    w = c.at("c_w", [P, TT, E], F32, 166)
    total = c.at("c_total", [P, TT], F32, 166.5)

    in_s, in_r1, in_r2 = c.sem("c_in_s"), c.sem("c_in_r1"), c.sem("c_in_r2")
    with nc.Block() as block:
        @block.sync
        def _(sp):
            sp.dma_start(wdT[:], tiled(c.dram["c_wdT"])).then_inc(in_s, 16)
            sp.dma_start(wgT[:], tiled(c.dram["c_wgT"])).then_inc(in_s, 16)
            sp.dma_start(s1T[:], tiled(c.dram["c_s1T"])).then_inc(in_s, 16)
            sp.dma_start(sgT[:], tiled(c.dram["c_sgT"])).then_inc(in_s, 16)
            sp.dma_start(s2T[:], tiled(c.dram["c_s2T"])).then_inc(in_s, 16)
            sp.dma_start(wupT[:], c.dram["c_wupT"]).then_inc(in_s, 16)
            sp.dma_start(bias[:], c.dram["c_bias"].partition_broadcast(P)).then_inc(in_s, 16)
            sp.dma_start(r1T[:], c.dram["c_r1T"].rearrange("e p n -> p e n")).then_inc(in_r1, 16)
            sp.dma_start(rgT[:], c.dram["c_rgT"].rearrange("e p n -> p e n")).then_inc(in_r1, 16)
            sp.dma_start(r2T[:], c.dram["c_r2T"].rearrange("e (k p) n -> p e k n", p=P)).then_inc(in_r2, 16)

    norm_and_transpose(c, "c_ln")

    lat_done, lat_moved, logit_done, prob_done = (c.sem(f"c_{n}") for n in ("lat_done", "lat_moved", "logit_done", "prob_done"))
    sg_done, s1_done, relu_done, sq_done, sh_done = (c.sem(f"c_{n}") for n in ("sg_done", "s1_done", "relu_done", "sq_done", "sh_done"))
    step = c.sem("c_step")
    JOBS = [(n, m) for n in range(2) for m in range(KH)]
    with nc.Block() as block:
        @block.tensor
        def _(pe):
            pe.wait_ge(in_s, 112)
            for t in range(TT):
                for k in range(KD):
                    last = nc.tensor.matmul(c.ps[:, 6, t * E:(t + 1) * E], c.xF[:, k, t * P:(t + 1) * P], wgT[:, k, :],
                                            start=k == 0, stop=k == KD - 1)
            last.then_inc(logit_done, 1)
            for n in range(2):
                for k in range(KD):
                    last = nc.tensor.matmul(c.ps[:, 4 + n, :], wdT[:, k, :], c.xF[:, k, n * BANK:(n + 1) * BANK],
                                            start=k == 0, stop=k == KD - 1)
                last.then_inc(lat_done, 1)
            for j, (n, m) in enumerate(JOBS):
                for bank, wT, freed, done in ((j % 2, sgT, relu_done, sg_done), (2 + j % 2, s1T, sh_done, s1_done)):
                    if j >= 2:
                        pe.wait_ge(freed, j - 1)
                    for k in range(KD):
                        last = nc.tensor.matmul(c.ps[:, bank, :], wT[:, k, m * P:(m + 1) * P],
                                                c.xF[:, k, n * BANK:(n + 1) * BANK], start=k == 0, stop=k == KD - 1)
                    last.then_inc(done, 1)

        @block.scalar
        def _(act):
            act.wait_ge(logit_done, 1)
            nc.scalar.activation(prob[:].rearrange("p t e -> p (t e)"), c.ps[:, 6, 0:TT * E], ACT.Sigmoid).then_inc(prob_done, 1)
            for n in range(2):
                act.wait_ge(lat_done, n + 1)
                nc.scalar.activation(xlF[:, n * BANK:(n + 1) * BANK], c.ps[:, 4 + n, :], ACT.Copy).then_inc(lat_moved, 1)
            for j, (n, m) in enumerate(JOBS):
                act.wait_ge(sg_done, j + 1)
                nc.scalar.activation(relu[:, j % 2, :], c.ps[:, j % 2, :], ACT.Relu).then_inc(relu_done, 1)
                act.wait_ge(relu_done, j + 1)
                if j >= 2:
                    act.wait_ge(sh_done, j - 1)
                nc.scalar.activation(sq[:, j % 2, :], relu[:, j % 2, :], ACT.Square).then_inc(sq_done, 1)

        @block.vector
        def _(dve):
            done = [0]

            def chained(ins):
                done[0] += 1
                ins.then_inc(step, 1)
                dve.wait_ge(step, done[0])

            dve.wait_ge(prob_done, 1)
            chained(nc.vector.tensor_tensor(sel[:], prob[:], bias[:].unsqueeze(1).to_broadcast([P, TT, E]), ALU.add))
            for t in range(TT):
                last = nc.vector.max(top[:, t, :], sel[:, t, :])
            chained(last)
            for t in range(TT):
                last = nc.vector.match_replace(rest[:, t, :], top[:, t, :], sel[:, t, :], -3e38)
            chained(last)
            chained(nc.vector.tensor_tensor(sel[:], sel[:], rest[:], ALU.not_equal))
            chained(nc.vector.tensor_tensor(sel[:], sel[:], prob[:], ALU.mult))
            chained(nc.vector.tensor_reduce(total[:], sel[:], AX.X, ALU.add))
            chained(nc.vector.reciprocal(total[:], total[:]))
            chained(nc.vector.tensor_scalar(total[:], total[:], SCALE, None, ALU.mult))
            chained(nc.vector.tensor_tensor(w[:], sel[:], total[:].unsqueeze(2).to_broadcast([P, TT, E]), ALU.mult))
            for j, (n, m) in enumerate(JOBS):
                dve.wait_ge(sq_done, j + 1)
                dve.wait_ge(s1_done, j + 1)
                nc.vector.tensor_tensor(sF[:, m, n * BANK:(n + 1) * BANK], c.ps[:, 2 + j % 2, :], sq[:, j % 2, :],
                                        ALU.mult).then_inc(sh_done, 1)

    UP = [(e, n, m) for e in range(E) for n in range(2) for m in range(KH)]
    g_done, a_done, r_done, q_done, h_done = (c.sem(f"c_e_{n}") for n in ("g_done", "a_done", "r_done", "q_done", "h_done"))
    y_done, y_added = c.sem("c_y_done"), c.sem("c_y_added")
    PER = 2 * KH
    with nc.Block() as block:
        @block.tensor
        def _(pe):
            pe.wait_ge(in_r1, 32)
            pe.wait_ge(in_r2, 16)

            def up(e):
                for i in range(PER):
                    j = e * PER + i
                    _, n, m = UP[j]
                    for bank, wT, freed, done in ((j % 2, rgT, r_done, g_done), (2 + j % 2, r1T, h_done, a_done)):
                        if j >= 2:
                            pe.wait_ge(freed, j - 1)
                        nc.tensor.matmul(c.ps[:, bank, :], wT[:, e, m * P:(m + 1) * P], xlF[:, n * BANK:(n + 1) * BANK],
                                         start=True, stop=True).then_inc(done, 1)

            def down(e):
                pe.wait_ge(h_done, (e + 1) * PER)
                for n in range(2):
                    if e >= 1:
                        pe.wait_ge(y_added, 2 * (e - 1) + n + 1)
                    for i in range(4):
                        t = 4 * n + i
                        for k in range(KH):
                            last = nc.tensor.matmul(c.ps[:, 4 + n, i * LAT:(i + 1) * LAT], hF[:, e % 2, k, t * P:(t + 1) * P],
                                                    r2T[:, e, k, :], start=k == 0, stop=k == KH - 1)
                    last.then_inc(y_done, 1)

            up(0)
            for e in range(E):
                if e + 1 < E:
                    up(e + 1)
                down(e)

        @block.scalar
        def _(act):
            for j, (e, n, m) in enumerate(UP):
                act.wait_ge(g_done, j + 1)
                nc.scalar.activation(relu[:, j % 2, :], c.ps[:, j % 2, :], ACT.Relu).then_inc(r_done, 1)
                act.wait_ge(r_done, j + 1)
                if j >= 2:
                    act.wait_ge(h_done, j - 1)
                nc.scalar.activation(sq[:, j % 2, :], relu[:, j % 2, :], ACT.Square).then_inc(q_done, 1)

        @block.vector
        def _(dve):
            def hidden(e):
                if e >= 2:
                    dve.wait_ge(y_done, 2 * (e - 1))
                for i in range(PER):
                    j = e * PER + i
                    _, n, m = UP[j]
                    dve.wait_ge(a_done, j + 1)
                    dve.wait_ge(q_done, j + 1)
                    nc.vector.tensor_tensor(hF[:, e % 2, m, n * BANK:(n + 1) * BANK], c.ps[:, 2 + j % 2, :], sq[:, j % 2, :],
                                            ALU.mult).then_inc(h_done, 1)

            hidden(0)
            for e in range(E):
                if e + 1 < E:
                    hidden(e + 1)
                for n in range(2):
                    dve.wait_ge(y_done, 2 * e + n + 1)
                    if e >= 1:
                        dve.wait_ge(y_added, 2 * (e - 1) + n + 1)
                    for i in range(4):
                        t = 4 * n + i
                        src = c.ps[:, 4 + n, i * LAT:(i + 1) * LAT]
                        if e == 0:
                            last = nc.vector.tensor_scalar(acc[:, t, :], src, w[:, t, e:e + 1], None, ALU.mult)
                        else:
                            last = nc.vector.scalar_tensor_tensor(acc[:, t, :], src, w[:, t, e:e + 1], acc[:, t, :],
                                                                  ALU.mult, ALU.add)
                    last.then_inc(y_added, 1)

    a_turned, a_moved, out_done, added = (c.sem(f"c_{n}") for n in ("a_turned", "a_moved", "out_done", "added"))
    with nc.Block() as block:
        @block.tensor
        def _(pe):
            for n in range(2):
                for i in range(4):
                    last = nc.tensor.transpose(c.ps[:, n, i * P:(i + 1) * P], acc[:, 4 * n + i, :], c.ident[:])
                last.then_inc(a_turned, 1)
            for t in range(TT):
                pe.wait_ge(a_moved, 1 + t // 4)
                if t >= 4:
                    pe.wait_ge(added, t - 3)
                for k in range(KH):
                    nc.tensor.matmul(c.ps[:, 4 + t % 4, :], sF[:, k, t * P:(t + 1) * P], s2T[:, k, :],
                                     start=k == 0, stop=False)
                nc.tensor.matmul(c.ps[:, 4 + t % 4, :], accF[:, t * P:(t + 1) * P], wupT[:], start=False,
                                 stop=True).then_inc(out_done, 1)

        @block.scalar
        def _(act):
            for n in range(2):
                act.wait_ge(a_turned, n + 1)
                nc.scalar.activation(accF[:, n * BANK:(n + 1) * BANK], c.ps[:, n, :], ACT.Copy).then_inc(a_moved, 1)

        @block.vector
        def _(dve):
            for t in range(TT):
                dve.wait_ge(out_done, t + 1)
                nc.vector.tensor_tensor(c.x[:, t, :], c.ps[:, 4 + t % 4, :], c.x[:, t, :], ALU.add).then_inc(added, 1)



def linear_attention(c):
    nc = c.nc
    H, D = 32, 64
    PAIRS, GP = H // 2, 4
    G, CH = PAIRS // GP, TT // 2
    F = H * D
    at = 52.0

    def take(name, shape, dt, kb):
        nonlocal at
        at += kb
        return c.at(f"d_{name}", shape, dt, at - kb)

    mask = take("mask", [P, 2, 2 * GP, P], F32, 8)
    qdec = take("qdec", [P, 2, GP, P], F32, 4)
    wv = take("wv", [P, 2, KD, DM], F32, 16)
    wq = take("wq", [P, 2, KD, P], F32, 4)
    wk = take("wk", [P, 2, KD, P], F32, 4)
    wg = take("wg", [P, 2, KD, P], F32, 4)
    wo = take("wo", [P, 2, GP, DM], F32, 16)
    v = take("v", [P, TT, DM], F32, 16)
    qF = take("qF", [P, 2, TOK], F32, 8)
    qD = take("qD", [P, 2, TOK], F32, 8)
    kF = take("kF", [P, 2, TOK], F32, 8)
    kT = take("kT", [P, 2, TT, P], F32, 8)
    ga = take("ga", [P, 2 * GP, TOK], F32, 32)
    A = take("A", [P, 2, 2, CH, P], F32, 8)
    S = take("S", [P, CH - 1, 2, P], F32, 3)
    sq = take("sq", [P, 2, BANK], F32, 4)
    sqsum = take("sqsum", [P, TOK], F32, 4)
    y = c.at("d_y", [P, TT, DM], F32, 32)
    kdec = c.at("d_kdec", [P, H], F32, 50.5)
    bdec = c.at("d_bdec", [P, PAIRS], F32, 50.75)
    nw = c.at("d_nw", [P, PAIRS], F32, 51)
    ones = c.at("d_ones", [P, 1], F32, 51.125)
    ms = c.at("d_ms", [P, TT], F32, 51.25)

    in_c = c.sem("d_in_c")
    in_p = [c.sem(f"d_in_p{i}") for i in range(2)]
    in_g = [c.sem(f"d_in_g{i}") for i in range(2)]
    normed, turned = c.sem("d_ln_n"), None
    a_done, a_moved = c.sem("d_a_done"), c.sem("d_a_moved")
    proj_done, proj_moved = c.sem("d_proj_done"), c.sem("d_proj_moved")
    t_done, t_moved = c.sem("d_t_done"), c.sem("d_t_moved")
    u_done, s_ready = c.sem("d_u_done"), c.sem("d_s_ready")
    o_done, sq_done, ga_done = c.sem("d_o_done"), c.sem("d_sq_done"), c.sem("d_ga_done")
    qd_done, sqsum_done = c.sem("d_qd_done"), c.sem("d_sqsum_done")
    step, zeroed = c.sem("d_step"), c.sem("d_zeroed")

    def first_job(p):
        return 6 * p + (0 if p == 0 else TT * (1 + (p - 1) // GP))

    def a_jobs(p):
        return 4 * p + TT * (p // GP)

    with nc.Block() as block:
        @block.sync
        def _(sp):
            sp.dma_start(kdec[:], c.dram["d_kdec"]).then_inc(in_c, 16)
            sp.dma_start(bdec[:], c.dram["d_bdec"]).then_inc(in_c, 16)
            sp.dma_start(nw[:], c.dram["d_nw"]).then_inc(in_c, 16)

    norm_and_transpose(c, "d_ln")

    with nc.Block() as block:
        @block.sync
        def _(sp):
            for p in range(PAIRS):
                if p >= 2:
                    sp.wait_ge(proj_done, first_job(p - 2) + 6)
                for w, name in ((wq, "d_wq"), (wk, "d_wk"), (wg, "d_wg")):
                    sp.dma_start(w[:, p % 2, :, :], c.dram[name][p, :, :, :]).then_inc(in_p[p % 2], 16)
                if p % GP == 0:
                    g = p // GP
                    if g >= 2:
                        sp.wait_ge(a_moved, a_jobs(GP * (g - 1)))
                        sp.wait_ge(qd_done, 2 * GP * (g - 1))
                    sp.dma_start(wv[:, g % 2, :, :], tiled(c.dram["d_wvT"])[:, :, g * DM:(g + 1) * DM]).then_inc(in_g[g % 2], 16)
                    sp.dma_start(mask[:, g % 2, :, :], c.dram["d_mask"][:, g * 2 * GP:(g + 1) * 2 * GP, :]).then_inc(in_g[g % 2], 16)
                    sp.dma_start(qdec[:, g % 2, :, :], c.dram["d_qdec"][:, g * GP:(g + 1) * GP, :]).then_inc(in_g[g % 2], 16)
                    sp.dma_start(wo[:, g % 2, :, :], tiled(c.dram["d_woT"])[:, g * GP:(g + 1) * GP, :]).then_inc(in_g[g % 2], 16)

        @block.tensor
        def _(pe):
            def project(j, w, n):
                if j >= 2:
                    pe.wait_ge(proj_moved, j - 1)
                for k in range(KD):
                    last = nc.tensor.matmul(c.ps[:, j % 2, :], w[:, k, :], c.xF[:, k, n * BANK:(n + 1) * BANK],
                                            start=k == 0, stop=k == KD - 1)
                last.then_inc(proj_done, 1)

            def queries_keys(p):
                pe.wait_ge(in_p[p % 2], 48 * (p // 2 + 1))
                for i in range(4):
                    project(first_job(p) + i, (wq, wk)[i // 2][:, p % 2, :, :], i % 2)

            def gates(p):
                for n in range(2):
                    project(first_job(p) + 4 + n, wg[:, p % 2, :, :], n)

            def values(g):
                pe.wait_ge(in_g[g % 2], 64 * (g // 2 + 1))
                for t in range(TT):
                    j = first_job(GP * g) + 6 + t
                    pe.wait_ge(proj_moved, j - 1)
                    for k in range(KD):
                        last = nc.tensor.matmul(c.ps[:, j % 2, :], c.xF[:, k, t * P:(t + 1) * P], wv[:, g % 2, k, :],
                                                start=k == 0, stop=k == KD - 1)
                    last.then_inc(proj_done, 1)

            def products(p):
                pe.wait_ge(proj_moved, first_job(p) + 4)
                for i in range(4):
                    b, hh = i // 2, i % 2
                    j, rows = a_jobs(p) + i, slice(hh * D, (hh + 1) * D)
                    if j >= 2:
                        pe.wait_ge(a_moved, j - 1)
                    for ch in range(CH):
                        tok = slice((b * CH + ch) * P, (b * CH + ch + 1) * P)
                        last = nc.tensor.matmul(c.ps[:, 2 + j % 2, ch * P:(ch + 1) * P], kF[rows, p % 2, tok], qF[rows, p % 2, tok],
                                                start=True, stop=True)
                    last.then_inc(a_done, 1)

            def turn_keys(p):
                for b in range(2):
                    if p >= 1:
                        pe.wait_ge(s_ready, 3 * p)
                    for ch in range(CH):
                        t = b * CH + ch
                        last = nc.tensor.transpose(c.ps[:, 4 + b, ch * P:(ch + 1) * P], kF[:, p % 2, t * P:(t + 1) * P], c.ident[:])
                    last.then_inc(t_done, 1)

            def updates(p):
                pe.wait_ge(t_moved, 2 * (p + 1))
                if p % GP == 0:
                    pe.wait_ge(proj_moved, first_job(p) + 6 + TT)
                for b in range(2):
                    for ch in range(CH - 1):
                        t = b * CH + ch
                        last = nc.tensor.matmul(c.ps[:, 4 + b, ch * P:(ch + 1) * P], kT[:, p % 2, t, :],
                                                v[:, t, p % GP * P:(p % GP + 1) * P], start=True, stop=True)
                last.then_inc(u_done, 1)

            def outputs(p):
                pe.wait_ge(s_ready, 3 * (p + 1))
                pe.wait_ge(qd_done, 2 * (p + 1))
                pe.wait_ge(a_moved, a_jobs(p) + 4)
                for b in range(2):
                    if p >= 1:
                        pe.wait_ge(ga_done, 2 * (p - 1) + b + 1)
                    for ch in range(CH):
                        t = b * CH + ch
                        col = slice(ch * P, (ch + 1) * P)
                        if ch > 0:
                            nc.tensor.matmul(c.ps[:, 6 + b, col], S[:, ch - 1, b, :], qD[:, p % 2, t * P:(t + 1) * P],
                                             start=True, stop=False, skip_group_check=True)
                        for hh in range(2):
                            h = p % GP * 2 + hh
                            last = nc.tensor.matmul(c.ps[hh * D:(hh + 1) * D, 6 + b, col], v[:, t, h * D:(h + 1) * D],
                                                    A[:, b, hh, ch, :], start=ch == 0, stop=True, skip_group_check=True)
                    last.then_inc(o_done, 1)

            def sum_outputs(g):
                pe.wait_ge(ga_done, 2 * GP * (g + 1))
                for t in range(TT):
                    j = a_jobs(GP * (g + 1)) - TT + t
                    pe.wait_ge(a_moved, j - 1)
                    for k in range(GP):
                        last = nc.tensor.matmul(c.ps[:, 2 + j % 2, :], ga[:, g % 2 * GP + k, t * P:(t + 1) * P], wo[:, g % 2, k, :],
                                                start=k == 0, stop=k == GP - 1)
                    last.then_inc(a_done, 1)

            queries_keys(0)
            gates(0)
            values(0)
            for p in range(PAIRS):
                products(p)
                turn_keys(p)
                if p + 1 < PAIRS:
                    queries_keys(p + 1)
                updates(p)
                if p + 1 < PAIRS:
                    gates(p + 1)
                outputs(p)
                if p + 1 < PAIRS and (p + 1) % GP == 0:
                    values((p + 1) // GP)
                if p % GP == GP - 1:
                    sum_outputs(p // GP)

        @block.scalar
        def _(act):
            def pair(p):
                j = first_job(p)
                for i in range(6):
                    act.wait_ge(proj_done, j + i + 1)
                    tok = slice(i % 2 * BANK, (i % 2 + 1) * BANK)
                    src = c.ps[:, (j + i) % 2, :]
                    if i == 0 and p >= 2:
                        act.wait_ge(a_done, a_jobs(p - 2) + 4)
                        act.wait_ge(qd_done, 2 * (p - 1))
                    if i == 2 and p >= 2:
                        act.wait_ge(t_done, 2 * (p - 1))
                    if i == 4 and p >= 2 * GP and p % GP == 0:
                        act.wait_ge(a_done, a_jobs(p - GP))
                    if i < 4:
                        dst = (qF, kF)[i // 2][:, p % 2, tok]
                        nc.scalar.activation(dst, src, ACT.Silu).then_inc(proj_moved, 1)
                    else:
                        nc.scalar.activation(ga[:, p % (2 * GP), tok], src, ACT.Sigmoid).then_inc(proj_moved, 1)

            def values(g):
                j = first_job(GP * g) + 6
                if g >= 1:
                    act.wait_ge(o_done, 2 * GP * g)
                for t in range(TT):
                    act.wait_ge(proj_done, j + t + 1)
                    nc.scalar.activation(v[:, t, :], c.ps[:, (j + t) % 2, :], ACT.Silu).then_inc(proj_moved, 1)

            def squares(p):
                for b in range(2):
                    act.wait_ge(o_done, 2 * p + b + 1)
                    if p >= 1:
                        act.wait_ge(sqsum_done, 2 * (p - 1) + b + 1)
                    nc.scalar.activation(sq[:, b, :], c.ps[:, 6 + b, :], ACT.Square).then_inc(sq_done, 1)

            pair(0)
            values(0)
            for p in range(PAIRS):
                if p + 1 < PAIRS:
                    pair(p + 1)
                squares(p)
                if p + 1 < PAIRS and (p + 1) % GP == 0:
                    values((p + 1) // GP)

        @block.gpsimd
        def _(pool):
            nc.gpsimd.memset(sqsum[:], 0.0).then_inc(zeroed, 1)
            pool.wait_ge(zeroed, 1)
            for p in range(PAIRS):
                g = p // GP
                if p % GP == 0:
                    pool.wait_ge(in_g[g % 2], 64 * (g // 2 + 1))
                if p >= 2:
                    pool.wait_ge(o_done, 2 * (p - 1))
                for n in range(2):
                    pool.wait_ge(proj_moved, first_job(p) + n + 1)
                    tok = slice(n * BANK, (n + 1) * BANK)
                    nc.gpsimd.tensor_tensor(qD[:, p % 2, tok].rearrange("p (c i) -> p c i", i=P),
                                            qF[:, p % 2, tok].rearrange("p (c i) -> p c i", i=P),
                                            qdec[:, g % 2, p % GP, :].unsqueeze(1).to_broadcast([P, CH, P]),
                                            ALU.mult).then_inc(qd_done, 1)
                for b in range(2):
                    pool.wait_ge(sq_done, 2 * p + b + 1)
                    if p >= 1:
                        pool.wait_ge(sqsum_done, 2 * (p - 1) + b + 1)
                    tok = slice(b * BANK, (b + 1) * BANK)
                    nc.gpsimd.tensor_tensor(sqsum[:, tok], sqsum[:, tok], sq[:, b, :], ALU.add).then_inc(sqsum_done, 1)

        @block.vector
        def _(dve):
            nc.vector.memset(S[:], 0.0).then_inc(step, 1)
            nc.vector.memset(ones[:], 1.0)
            dve.wait_ge(step, 1)
            dve.wait_ge(in_c, 48)
            steps = [1]

            def mask_products(p):
                g = p // GP
                if p % GP == 0:
                    dve.wait_ge(in_g[g % 2], 64 * (g // 2 + 1))
                for i in range(4):
                    b, hh = i // 2, i % 2
                    j, h = a_jobs(p) + i, p % GP * 2 + hh
                    dve.wait_ge(a_done, j + 1)
                    if p >= 1:
                        dve.wait_ge(o_done, 2 * (p - 1) + b + 1)
                    nc.vector.tensor_tensor(A[:, b, hh, :, :], c.ps[:, 2 + j % 2, :].rearrange("p (c i) -> p c i", i=P),
                                            mask[:, g % 2, h, :].unsqueeze(1).to_broadcast([P, CH, P]),
                                            ALU.mult).then_inc(a_moved, 1)

            def decay_keys(p):
                if p >= 2:
                    dve.wait_ge(u_done, p - 1)
                for b in range(2):
                    dve.wait_ge(t_done, 2 * p + b + 1)
                    nc.vector.tensor_tensor(kT[:, p % 2, b * CH:(b + 1) * CH, :].rearrange("p c (h d) -> p c h d", h=2),
                                            c.ps[:, 4 + b, :].rearrange("p (c h d) -> p c h d", c=CH, h=2),
                                            kdec[:, 2 * p:2 * p + 2].unsqueeze(1).unsqueeze(3).to_broadcast([P, CH, 2, D]),
                                            ALU.mult).then_inc(t_moved, 1)

            def states(p):
                dve.wait_ge(u_done, p + 1)
                if p >= 1:
                    dve.wait_ge(o_done, 2 * p)
                for ch in range(CH - 1):
                    for hh in range(2):
                        rows, cols = slice(hh * D, (hh + 1) * D), slice(hh * D, (hh + 1) * D)
                        new = c.ps[rows, 4:6, ch * P + hh * D:ch * P + (hh + 1) * D]
                        if ch == 0:
                            last = nc.vector.tensor_copy(S[rows, 0, :, cols], new)
                        else:
                            last = nc.vector.scalar_tensor_tensor(S[rows, ch, :, cols], S[rows, ch - 1, :, cols],
                                                                  bdec[rows, p:p + 1], new, ALU.mult, ALU.add)
                        if hh == 0:
                            last.then_inc(step, 1)
                            steps[0] += 1
                    last.then_inc(s_ready, 1)
                    dve.wait_ge(step, steps[0])
                    dve.wait_ge(s_ready, 3 * p + ch + 1)

            def gate(p):
                for b in range(2):
                    tok = slice(b * BANK, (b + 1) * BANK)
                    dve.wait_ge(sq_done, 2 * p + b + 1)
                    nc.vector.scalar_tensor_tensor(ga[:, p % (2 * GP), tok], c.ps[:, 6 + b, :], nw[:, p:p + 1],
                                                   ga[:, p % (2 * GP), tok], ALU.mult, ALU.mult).then_inc(ga_done, 1)

            def add_outputs(g):
                for t in range(TT):
                    j = a_jobs(GP * (g + 1)) - TT + t
                    dve.wait_ge(a_done, j + 1)
                    if g == 0:
                        nc.vector.tensor_copy(y[:, t, :], c.ps[:, 2 + j % 2, :]).then_inc(a_moved, 1)
                    else:
                        nc.vector.tensor_tensor(y[:, t, :], c.ps[:, 2 + j % 2, :], y[:, t, :], ALU.add).then_inc(a_moved, 1)

            for p in range(PAIRS):
                mask_products(p)
                decay_keys(p)
                states(p)
                gate(p)
                if p % GP == GP - 1:
                    add_outputs(p // GP)

    sum_done, ms_done, rs_done = c.sem("d_sum_done"), c.sem("d_ms_done"), c.sem("d_rs_done")
    with nc.Block() as block:
        @block.tensor
        def _(pe):
            for t in range(TT):
                last = nc.tensor.matmul(c.ps[:, 0, t:t + 1], sqsum[:, t * P:(t + 1) * P], ones[:], start=True, stop=True)
            last.then_inc(sum_done, 1)

        @block.vector
        def _(dve):
            dve.wait_ge(sum_done, 1)
            nc.vector.tensor_scalar(c.var_eps[:], c.ps[:, 0, 0:TT], 1.0 / F, 1e-5, ALU.mult, ALU.add).then_inc(ms_done, 1)
            dve.wait_ge(rs_done, 1)
            for t in range(TT):
                nc.vector.scalar_tensor_tensor(c.x[:, t, :], y[:, t, :], ms[:, t:t + 1], c.x[:, t, :], ALU.mult, ALU.add)

        @block.gpsimd
        def _(pool):
            pool.wait_ge(ms_done, 1)
            nc.gpsimd.tensor_tensor(ms[:], c.var_eps[:], c.neg_half[:], ALU.pow).then_inc(rs_done, 1)



def gated_cross_attention(c):
    nc = c.nc
    H, DH, KEYS = 16, 32, 1024
    ST = CTX // P
    W = P + 1
    ctxT = c.at("e_ctxT", [P, KD, CTX], F32, 52)
    qF = c.at("e_qF", [P, KD, TOK], F32, 52)
    gF = c.at("e_gF", [P, KD, TOK], F32, 68)
    kf = c.at("e_kf", [P, ST, DM], F32, 84)
    v = c.at("e_v", [P, ST, KD, W], F32, 116)
    wkT = c.at("e_wkT", [P, KD, DM], F32, 149)
    wvT = c.at("e_wvT", [P, KD, DM], F32, 157)
    wqT = c.at("e_wqT", [P, KD, DM], F32, 165)
    wgT = c.at("e_wgT", [P, KD, DM], F32, 173)
    woT = c.at("e_woT", [P, KD, DM], F32, 181)
    ex = c.at("e_ex", [P, 2, BANK], F32, 189)
    kv = c.at("e_kv", [P, 2, KD, P], F32, 193)
    gz = c.at("e_gz", [P, 2, BANK], F32, 197)
    z = c.at("e_z", [H, TOK], F32, 201)
    ksum = c.at("e_ksum", [P, 2, KD, H], F32, 205)
    blocks = c.at("e_blocks", [P, P], F32, 205.5)
    heads = c.at("e_heads", [P, KD, H], F32, 206)
    headsT = c.at("e_headsT", [H, KD, P], F32, 46)
    bg = c.at("e_bg", [P, KD], F32, 50.5)

    in_k, in_v, in_w, in_b, in_h = (c.sem(f"e_{n}") for n in ("in_k", "in_v", "in_w", "in_b", "in_h"))
    in_ctx = [c.sem(f"e_in_ctx{n}") for n in range(4)]
    with nc.Block() as block:
        @block.sync
        def _(sp):
            sp.dma_start(wkT[:], tiled(c.dram["e_wkT"])).then_inc(in_k, 16)
            for n in range(4):
                sp.dma_start(ctxT[:, :, n * BANK:(n + 1) * BANK],
                             tiled(c.dram["ctxT"])[:, :, n * BANK:(n + 1) * BANK]).then_inc(in_ctx[n], 16)
                if n == 0:
                    sp.dma_start(wvT[:], tiled(c.dram["e_wvT"])).then_inc(in_v, 16)
            for w, name in ((wqT, "e_wqT"), (wgT, "e_wgT"), (woT, "e_woT")):
                sp.dma_start(w[:], tiled(c.dram[name])).then_inc(in_w, 16)
            sp.dma_start(bg[:], c.dram["e_bg"]).then_inc(in_b, 16)
            sp.dma_start(blocks[:], c.dram["e_blocks"]).then_inc(in_b, 16)
            sp.dma_start(heads[:], c.dram["e_heads"]).then_inc(in_b, 16)

    k_done, k_exp, k_min, k_ready = (c.sem(f"e_{n}") for n in ("k_done", "k_exp", "k_min", "k_ready"))
    v_done, v_ready, ones_set = c.sem("e_v_done"), c.sem("e_v_ready"), c.sem("e_ones_set")
    normed, aggr_done, rstd_done = c.sem("e_normed"), c.sem("e_aggr_done"), c.sem("e_rstd_done")
    with nc.Block() as block:
        @block.tensor
        def _(pe):
            pe.wait_ge(in_k, 16)
            pe.wait_ge(in_v, 16)
            for j in range(ST):
                pe.wait_ge(in_ctx[j // 4], 16)
                for bank, wT, freed, done in ((j % 4, wkT, k_ready, k_done), (4 + j % 4, wvT, v_ready, v_done)):
                    if j >= 4:
                        pe.wait_ge(freed, j - 3)
                    for k in range(KD):
                        last = nc.tensor.matmul(c.ps[:, bank, :], ctxT[:, k, j * P:(j + 1) * P], wT[:, k, :],
                                                start=k == 0, stop=k == KD - 1)
                    last.then_inc(done, 1)

        @block.scalar
        def _(act):
            for j in range(ST):
                act.wait_ge(k_done, j + 1)
                if j >= 2:
                    act.wait_ge(k_ready, j - 1)
                nc.scalar.activation(ex[:, j % 2, :], c.ps[:, j % 4, :], ACT.Relu, scale=-1.0).then_inc(k_min, 1)
                act.wait_ge(k_min, j + 1)
                nc.scalar.activation(ex[:, j % 2, :], ex[:, j % 2, :], ACT.Exp, scale=-1.0).then_inc(k_exp, 1)
                act.wait_ge(v_done, j + 1)
                nc.scalar.activation(v[:, j, :, 0:P], c.ps[:, 4 + j % 4, :].rearrange("p (k d) -> p k d", k=KD),
                                     ACT.Copy).then_inc(v_ready, 1)

        @block.gpsimd
        def _(pool):
            nc.gpsimd.memset(v[:, :, :, P:W], 1.0)
            rstd_pool(c, aggr_done, rstd_done)

        @block.vector
        def _(dve):
            layernorm_dve(c, "e", aggr_done, rstd_done, normed)
            for j in range(ST):
                dve.wait_ge(k_exp, j + 1)
                nc.vector.scalar_tensor_tensor(kf[:, j, :], c.ps[:, j % 4, :], 0.0, ex[:, j % 2, :],
                                               ALU.max, ALU.add).then_inc(k_ready, 1)

    turn_normed(c, "e")

    kv_done, kv_ready = c.sem("e_kv_done"), c.sem("e_kv_ready")
    q_done, q_exp, q_min, q_ready = (c.sem(f"e_{n}") for n in ("q_done", "q_exp", "q_min", "q_ready"))
    g_done, g_ready = c.sem("e_g_done"), c.sem("e_g_ready")
    JOBS = [(n, m) for n in range(2) for m in range(KD)]
    with nc.Block() as block:
        @block.sync
        def _(sp):
            sp.dma_start(headsT[:], c.dram["e_headsT"]).then_inc(in_h, 16)
            sp.wait_ge(in_h, 16)

        @block.tensor
        def _(pe):
            for b in range(2):
                for m in range(KD):
                    for s in range(ST // 2):
                        t = b * ST // 2 + s
                        last = nc.tensor.matmul(c.ps[:, 2 * b + m // 2, m % 2 * W:(m % 2 + 1) * W],
                                                kf[:, t, m * P:(m + 1) * P], v[:, t, m, :],
                                                start=s == 0, stop=s == ST // 2 - 1)
                last.then_inc(kv_done, 1)
            pe.wait_ge(in_w, 48)
            for j, (n, m) in enumerate(JOBS):
                if j >= 2:
                    pe.wait_ge(q_ready, j - 1)
                for k in range(KD):
                    last = nc.tensor.matmul(c.ps[:, 4 + j % 2, :], wqT[:, k, m * P:(m + 1) * P],
                                            c.xF[:, k, n * BANK:(n + 1) * BANK], start=k == 0, stop=k == KD - 1)
                last.then_inc(q_done, 1)
            for j, (n, m) in enumerate(JOBS):
                if j >= 2:
                    pe.wait_ge(g_ready, j - 1)
                for k in range(KD):
                    last = nc.tensor.matmul(c.ps[:, 6 + j % 2, :], wgT[:, k, m * P:(m + 1) * P],
                                            c.xF[:, k, n * BANK:(n + 1) * BANK], start=k == 0, stop=k == KD - 1)
                last.then_inc(g_done, 1)

        @block.scalar
        def _(act):
            for j, (n, m) in enumerate(JOBS):
                act.wait_ge(q_done, j + 1)
                if j >= 2:
                    act.wait_ge(q_ready, j - 1)
                nc.scalar.activation(ex[:, j % 2, :], c.ps[:, 4 + j % 2, :], ACT.Relu, scale=-1.0).then_inc(q_min, 1)
                act.wait_ge(q_min, j + 1)
                nc.scalar.activation(ex[:, j % 2, :], ex[:, j % 2, :], ACT.Exp, scale=-1.0).then_inc(q_exp, 1)
            act.wait_ge(in_b, 48)
            for j, (n, m) in enumerate(JOBS):
                act.wait_ge(g_done, j + 1)
                nc.scalar.activation(gF[:, m, n * BANK:(n + 1) * BANK], c.ps[:, 6 + j % 2, :], ACT.Sigmoid,
                                     bias=bg[:, m:m + 1]).then_inc(g_ready, 1)

        @block.vector
        def _(dve):
            dve.wait_ge(in_b, 48)
            for b in range(2):
                dve.wait_ge(kv_done, b + 1)
                for m in range(KD):
                    col = m % 2 * W
                    nc.vector.tensor_tensor(kv[:, b, m, :], c.ps[:, 2 * b + m // 2, col:col + P], blocks[:], ALU.mult)
                    nc.vector.tensor_scalar(ksum[:, b, m, :], heads[:, m, :], c.ps[:, 2 * b + m // 2, col + P:col + W],
                                            None, ALU.mult)
            for j, (n, m) in enumerate(JOBS):
                dve.wait_ge(q_exp, j + 1)
                nc.vector.scalar_tensor_tensor(qF[:, m, n * BANK:(n + 1) * BANK], c.ps[:, 4 + j % 2, :], 0.0, ex[:, j % 2, :],
                                               ALU.max, ALU.add).then_inc(q_ready, 1)

    den_done, z_step, zb_done, gz_done, num_done, ag_done = (
        c.sem(f"e_{n}") for n in ("den_done", "z_step", "zb_done", "gz_done", "num_done", "ag_done"))
    out_done, added = c.sem("e_out_done"), c.sem("e_added")
    with nc.Block() as block:
        @block.tensor
        def _(pe):
            for b in range(2):
                for m in range(KD):
                    last = nc.tensor.matmul(c.ps[0:H, b, :], ksum[:, b, m, :], qF[:, m, b * BANK:(b + 1) * BANK],
                                            start=m == 0, stop=m == KD - 1)
                last.then_inc(den_done, 1)
            for j, (b, m) in enumerate(JOBS):
                if j >= 2:
                    pe.wait_ge(ag_done, j - 1)
                nc.tensor.matmul(c.ps[:, 4 + j % 2, :], kv[:, b, m, :], qF[:, m, b * BANK:(b + 1) * BANK],
                                 start=True, stop=True).then_inc(num_done, 1)
                pe.wait_ge(z_step, 2 * (b + 1))
                nc.tensor.matmul(c.ps[:, 2 + j % 2, :], headsT[:, m, :], z[:, b * BANK:(b + 1) * BANK],
                                 start=True, stop=True).then_inc(zb_done, 1)
            for t in range(TT):
                pe.wait_ge(ag_done, KD * (1 + t // 4))
                if t >= 2:
                    pe.wait_ge(added, t - 1)
                for k in range(KD):
                    last = nc.tensor.matmul(c.ps[:, 6 + t % 2, :], gF[:, k, t * P:(t + 1) * P], woT[:, k, :],
                                            start=k == 0, stop=k == KD - 1)
                last.then_inc(out_done, 1)

        @block.vector
        def _(dve):
            for b in range(2):
                dve.wait_ge(den_done, b + 1)
                nc.vector.tensor_scalar(z[:, b * BANK:(b + 1) * BANK], c.ps[0:H, b, :], 1e-6, None, ALU.add).then_inc(z_step, 1)
                dve.wait_ge(z_step, 2 * b + 1)
                nc.vector.reciprocal(z[:, b * BANK:(b + 1) * BANK], z[:, b * BANK:(b + 1) * BANK]).then_inc(z_step, 1)
            for j, (b, m) in enumerate(JOBS):
                tok = slice(b * BANK, (b + 1) * BANK)
                dve.wait_ge(zb_done, j + 1)
                nc.vector.tensor_tensor(gz[:, j % 2, :], c.ps[:, 2 + j % 2, :], gF[:, m, tok], ALU.mult).then_inc(gz_done, 1)
                dve.wait_ge(gz_done, j + 1)
                nc.vector.tensor_tensor(gF[:, m, tok], c.ps[:, 4 + j % 2, :], gz[:, j % 2, :], ALU.mult).then_inc(ag_done, 1)
            for t in range(TT):
                dve.wait_ge(out_done, t + 1)
                nc.vector.tensor_tensor(c.x[:, t, :], c.ps[:, 6 + t % 2, :], c.x[:, t, :], ALU.add).then_inc(added, 1)



MX = 32
FP8_ROUND = 1.5 * 2.0 ** 20
FP8_SMALL = 2.0 ** -6


def mx_round(c, step, done, src, aux, scale, inv):
    nc, dve = c.nc, c.nc.vector
    blocks = src.rearrange("p (b m) -> p b m", m=MX)

    def chained(ins):
        done[0] += 1
        ins.then_inc(step, 1)
        dve.wait_ge(step, done[0])

    chained(nc.vector.tensor_reduce(scale, blocks, AX.X, ALU.max, apply_absolute_value=True))
    chained(nc.vector.tensor_scalar(scale, scale, 1.0 / 448.0, 1e-30, ALU.mult, ALU.max))
    chained(nc.vector.reciprocal(inv, scale))
    chained(nc.vector.tensor_tensor(blocks, blocks, inv.unsqueeze(2).to_broadcast(list(blocks.shape)), ALU.mult))
    chained(nc.vector.tensor_scalar(aux.bitcast(U32), src.bitcast(U32), 0x7F800000, None, ALU.bitwise_and))
    chained(nc.vector.tensor_scalar(aux, aux, FP8_SMALL, FP8_ROUND, ALU.max, ALU.mult))
    chained(nc.vector.tensor_tensor(src, src, aux, ALU.add))
    return nc.vector.tensor_tensor(src, src, aux, ALU.subtract)


def mx_feed_forward(c):
    nc = c.nc
    INTER = 2048
    NCH, UNIT = INTER // BANK, 2 * DM
    gT = c.at("f_gT", [P, 2, KD, BANK], F32, 52)
    uT = c.at("f_uT", [P, 2, KD, BANK], F32, 68)
    dT = c.at("f_dT", [P, 2, KD, DM], F32, 84)
    w = c.at("f_w", [P, 4, KD * DM], F32, 100)
    h = c.at("f_h", [P, 2, TT * BANK], F32, 132)
    hF = c.at("f_hF", [P, 2, KD, P], F32, 164)
    silu = c.at("f_silu", [P, 2, BANK], F32, 168)
    aux = c.at("f_aux", [P, UNIT], F32, 172)
    scale = c.at("f_scale", [P, 4, UNIT // MX], F32, 176)
    inv = c.at("f_inv", [P, UNIT // MX], F32, 176.5)
    xn = c.xn[:].rearrange("p t n -> p (t n)")
    WJOBS = [(name, wT, n) for n in range(NCH) for name, wT in (("f_g", gT), ("f_u", uT), ("f_d", dT))]

    PE_PLAN = [("w", j, r) for j in range(2) for r in range(4)] + [("x", 0), ("x", 1)]
    DVE_PLAN = [("w", j, half) for j in range(2) for half in range(2)] + [("x", 0)]
    for n in range(NCH):
        next_w = {0: (3 * n + 2, 0), 1: (3 * n + 2, 1)}
        if n + 1 < NCH:
            next_w.update({2: (3 * n + 3, 0), 3: (3 * n + 3, 1), 4: (3 * n + 4, 0), 5: (3 * n + 4, 1)})
        for t in range(TT):
            if n >= 1:
                PE_PLAN.append(("h", n - 1, t))
            if n == 0 and t >= 2 and t % 2 == 0:
                PE_PLAN += [("x", t), ("x", t + 1)]
            PE_PLAN.append(("up", n, t))
            if t - 1 in next_w:
                j, half = next_w[t - 1]
                PE_PLAN += [("w", j, 2 * half), ("w", j, 2 * half + 1)]
            DVE_PLAN.append(("mult", n, t))
            if n == 0 and t < 3:
                DVE_PLAN.append(("x", t + 1))
            if t in next_w:
                DVE_PLAN.append(("w",) + next_w[t])
            if t % 2 == 1:
                DVE_PLAN.append(("h", n, t // 2))
            if n >= 1:
                PE_PLAN.append(("down", n - 1, t))
                DVE_PLAN.append(("add", n - 1, t))
    for t in range(TT):
        PE_PLAN += ([("h", NCH - 1, 0)] if t == 0 else []) + ([("h", NCH - 1, t + 1)] if t + 1 < TT else [])
        PE_PLAN.append(("down", NCH - 1, t))
        DVE_PLAN.append(("add", NCH - 1, t))
    TURNS = [e for e in PE_PLAN if e[0] in "wxh"]
    UNITS = [e for e in DVE_PLAN if e[0] in "wxh"]

    in_w = [c.sem(f"f_in_w{i}") for i in range(4)]
    step, rounded, quantised = c.sem("f_step"), c.sem("f_rounded"), c.sem("f_quantised")
    turned, moved = c.sem("f_turned"), c.sem("f_moved")
    normed, aggr_done, rstd_done = c.sem("f_normed"), c.sem("f_aggr_done"), c.sem("f_rstd_done")
    g_done, u_done, silu_done, h_done, out_done, added = (c.sem(f"f_{n}") for n in (
        "g_done", "u_done", "silu_done", "h_done", "out_done", "added"))

    def unit_rows(e):
        if e[0] == "w":
            return w[:, e[1] % 4, e[2] * UNIT:(e[2] + 1) * UNIT]
        if e[0] == "x":
            return xn[:, e[1] * UNIT:(e[1] + 1) * UNIT]
        return h[:, e[1] % 2, e[2] * UNIT:(e[2] + 1) * UNIT]

    def turn_rows(e):
        if e[0] == "w":
            _, j, r = e
            return w[:, j % 4, r * DM:(r + 1) * DM], WJOBS[j][1][:, WJOBS[j][2] % 2, :, r * P:(r + 1) * P], ("w", j, r // 2)
        if e[0] == "x":
            t = e[1]
            return c.xn[:, t, :], c.xF[:, :, t * P:(t + 1) * P], ("x", t // 2)
        _, n, t = e
        return h[:, n % 2, t * BANK:(t + 1) * BANK], hF[:, (n * TT + t) % 2, :, :], ("h", n, t // 2)

    with nc.Block() as block:
        @block.sync
        def _(sp):
            for j, (name, _, n) in enumerate(WJOBS):
                if j >= 4:
                    sp.wait_ge(turned, TURNS.index(("w", j - 4, 3)) + 1)
                rows = tiled(c.dram[name])[:, :, n * BANK:(n + 1) * BANK] if name == "f_d" else tiled(c.dram[name][n * BANK:(n + 1) * BANK, :])
                sp.dma_start(w[:, j % 4, :].rearrange("p (m n) -> p m n", m=4), rows).then_inc(in_w[j % 4], 16)

        @block.gpsimd
        def _(pool):
            rstd_pool(c, aggr_done, rstd_done)
            for i, e in enumerate(UNITS):
                blocks = unit_rows(e).rearrange("p (b m) -> p b m", m=MX)
                pool.wait_ge(rounded, i + 1)
                nc.gpsimd.tensor_tensor(blocks, blocks, scale[:, i % 4, :].unsqueeze(2).to_broadcast(list(blocks.shape)),
                                        ALU.mult).then_inc(quantised, 1)

        @block.vector
        def _(dve):
            layernorm_dve(c, "f", aggr_done, rstd_done, normed)
            dve.wait_ge(normed, TT)
            done, i = [0], 0
            for e in DVE_PLAN:
                if e[0] in "wxh":
                    if e[0] == "w":
                        dve.wait_ge(in_w[e[1] % 4], 16 * (e[1] // 4 + 1))
                    elif e[0] == "h":
                        dve.wait_ge(h_done, TT * e[1] + 2 * e[2] + 2)
                    if i >= 1:
                        dve.wait_ge(rounded, i)
                    if i >= 4:
                        dve.wait_ge(quantised, i - 3)
                    mx_round(c, step, done, unit_rows(e), aux[:], scale[:, i % 4, :], inv[:]).then_inc(rounded, 1)
                    i += 1
                elif e[0] == "mult":
                    _, n, t = e
                    j = TT * n + t
                    dve.wait_ge(silu_done, j + 1)
                    dve.wait_ge(u_done, j + 1)
                    if n >= 2:
                        dve.wait_ge(turned, TURNS.index(("h", n - 2, t)) + 1)
                    nc.vector.tensor_tensor(h[:, n % 2, t * BANK:(t + 1) * BANK], c.ps[:, 4 + j % 2, :], silu[:, j % 2, :],
                                            ALU.mult).then_inc(h_done, 1)
                else:
                    _, n, t = e
                    j = TT * n + t
                    dve.wait_ge(out_done, j + 1)
                    if n >= 1:
                        dve.wait_ge(added, j - TT + 1)
                    nc.vector.tensor_tensor(c.x[:, t, :], c.ps[:, 6 + j % 2, :], c.x[:, t, :], ALU.add).then_inc(added, 1)

        @block.tensor
        def _(pe):
            for e in PE_PLAN:
                if e[0] in "wxh":
                    i = TURNS.index(e)
                    rows, _, unit = turn_rows(e)
                    pe.wait_ge(quantised, UNITS.index(unit) + 1)
                    if i >= 2:
                        pe.wait_ge(moved, i - 1)
                    for k in range(KD):
                        last = nc.tensor.transpose(c.ps[:, i % 2, k * P:(k + 1) * P], rows[:, k * P:(k + 1) * P], c.ident[:])
                    last.then_inc(turned, 1)
                elif e[0] == "up":
                    _, n, t = e
                    j = TT * n + t
                    pe.wait_ge(moved, TURNS.index(("w", 3 * n + 1, 3)) + 1)
                    pe.wait_ge(moved, TURNS.index(("x", t)) + 1)
                    for bank, wT, freed, done_ in ((2 + j % 2, gT, silu_done, g_done), (4 + j % 2, uT, h_done, u_done)):
                        if j >= 2:
                            pe.wait_ge(freed, j - 1)
                        for k in range(KD):
                            last = nc.tensor.matmul(c.ps[:, bank, :], c.xF[:, k, t * P:(t + 1) * P], wT[:, n % 2, k, :],
                                                    start=k == 0, stop=k == KD - 1)
                        last.then_inc(done_, 1)
                else:
                    _, n, t = e
                    j = TT * n + t
                    pe.wait_ge(moved, TURNS.index(("w", 3 * n + 2, 3)) + 1)
                    pe.wait_ge(moved, TURNS.index(("h", n, t)) + 1)
                    if j >= 2:
                        pe.wait_ge(added, j - 1)
                    for k in range(KD):
                        last = nc.tensor.matmul(c.ps[:, 6 + j % 2, :], hF[:, j % 2, k, :], dT[:, n % 2, k, :],
                                                start=k == 0, stop=k == KD - 1)
                    last.then_inc(out_done, 1)

        @block.scalar
        def _(act):
            for e in PE_PLAN:
                if e[0] in "wxh":
                    i = TURNS.index(e)
                    act.wait_ge(turned, i + 1)
                    if e[0] == "w" and e[2] == 0:
                        name, _, n = WJOBS[e[1]]
                        if name != "f_d" and n >= 2:
                            act.wait_ge(g_done, TT * (n - 1))
                            act.wait_ge(u_done, TT * (n - 1))
                        elif name == "f_d" and n >= 2:
                            act.wait_ge(out_done, TT * (n - 1))
                    elif e[0] == "h" and TT * e[1] + e[2] >= 2:
                        act.wait_ge(out_done, TT * e[1] + e[2] - 1)
                    nc.scalar.activation(turn_rows(e)[1], c.ps[:, i % 2, :].rearrange("p (k o) -> p k o", k=KD),
                                         ACT.Copy).then_inc(moved, 1)
                elif e[0] == "up":
                    j = TT * e[1] + e[2]
                    act.wait_ge(g_done, j + 1)
                    if j >= 2:
                        act.wait_ge(h_done, j - 1)
                    nc.scalar.activation(silu[:, j % 2, :], c.ps[:, 2 + j % 2, :], ACT.Silu).then_inc(silu_done, 1)


def store_result(c):
    nc, stored = c.nc, c.stored
    with nc.Block() as block:
        @block.sync
        def _(sp):
            sp.dma_start(tiled(c.out), c.x[:]).then_inc(stored, 16)
            sp.wait_ge(stored, 16)


STAGES = [mixer, cross_attention, experts, linear_attention, gated_cross_attention, mx_feed_forward]


def build(nc, dram, out, phases=range(6)):
    c = Core(nc, dram, out)
    for stage in (load_constants, *(STAGES[s] for s in phases), store_result):
        c.stage_sems = []
        stage(c)
        nc.clear_and_free_semaphores(c.stage_sems)
        nc.all_engine_barrier()


def _layout(i):
    c = np.ascontiguousarray
    a = {}
    a["x"] = c(i["x"].reshape(TOK, DM))
    a["c_ident"] = np.eye(P, dtype=np.float32)
    w = i["L0_attn_W_in"]
    a["winx"] = c(w[:1024])
    a["winzT"] = c(w[1024:].T)
    a["convT"] = c(i["L0_attn_conv_w"].T)
    a["woutT"] = c(i["L0_attn_W_out"].T)
    a["Dv"] = c(i["L0_attn_D"].reshape(8, P).T)
    a["ctxT"] = c(i["ctx_2048"].reshape(CTX, DM).T)
    wkv = i["L0_xattn_wkv"]
    a["b_wkT"], a["b_wvT"] = c(wkv[:512].T), c(wkv[512:].T)
    a["b_wq"], a["b_wp"] = c(i["L0_xattn_wq"]), c(i["L0_xattn_wp"])
    bkv = i["L0_xattn_bkv"]
    a["b_bq"], a["b_bk"] = c(i["L0_xattn_bq"].reshape(4, P).T), c(bkv[:512].reshape(4, P).T)
    a["b_bv"], a["b_bp"] = c(bkv[512:]), c(i["L0_xattn_bp"])
    a["c_s1T"], a["c_sgT"], a["c_s2T"] = (c(i[f"L0_ffn_{n}"].T) for n in ("sw1", "swg", "sw2"))
    a["c_wdT"], a["c_wupT"], a["c_wgT"] = (c(i[f"L0_ffn_{n}"].T) for n in ("Wdown", "Wup", "Wg"))
    a["c_r1T"], a["c_rgT"], a["c_r2T"] = (c(i[f"L0_ffn_{n}"].transpose(0, 2, 1)) for n in ("rw1", "rwg", "rw2"))
    a["c_bias"] = c(i["L0_ffn_biases"])
    qkv = i["L1_attn_qkv_w"].reshape(32, 3, 64, DM)

    def by_pair(w):
        return c(w.reshape(16, P, KD, P).transpose(0, 3, 2, 1))
    a["d_wq"], a["d_wk"], a["d_wg"] = by_pair(qkv[:, 0]), by_pair(qkv[:, 1]), by_pair(i["L1_attn_gate_w"])
    a["d_wvT"] = c(qkv[:, 2].reshape(2048, DM).T)
    a["d_woT"] = c(i["L1_attn_out_w"].T)
    a["d_nw"] = c(i["L1_attn_norm_w"].reshape(16, P).T)
    slope = (2.0 ** (-8.0 / 32)) ** np.arange(1, 33) * (1 + 1e-5)
    r = np.arange(1, P + 1)
    gap = r[None, :] - r[:, None]
    mask = np.where(gap[:, None, :] >= 0, np.exp(-slope[None, :, None] * np.maximum(gap, 0)[:, None, :]), 0.0)
    a["d_mask"] = c(mask.astype(np.float32))
    a["d_qdec"] = c(np.repeat(np.exp(-slope[:, None] * r), 64, 0).reshape(16, P, P).transpose(1, 0, 2).astype(np.float32))
    a["d_kdec"] = c(np.exp(-slope[None, :] * (P - r)[:, None]).astype(np.float32))
    a["d_bdec"] = c(np.repeat(np.exp(-slope * P), 64).reshape(16, P).T.astype(np.float32))
    wkv = i["L1_xattn_Wkv"]
    a["e_wkT"], a["e_wvT"] = c(wkv[:512].T), c(wkv[512:].T)
    a["e_wqT"], a["e_wgT"], a["e_woT"] = (c(i[f"L1_xattn_{n}"].T) for n in ("Wq", "Wg", "Wo"))
    a["e_bg"] = c(i["L1_xattn_bg"].reshape(4, P).T)
    head = np.arange(DM) // 32
    a["e_blocks"] = (head[:P, None] == head[None, :P]).astype(np.float32)
    belongs = (head[:, None] == np.arange(16)).astype(np.float32).reshape(KD, P, 16)
    a["e_heads"], a["e_headsT"] = c(belongs.transpose(1, 0, 2)), c(belongs.transpose(2, 0, 1))
    a["f_g"], a["f_u"], a["f_d"] = (c(i[f"L1_ffn_{n}_w"]) for n in ("gate", "up", "down"))
    return a


def kernel(**inputs):
    import concourse.bacc as _bacc
    from concourse.bass_utils import run_bass_kernel_spmd as _run

    nc = _bacc.Bacc("TRN2", target_bir_lowering=False, num_devices=1)
    arrays = {f"in_{k}": v for k, v in _layout({k: np.asarray(v) for k, v in inputs.items()}).items()}
    dram = {k[3:]: nc.dram_tensor(k, v.shape, mybir.dt.from_np(v.dtype), kind="ExternalInput").ap()
            for k, v in arrays.items()}
    out = nc.dram_tensor("out_0", (TOK, DM), F32, kind="ExternalOutput").ap()
    build(nc, dram, out)
    r = _run(nc, [arrays], core_ids=[0])
    return r.results[0]["out_0"].reshape(2, 512, 512)
```

```python
import numpy as np
from concourse import mybir

F32 = mybir.dt.float32
BF16 = mybir.dt.bfloat16
U32 = mybir.dt.uint32
F32R = mybir.dt.float32r
ALU = mybir.AluOpType
ACT = mybir.ActivationFunctionType
AX = mybir.AxisListType

P = 128
TOK, DM = 1024, 512
TT, KD = TOK // P, DM // P
BANK = 512
CTX = 2048


class Core:

    def __init__(self, nc, dram, out):
        self.nc, self.dram, self.out = nc, dram, out
        self.base = -(-nc.sbuf_base // 64) * 64
        self.x = self.at("x", [P, TT, DM], F32, 0)
        self.xF = self.at("xF", [P, KD, TOK], F32, 16)
        self.xn = self.at("xn", [P, TT, DM], F32, 32)
        self.ident = self.at("ident", [P, P], F32, 48)
        self.identb = self.at("identb", [P, P], BF16, 48.5)
        self.stats = self.at("stats", [P, TT, 6], F32, 48.75)
        self.mv = self.at("mv", [P, TT, 2], F32, 49)
        self.rstd = self.at("rstd", [P, TT], F32, 49.125)
        self.var_eps = self.at("var_eps", [P, TT], F32, 49.25)
        self.neg_half = self.at("neg_half", [P, TT], F32, 49.375)
        self.stored = nc.alloc_semaphore("stored")
        self.ps = nc.alloc_psum_tensor("ps", [P, 8, BANK], F32)

    def at(self, name, shape, dt, kb):
        off = self.base + int(kb * 1024)
        return self.nc.alloc_sbuf_tensor_at(name, shape, dt, offset=off)

    def sem(self, name):
        s = self.nc.alloc_semaphore(name)
        self.stage_sems.append(s)
        return s


def tiled(ap):
    return ap.rearrange("(k p) n -> p k n", p=P)


def rstd_pool(c, aggr_done, rstd_done):
    c.nc.gpsimd.wait_ge(aggr_done, TT + 1)
    c.nc.gpsimd.tensor_tensor(c.rstd[:], c.var_eps[:], c.neg_half[:], ALU.pow).then_inc(rstd_done, 1)


def layernorm_dve(c, tag, aggr_done, rstd_done, normed):
    nc, dve = c.nc, c.nc.vector
    stats_done = c.sem(f"{tag}_stats_done")
    for t in range(TT):
        nc.vector.bn_stats(c.stats[:, t, :], c.x[:, t, :]).then_inc(stats_done, 1)
    for t in range(TT):
        dve.wait_ge(stats_done, t + 1)
        nc.vector.bn_aggr(c.mv[:, t, :], c.stats[:, t, :]).then_inc(aggr_done, 1)
    dve.wait_ge(aggr_done, TT)
    nc.vector.tensor_scalar(c.var_eps[:], c.mv[:, :, 1], 1e-5, None, ALU.add).then_inc(aggr_done, 1)
    dve.wait_ge(rstd_done, 1)
    for t in range(TT):
        nc.vector.tensor_scalar(c.xn[:, t, :], c.x[:, t, :], c.mv[:, t, 0:1], c.rstd[:, t:t + 1],
                                ALU.subtract, ALU.mult).then_inc(normed, 1)


def norm_and_transpose(c, tag):
    nc = c.nc
    normed, turned = c.sem(f"{tag}_normed"), c.sem(f"{tag}_turned")
    moved_act, moved_dve = c.sem(f"{tag}_moved_act"), c.sem(f"{tag}_moved_dve")
    aggr_done, rstd_done = c.sem(f"{tag}_aggr_done"), c.sem(f"{tag}_rstd_done")
    with nc.Block() as block:
        @block.gpsimd
        def _(pool):
            rstd_pool(c, aggr_done, rstd_done)

        @block.vector
        def _(dve):
            layernorm_dve(c, tag, aggr_done, rstd_done, normed)
            for t in range(1, TT, 2):
                dve.wait_ge(turned, t + 1)
                nc.vector.tensor_copy(c.xF[:, :, t * P:(t + 1) * P],
                                      c.ps[:, t, :].rearrange("p (k t) -> p k t", k=KD)).then_inc(moved_dve, 1)
            dve.wait_ge(moved_dve, TT // 2)

        @block.scalar
        def _(act):
            for t in range(0, TT, 2):
                act.wait_ge(turned, t + 1)
                nc.scalar.activation(c.xF[:, :, t * P:(t + 1) * P],
                                     c.ps[:, t, :].rearrange("p (k t) -> p k t", k=KD), ACT.Copy).then_inc(moved_act, 1)
            act.wait_ge(moved_act, TT // 2)

        @block.tensor
        def _(pe):
            for t in range(TT):
                pe.wait_ge(normed, t + 1)
                for k in range(KD):
                    last = nc.tensor.transpose(c.ps[:, t, k * P:(k + 1) * P], c.xn[:, t, k * P:(k + 1) * P], c.ident[:])
                last.then_inc(turned, 1)


def norm_and_split(c, tag, high, low):
    aggr_done, rstd_done, normed = c.sem(f"{tag}_aggr_done"), c.sem(f"{tag}_rstd_done"), c.sem(f"{tag}_normed")
    turn_and_split(c, tag, high, low, (aggr_done, rstd_done, normed))


def turn_and_split(c, tag, high, low, norm=None):
    nc = c.nc
    turned, high_done, low_done = c.sem(f"{tag}_turned"), c.sem(f"{tag}_high_done"), c.sem(f"{tag}_low_done")

    def tile_of(part, t):
        return part[:, :, t * P:(t + 1) * P]

    with nc.Block() as block:
        if norm:
            @block.gpsimd
            def _(pool):
                rstd_pool(c, norm[0], norm[1])

        @block.vector
        def _(dve):
            if norm:
                layernorm_dve(c, tag, *norm)
            for t in range(TT):
                dve.wait_ge(high_done, t + 1)
                nc.vector.tensor_tensor(tile_of(low, t), c.ps[:, t, :].rearrange("p (k t) -> p k t", k=KD),
                                        tile_of(high, t).bitcast(F32), ALU.subtract).then_inc(low_done, 1)
            dve.wait_ge(low_done, TT)

        @block.scalar
        def _(act):
            for t in range(TT):
                act.wait_ge(turned, t + 1)
                nc.scalar.activation(tile_of(high, t), c.ps[:, t, :].rearrange("p (k t) -> p k t", k=KD),
                                     ACT.Copy).then_inc(high_done, 1)

        @block.tensor
        def _(pe):
            for t in range(TT):
                if norm:
                    pe.wait_ge(norm[2], t + 1)
                for k in range(KD):
                    last = nc.tensor.transpose(c.ps[:, t, k * P:(k + 1) * P], c.xn[:, t, k * P:(k + 1) * P], c.ident[:])
                last.then_inc(turned, 1)


def product_of_parts(nc, out, lhsT, rhs, start, stop):
    nc.tensor.matmul(out, lhsT[0], rhs[0], start=start, stop=False)
    nc.tensor.matmul(out, lhsT[0], rhs[1], start=False, stop=False)
    return nc.tensor.matmul(out, lhsT[1], rhs[0], start=False, stop=stop)


def turn_normed(c, tag):
    nc = c.nc
    turned = c.sem(f"{tag}_turned")
    moved_act, moved_dve = c.sem(f"{tag}_moved_act"), c.sem(f"{tag}_moved_dve")
    with nc.Block() as block:
        @block.vector
        def _(dve):
            for t in range(1, TT, 2):
                dve.wait_ge(turned, t + 1)
                nc.vector.tensor_copy(c.xF[:, :, t * P:(t + 1) * P],
                                      c.ps[:, t, :].rearrange("p (k t) -> p k t", k=KD)).then_inc(moved_dve, 1)

        @block.scalar
        def _(act):
            for t in range(0, TT, 2):
                act.wait_ge(turned, t + 1)
                nc.scalar.activation(c.xF[:, :, t * P:(t + 1) * P],
                                     c.ps[:, t, :].rearrange("p (k t) -> p k t", k=KD), ACT.Copy).then_inc(moved_act, 1)

        @block.tensor
        def _(pe):
            for t in range(TT):
                for k in range(KD):
                    last = nc.tensor.transpose(c.ps[:, t, k * P:(k + 1) * P], c.xn[:, t, k * P:(k + 1) * P], c.ident[:])
                last.then_inc(turned, 1)



def mixer(c):
    nc = c.nc
    INTER = 1024
    KI = INTER // P
    HALVES, KHALF = 2, KI // 2

    def parts(name, shape, high_at, low_at):
        return [c.at(f"a_{name}_high", shape, F32R, high_at), c.at(f"a_{name}_low", shape, F32R, low_at)]

    winx = c.at("a_winx", [P, KI, DM], F32, 52)
    convT = c.at("a_convT", [P, 2, KI, BANK], F32, 68)
    winx_parts = parts("winx", [P, KI, DM], 100, 116)
    conv_parts = parts("conv", [P, 2, KI, BANK], 132, 164)
    wp_parts = parts("wp", [P, KD, INTER], 52, 68)
    winzT = c.at("a_winzT", [P, KD, INTER], F32, 84)
    winz_parts = parts("winz", [P, KD, INTER], 100, 116)
    woutT = c.at("a_woutT", [P, KI, DM], F32, 132)
    wout_parts = parts("wout", [P, KI, DM], 148, 164)
    g_parts = parts("g", [P, KI, BANK], 84, 132)
    sz = c.at("a_sz", [P, 2, BANK], F32, 180)
    g = c.at("a_g", [P, 2, BANK], F32, 184)
    x_parts = parts("x", [P, KD, TOK], 16, 188)
    Dv = c.at("a_D", [P, KI], F32, 50)
    in_z, in_out, in_d, in_rows = (c.sem(f"a_{n}") for n in ("in_z", "in_out", "in_d", "in_rows"))
    in_x = [c.sem(f"a_in_x{q}") for q in range(2)]
    in_conv = [[c.sem(f"a_in_conv{h}{q}") for q in range(2)] for h in range(HALVES)]
    high, low, half_set = c.sem("a_high"), c.sem("a_low"), c.sem("a_half_set")
    fused, fused_high, fused_low = c.sem("a_fused"), c.sem("a_fused_high"), c.sem("a_fused_low")
    normed, aggr_done, rstd_done = c.sem("a_normed"), c.sem("a_aggr_done"), c.sem("a_rstd_done")

    def rows(q):
        return slice(q * KHALF, (q + 1) * KHALF)

    SPLITS = [(in_x[0], winx[:, rows(0)], [w[:, rows(0)] for w in winx_parts]),
              (in_conv[0][0], convT[:, 0, rows(0)], [w[:, 0, rows(0)] for w in conv_parts]),
              (in_x[1], winx[:, rows(1)], [w[:, rows(1)] for w in winx_parts]),
              (in_conv[0][1], convT[:, 0, rows(1)], [w[:, 0, rows(1)] for w in conv_parts]),
              (in_conv[1][0], convT[:, 1, rows(0)], [w[:, 1, rows(0)] for w in conv_parts]),
              (in_conv[1][1], convT[:, 1, rows(1)], [w[:, 1, rows(1)] for w in conv_parts])]

    with nc.Block() as block:
        @block.sync
        def _(sp):
            conv = tiled(c.dram["convT"])
            for q in range(2):
                sp.dma_start(winx[:, rows(q)], tiled(c.dram["winx"])[:, rows(q)]).then_inc(in_x[q], 16)
                sp.dma_start(convT[:, 0, rows(q)], conv[:, rows(q), 0:BANK]).then_inc(in_conv[0][q], 16)
            for q in range(2):
                sp.dma_start(convT[:, 1, rows(q)], conv[:, rows(q), BANK:]).then_inc(in_conv[1][q], 16)
            sp.dma_start(Dv[:], c.dram["Dv"]).then_inc(in_d, 16)
            sp.dma_start(c.x[:], tiled(c.dram["x"])).then_inc(in_rows, 16)
            sp.dma_start(c.ident[:], c.dram["c_ident"]).then_inc(in_rows, 16)
            sp.wait_ge(low, len(SPLITS))
            sp.dma_start(winzT[:], tiled(c.dram["winzT"])).then_inc(in_z, 16)
            sp.wait_ge(in_d, 16)

        @block.tensor
        def _(pe):
            for n in range(HALVES):
                for m in range(KD):
                    for k in range(KI):
                        if k % KHALF == 0:
                            pe.wait_ge(low, 2 + 2 * (k // KHALF) if n == 0 else 5 + k // KHALF)
                        last = product_of_parts(nc, c.ps[:, n * KD + m, :], [w[:, k, m * P:(m + 1) * P] for w in winx_parts],
                                                [w[:, n, k, :] for w in conv_parts], k == 0, k == KI - 1)
                    last.then_inc(fused, 1)

        @block.scalar
        def _(act):
            for loaded, src, dst in SPLITS:
                act.wait_ge(loaded, 16)
                nc.scalar.activation(dst[0], src, ACT.Copy).then_inc(high, 1)
            for j in range(2 * KD):
                n, m = j // KD, j % KD
                act.wait_ge(fused, j + 1)
                nc.scalar.activation(wp_parts[0][:, m, n * BANK:(n + 1) * BANK], c.ps[:, j, :], ACT.Copy).then_inc(fused_high, 1)

        @block.gpsimd
        def _(pool):
            nc.gpsimd.memset(c.neg_half[:], -0.5).then_inc(half_set, 1)
            pool.wait_ge(half_set, 1)
            rstd_pool(c, aggr_done, rstd_done)

        @block.vector
        def _(dve):
            for i, (_, src, dst) in enumerate(SPLITS):
                dve.wait_ge(high, i + 1)
                nc.vector.tensor_tensor(dst[1], src, dst[0].bitcast(F32), ALU.subtract).then_inc(low, 1)
            dve.wait_ge(in_rows, 32)
            nc.vector.tensor_copy(c.identb[:], c.ident[:])
            layernorm_dve(c, "a", aggr_done, rstd_done, normed)
            for j in range(2 * KD):
                n, m = j // KD, j % KD
                dve.wait_ge(fused_high, j + 1)
                nc.vector.tensor_tensor(wp_parts[1][:, m, n * BANK:(n + 1) * BANK], c.ps[:, j, :],
                                        wp_parts[0][:, m, n * BANK:(n + 1) * BANK].bitcast(F32), ALU.subtract).then_inc(fused_low, 1)

    turn_and_split(c, "a", *x_parts)

    z_done, y_done, silu_done, g_done = (c.sem(f"a_{n}") for n in ("z_done", "y_done", "silu_done", "g_done"))
    g_high, g_low = c.sem("a_g_high"), c.sem("a_g_low")
    wz_high, wz_low, wo_high, wo_low = (c.sem(f"a_{n}") for n in ("wz_high", "wz_low", "wo_high", "wo_low"))
    out_done, added = c.sem("a_out_done"), c.sem("a_added")
    JOBS = [(n, m) for n in range(HALVES) for m in range(KI)]
    OUT = TT // HALVES
    with nc.Block() as block:
        @block.sync
        def _(sp):
            sp.dma_start(woutT[:], tiled(c.dram["woutT"])).then_inc(in_out, 16)

        @block.tensor
        def _(pe):
            for j, (n, m) in enumerate(JOBS):
                tok = slice(n * BANK, (n + 1) * BANK)
                if j < 2:
                    pe.wait_ge(wz_low, j + 1)
                if j == KI // 2:
                    pe.wait_ge(wz_low, 2)
                if j >= 2:
                    pe.wait_ge(silu_done, j - 1)
                for k in range(KD):
                    last = product_of_parts(nc, c.ps[:, j % 2, :], [w[:, k, m * P:(m + 1) * P] for w in winz_parts],
                                            [x[:, k, tok] for x in x_parts], k == 0, k == KD - 1)
                last.then_inc(z_done, 1)
                if j >= 2:
                    pe.wait_ge(g_done, j - 1)
                for k in range(KD):
                    last = product_of_parts(nc, c.ps[:, 2 + j % 2, :], [w[:, k, m * P:(m + 1) * P] for w in wp_parts],
                                            [x[:, k, tok] for x in x_parts], k == 0, k == KD - 1)
                last.then_inc(y_done, 1)
                if m < KI - 1:
                    continue
                for t in range(OUT * n, OUT * (n + 1)):
                    pe.wait_ge(wo_low, 1)
                    pe.wait_ge(g_low, KI * (n + 1))
                    if t >= 4:
                        pe.wait_ge(added, t - 3)
                    col = slice(t % OUT * P, (t % OUT + 1) * P)
                    for k in range(KI):
                        last = product_of_parts(nc, c.ps[:, 4 + t % 4, :], [w[:, k, col] for w in g_parts],
                                                [w[:, k, :] for w in wout_parts], k == 0, k == KI - 1)
                    last.then_inc(out_done, 1)

        @block.scalar
        def _(act):
            act.wait_ge(in_z, 16)
            for half in range(2):
                col = slice(half * BANK, (half + 1) * BANK)
                nc.scalar.activation(winz_parts[0][:, :, col], winzT[:, :, col], ACT.Copy).then_inc(wz_high, 1)
            act.wait_ge(in_out, 16)
            nc.scalar.activation(wout_parts[0][:], woutT[:], ACT.Copy).then_inc(wo_high, 1)

            def high_gated(j):
                n, m = JOBS[j]
                act.wait_ge(g_done, j + 1)
                if m == 0:
                    act.wait_ge(wz_low, 2)
                    if n >= 1:
                        act.wait_ge(out_done, OUT * n)
                nc.scalar.activation(g_parts[0][:, m, :], g[:, j % 2, :], ACT.Copy).then_inc(g_high, 1)

            for j, (n, m) in enumerate(JOBS):
                act.wait_ge(z_done, j + 1)
                if j >= 2:
                    act.wait_ge(g_done, j - 1)
                nc.scalar.activation(sz[:, j % 2, :], c.ps[:, j % 2, :], ACT.Silu).then_inc(silu_done, 1)
                if m >= 1:
                    high_gated(j - 1)
                if m == KI - 1:
                    high_gated(j)

        @block.vector
        def _(dve):
            for half in range(2):
                col = slice(half * BANK, (half + 1) * BANK)
                dve.wait_ge(wz_high, half + 1)
                nc.vector.tensor_tensor(winz_parts[1][:, :, col], winzT[:, :, col], winz_parts[0][:, :, col].bitcast(F32),
                                        ALU.subtract).then_inc(wz_low, 1)
            dve.wait_ge(wo_high, 1)
            nc.vector.tensor_tensor(wout_parts[1][:], woutT[:], wout_parts[0][:].bitcast(F32), ALU.subtract).then_inc(wo_low, 1)
            dve.wait_ge(wo_low, 1)
            dve.wait_ge(in_d, 16)
            for j, (n, m) in enumerate(JOBS):
                dve.wait_ge(y_done, j + 1)
                dve.wait_ge(silu_done, j + 1)
                if j >= 2:
                    dve.wait_ge(g_low, j - 1)
                nc.vector.scalar_tensor_tensor(g[:, j % 2, :], c.ps[:, 2 + j % 2, :], Dv[:, m:m + 1],
                                               sz[:, j % 2, :], ALU.mult, ALU.mult).then_inc(g_done, 1)
                dve.wait_ge(g_high, j + 1)
                nc.vector.tensor_tensor(g_parts[1][:, m, :], g[:, j % 2, :], g_parts[0][:, m, :].bitcast(F32),
                                        ALU.subtract).then_inc(g_low, 1)
                if m < KI - 1:
                    continue
                for t in range(OUT * n, OUT * (n + 1)):
                    dve.wait_ge(out_done, t + 1)
                    nc.vector.tensor_tensor(c.x[:, t, :], c.ps[:, 4 + t % 4, :], c.x[:, t, :], ALU.add).then_inc(added, 1)
            dve.wait_ge(added, TT)



ROUND = 1.5 * 2.0 ** 23


def int8_rows(c, tag, src, ints, scale, n):
    nc, dve = c.nc, c.nc.vector
    step = c.sem(f"{tag}_step")
    inv = c.at(f"{tag}_inv", [P, n], F32, 50.5)
    nc.vector.tensor_reduce(scale[:], src[:], AX.X, ALU.max, apply_absolute_value=True).then_inc(step, 1)
    dve.wait_ge(step, 1)
    nc.vector.tensor_scalar(scale[:], scale[:], 1.0 / 127.0, 1e-8, ALU.mult, ALU.max).then_inc(step, 1)
    dve.wait_ge(step, 2)
    nc.vector.reciprocal(inv[:], scale[:]).then_inc(step, 1)
    dve.wait_ge(step, 3)
    for j in range(n):
        nc.vector.tensor_scalar(src[:, j, :], src[:, j, :], inv[:, j:j + 1], ROUND, ALU.mult, ALU.add).then_inc(step, 1)
    for j in range(n):
        dve.wait_ge(step, 4 + j)
        last = nc.vector.tensor_scalar(ints[:, j, :], src[:, j, :], -ROUND, None, ALU.add)
    return last


def cross_attention(c):
    nc = c.nc
    H, DH, KEYS = 16, 32, 1024
    KT = KEYS // P
    KF = c.at("b_KF", [P, KD, CTX], F32, 52)
    V = c.at("b_V", [P, CTX // P, H, DH], F32, 84)
    wpT = c.at("b_wpT", [P, KD, DM], BF16, 117)
    bv = c.at("b_bv", [P, DM], F32, 121)
    swp_row = c.at("b_swp_row", [P, DM], F32, 121)
    wqT = c.at("b_wqT", [P, KD, DM], BF16, 123)
    wq_int = c.at("b_wq_int", [P, KD, DM], BF16, 127)
    wp_int = c.at("b_wp_int", [P, KD, DM], BF16, 131)
    xq = c.at("b_xq", [P, TT, DM], BF16, 135)
    wk_parts = [c.at("b_wk_high", [P, KD, DM], F32R, 143), c.at("b_wk_low", [P, KD, DM], F32R, 151)]
    wv_parts = [c.at("b_wv_high", [P, KD, DM], F32R, 159), c.at("b_wv_low", [P, KD, DM], F32R, 167)]
    wkT = c.at("b_wkT", [P, KD, DM], F32, 175)
    wvT = c.at("b_wvT", [P, KD, DM], F32, 183)
    wq = c.at("b_wq", [P, KD, DM], F32, 175)
    wp = c.at("b_wp", [P, KD, DM], F32, 183)
    CHUNK = 2 * P
    ctxT = c.at("b_ctxT", [P, 2, KD, CHUNK], F32, 191)
    ctx_parts = [c.at("b_ctx_high", [P, 2, KD, CHUNK], F32R, 199), c.at("b_ctx_low", [P, 2, KD, CHUNK], F32R, 16)]
    xqF = c.at("b_xqF", [P, KD, TOK], BF16, 143)
    sx_row = c.at("b_sx_row", [P, TOK], F32, 151)
    q_raw = c.at("b_q_raw", [P, 2, BANK], F32, 155)
    qF = c.at("b_qF", [P, KD, TOK], F32, 16)
    o = c.at("b_o", [P, TT, DM], F32, 32)
    kS = c.at("b_kS", [P, 2, 4, KEYS], F32R, 123)
    qS = c.at("b_qS", [P, 2, 4, BANK], F32R, 155)
    k_parts = c.at("b_k_parts", [P, 2, KEYS], F32R, 171)
    q_parts = c.at("b_q_parts", [P, 2, BANK], F32R, 179)
    pr = c.at("b_pr", [P, 2, BANK], F32, 183)
    pr_hi = c.at("b_pr_hi", [P, 3, BANK], F32R, 187)
    pr_lo = c.at("b_pr_lo", [P, 3, BANK], F32R, 193)
    oT = c.at("b_oT", [2 * DH + 1, BANK], F32, 199)
    VS = c.at("b_VS", [P, 2, KT, 2 * DH + 1], F32R, 201)
    nm_parts = c.at("b_nm_parts", [16, 2, 2, P], F32R, 205.25)
    nm = c.at("b_nm", [P, 2, 16], F32, 207.3125)
    oinv = c.at("b_oinv", [P, 2, 4], F32, 207.4375)
    fold = c.at("b_fold", [2 * DH + 1, DH + 1], F32, 116)
    mark = c.at("b_mark", [1, 1], F32, 116.25)
    oq = c.at("b_oq", [P, TT, DM], BF16, 123)
    oqF = c.at("b_oqF", [P, KD, TOK], BF16, 131)
    bq = c.at("b_bq", [P, KD], F32, 50.0625)
    bk = c.at("b_bk", [P, KD], F32, 50.125)
    sx = c.at("b_sx", [P, TT], F32, 50.1875)
    swq = c.at("b_swq", [P, KD], F32, 50.25)
    swp = c.at("b_swp", [P, KD], F32, 50.3125)
    so = c.at("b_so", [P, TT], F32, 50.375)
    bp = c.at("b_bp", [P, DM], F32, 30)

    NC = CTX // CHUNK
    in_k, in_v, in_wq, in_b = c.sem("b_in_k"), c.sem("b_in_v"), c.sem("b_in_wq"), c.sem("b_in_b")
    in_ctx = [c.sem(f"b_in_ctx{slot}") for slot in range(2)]
    w_high, w_low, ctx_high, ctx_low = (c.sem(f"b_{n}") for n in ("w_high", "w_low", "ctx_high", "ctx_low"))

    k_done, k_moved, v_done, v_moved = (c.sem(f"b_{n}") for n in ("k_done", "k_moved", "v_done", "v_moved"))
    normed, aggr_done, rstd_done = c.sem("b_normed"), c.sem("b_aggr_done"), c.sem("b_rstd_done")
    with nc.Block() as block:
        @block.sync
        def _(sp):
            def context(n):
                if n >= 2:
                    sp.wait_ge(ctx_low, n - 1)
                sp.dma_start(ctxT[:, n % 2], tiled(c.dram["ctxT"])[:, :, n * CHUNK:(n + 1) * CHUNK]).then_inc(in_ctx[n % 2], 16)

            sp.dma_start(wkT[:], tiled(c.dram["b_wkT"])).then_inc(in_k, 16)
            context(0)
            sp.dma_start(wvT[:], tiled(c.dram["b_wvT"])).then_inc(in_v, 16)
            context(1)
            sp.dma_start(bq[:], c.dram["b_bq"]).then_inc(in_b, 16)
            sp.dma_start(bk[:], c.dram["b_bk"]).then_inc(in_b, 16)
            sp.dma_start(bv[:], c.dram["b_bv"].partition_broadcast(P)).then_inc(in_b, 16)
            sp.dma_start(bp[:], c.dram["b_bp"].partition_broadcast(P)).then_inc(in_b, 16)
            sp.wait_ge(w_low, 2)
            sp.dma_start(wq[:], tiled(c.dram["b_wq"])).then_inc(in_wq, 16)
            sp.dma_start(wp[:], tiled(c.dram["b_wp"])).then_inc(in_wq, 16)
            for n in range(2, NC):
                context(n)

        @block.tensor
        def _(pe):
            for n in range(NC):
                pe.wait_ge(w_low, 1)
                pe.wait_ge(ctx_low, n + 1)
                for m in range(KD):
                    j = n * KD + m
                    if j >= 4:
                        pe.wait_ge(k_moved, j - 3)
                    for k in range(KD):
                        last = product_of_parts(nc, c.ps[:, j % 4, 0:CHUNK], [w[:, k, m * P:(m + 1) * P] for w in wk_parts],
                                                [x[:, n % 2, k, :] for x in ctx_parts], k == 0, k == KD - 1)
                    last.then_inc(k_done, 1)
                pe.wait_ge(w_low, 2)
                for i in range(CHUNK // P):
                    j = n * (CHUNK // P) + i
                    if j >= 4:
                        pe.wait_ge(v_moved, j - 3)
                    for k in range(KD):
                        last = product_of_parts(nc, c.ps[:, 4 + j % 4, :], [x[:, n % 2, k, i * P:(i + 1) * P] for x in ctx_parts],
                                                [w[:, k, :] for w in wv_parts], k == 0, k == KD - 1)
                    last.then_inc(v_done, 1)

        @block.scalar
        def _(act):
            def high_context(n):
                act.wait_ge(in_ctx[n % 2], 16 * (n // 2 + 1))
                if n >= 2:
                    act.wait_ge(v_done, (n - 1) * (CHUNK // P))
                nc.scalar.activation(ctx_parts[0][:, n % 2], ctxT[:, n % 2], ACT.Copy).then_inc(ctx_high, 1)

            act.wait_ge(in_k, 16)
            nc.scalar.activation(wk_parts[0][:], wkT[:], ACT.Copy).then_inc(w_high, 1)
            high_context(0)
            act.wait_ge(in_v, 16)
            nc.scalar.activation(wv_parts[0][:], wvT[:], ACT.Copy).then_inc(w_high, 1)
            high_context(1)
            act.wait_ge(in_b, 64)
            for j in range(NC * KD):
                n, m = j // KD, j % KD
                act.wait_ge(k_done, j + 1)
                nc.scalar.activation(KF[:, m, n * CHUNK:(n + 1) * CHUNK], c.ps[:, j % 4, 0:CHUNK], ACT.Identity,
                                     bias=bk[:, m:m + 1]).then_inc(k_moved, 1)
                if m == KD - 1 and n + 2 < NC:
                    high_context(n + 2)

        @block.gpsimd
        def _(pool):
            rstd_pool(c, aggr_done, rstd_done)

        @block.vector
        def _(dve):
            def low_weights(i, raw, parts):
                dve.wait_ge(w_high, i + 1)
                nc.vector.tensor_tensor(parts[1][:], raw[:], parts[0][:].bitcast(F32), ALU.subtract).then_inc(w_low, 1)

            def low_context(n):
                dve.wait_ge(ctx_high, n + 1)
                nc.vector.tensor_tensor(ctx_parts[1][:, n % 2], ctxT[:, n % 2], ctx_parts[0][:, n % 2].bitcast(F32),
                                        ALU.subtract).then_inc(ctx_low, 1)

            low_weights(0, wkT, wk_parts)
            low_context(0)
            low_weights(1, wvT, wv_parts)
            low_context(1)
            layernorm_dve(c, "b", aggr_done, rstd_done, normed)
            dve.wait_ge(normed, TT)
            dve.wait_ge(in_b, 64)
            for n in range(NC):
                for j in range(n * (CHUNK // P), (n + 1) * (CHUNK // P)):
                    dve.wait_ge(v_done, j + 1)
                    nc.vector.tensor_tensor(V[:, j, :, :], c.ps[:, 4 + j % 4, :].rearrange("p (h d) -> p h d", h=H),
                                            bv[:].rearrange("p (h d) -> p h d", h=H), ALU.add).then_inc(v_moved, 1)
                if n + 2 < NC:
                    low_context(n + 2)
                if n == 0:
                    int8_rows(c, "b_x8", c.xn, xq, sx, TT)
                elif n == 1:
                    dve.wait_ge(in_wq, 32)
                    int8_rows(c, "b_wq8", wq, wq_int, swq, KD)
                elif n == 2:
                    int8_rows(c, "b_wp8", wp, wp_int, swp, KD)
                elif n == 3:
                    for t in range(TT):
                        nc.vector.tensor_tensor(c.x[:, t, :], c.x[:, t, :], bp[:], ALU.add)

    turned, turned_act, turned_dve = c.sem("b_turned"), c.sem("b_turned_act"), c.sem("b_turned_dve")
    spread, spread_moved = c.sem("b_spread"), c.sem("b_spread_moved")
    SOURCES = ([(wq_int, wqT, m) for m in range(KD)] + [(wp_int, wpT, m) for m in range(KD)]
               + [(xq, xqF, t) for t in range(TT)])

    def turn_target(j):
        _, dst, m = SOURCES[j]
        return dst[:, :, m * P:(m + 1) * P]

    def turned_bank(j):
        return c.ps[:, j % 4, 0:BANK // 2].bitcast(BF16).rearrange("p (k t) -> p k t", k=KD)

    with nc.Block() as block:
        @block.tensor
        def _(pe):
            for j, (src, _, m) in enumerate(SOURCES):
                if j >= 4 and j % 2 == 0:
                    pe.wait_ge(turned_act, (j - 4) // 2 + 1)
                elif j >= 4:
                    pe.wait_ge(turned_dve, (j - 4) // 2 + 1)
                for k in range(KD):
                    last = nc.tensor.transpose(turned_bank(j)[:, k, :], src[:, m, k * P:(k + 1) * P], c.identb[:])
                last.then_inc(turned, 1)
            for t in range(TT):
                last = nc.tensor.matmul(c.ps[:, 4 + t // 4, t % 4 * P:(t % 4 + 1) * P],
                                        sx[:, t:t + 1].to_broadcast([P, P]), c.ident[:], start=True, stop=True)
            last.then_inc(spread, 1)
            for m in range(KD):
                last = nc.tensor.matmul(c.ps[:, 6, m * P:(m + 1) * P],
                                        swp[:, m:m + 1].to_broadcast([P, P]), c.ident[:], start=True, stop=True)
            last.then_inc(spread, 1)

        @block.scalar
        def _(act):
            for j in range(0, len(SOURCES), 2):
                act.wait_ge(turned, j + 1)
                nc.scalar.activation(turn_target(j), turned_bank(j), ACT.Copy).then_inc(turned_act, 1)
            act.wait_ge(spread, 1)
            nc.scalar.activation(sx_row[:].rearrange("p (a n) -> p a n", a=2), c.ps[:, 4:6, :], ACT.Copy)
            act.wait_ge(spread, 2)
            nc.scalar.activation(swp_row[:], c.ps[:, 6, :], ACT.Copy).then_inc(spread_moved, 1)

        @block.vector
        def _(dve):
            for j in range(1, len(SOURCES), 2):
                dve.wait_ge(turned, j + 1)
                nc.vector.tensor_copy(turn_target(j), turned_bank(j)).then_inc(turned_dve, 1)

    scales_ready = c.sem("b_scales_ready")
    q_done, q_scaled, q_ready = c.sem("b_q_done"), c.sem("b_q_scaled"), c.sem("b_q_ready")
    with nc.Block() as block:
        @block.tensor
        def _(pe):
            for j in range(2 * KD):
                n, m = j // KD, j % KD
                for k in range(KD):
                    last = nc.tensor.matmul(c.ps[:, j, :], wqT[:, k, m * P:(m + 1) * P],
                                            xqF[:, k, n * BANK:(n + 1) * BANK], start=k == 0, stop=k == KD - 1)
                last.then_inc(q_done, 1)

        @block.vector
        def _(dve):
            nc.vector.tensor_scalar(swq[:], swq[:], DH ** -0.5, None, ALU.mult).then_inc(scales_ready, 1)
            nc.vector.tensor_scalar(bq[:], bq[:], DH ** -0.5, None, ALU.mult).then_inc(scales_ready, 1)
            dve.wait_ge(scales_ready, 2)
            for j in range(2 * KD):
                n, m = j // KD, j % KD
                dve.wait_ge(q_done, j + 1)
                if j >= 2:
                    dve.wait_ge(q_ready, j - 1)
                nc.vector.scalar_tensor_tensor(q_raw[:, j % 2, :], c.ps[:, j, :], swq[:, m:m + 1],
                                               sx_row[:, n * BANK:(n + 1) * BANK], ALU.mult, ALU.mult).then_inc(q_scaled, 1)

        @block.scalar
        def _(act):
            act.wait_ge(scales_ready, 2)
            for j in range(2 * KD):
                n, m = j // KD, j % KD
                act.wait_ge(q_scaled, j + 1)
                nc.scalar.activation(qF[:, m, n * BANK:(n + 1) * BANK], q_raw[:, j % 2, :], ACT.Identity,
                                     bias=bq[:, m:m + 1]).then_inc(q_ready, 1)

    GROUPS = [(b, f) for b in range(2) for f in range(KD)]
    NG, QT = len(GROUPS), BANK // P
    STEPS, UNITS = 4 * KT, 4 * QT
    HEADS, NS = 4 * NG, NG * STEPS
    LAG = 3
    in_st = [[c.sem(f"b_in_st{i}{h}") for h in range(4)] for i in range(2)]
    in_rows = [c.sem(f"b_in_rows{i}") for i in range(2)]
    split_done, split_low, vsplit_done = c.sem("b_split_done"), c.sem("b_split_low"), c.sem("b_vsplit_done")
    job_done, job_read = c.sem("b_job_done"), c.sem("b_job_read")
    nm_split, ones_set, vones_set, fold_set = (c.sem(f"b_{n}") for n in ("nm_split", "ones_set", "vones_set", "fold_set"))
    st_done, exp_done, hi_done, lo_done, av_done = (c.sem(f"b_{n}") for n in ("st_done", "exp_done", "hi_done", "lo_done", "av_done"))
    o_moved, inv_done = c.sem("b_o_moved"), c.sem("b_inv_done")

    JOBS, JOBS_AT = [("max", 0, u) for u in range(UNITS)] + [("turn", 0, 0)], []
    FIRST_JOBS = len(JOBS)
    LEAD, TURN_AT, HEAD_AT = 8, 25, KT + 5
    MAX_AT = {(g + 1, u): max(0, STEPS * g - LEAD + 2 * u) for g in range(NG - 1) for u in range(UNITS)}
    for n in range(NS + 8):
        g, here = n // STEPS, len(JOBS)
        JOBS += [("max",) + gu for gu, at in MAX_AT.items() if at == n]
        if n >= HEAD_AT and (n - HEAD_AT) % KT == 0 and (n - HEAD_AT) // KT < HEADS:
            JOBS.append(("head", (n - HEAD_AT) // KT, 0))
        if g + 1 < NG and n % STEPS == TURN_AT:
            JOBS.append(("turn", g + 1, 0))
        JOBS_AT.append(range(here, len(JOBS)))

    with nc.Block() as block:
        @block.gpsimd
        def _(pool):
            def split_group(g, part):
                b, f = GROUPS[g]
                k, q = KF[:, f, b * KEYS:(b + 1) * KEYS], qF[:, f, b * BANK:(b + 1) * BANK]
                if part == 0:
                    for h in range(4):
                        pool.wait_ge(in_st[(g - 1) % 2][h], 96 * ((g - 1) // 2 + 1))
                src, parts = ((k, k_parts), (q, q_parts))[part % 2]
                if part < 2:
                    nc.gpsimd.tensor_copy(parts[:, 0, :], src).then_inc(split_done, 1)
                else:
                    pool.wait_ge(split_done, 2 + 4 * (g - 1) + part - 1)
                    nc.gpsimd.tensor_tensor(parts[:, 1, :], src, parts[:, 0, :].bitcast(F32), ALU.subtract).then_inc(split_done, 1)

            def split_values(q, part):
                (b, f), h = GROUPS[q // 4], q % 4
                src = V[:, b * KT:(b + 1) * KT, 4 * f + h, :]
                if part == 0:
                    if q >= 2:
                        pool.wait_ge(av_done, KT * (q - 1))
                    nc.gpsimd.tensor_copy(VS[:, q % 2, :, 0:DH], src).then_inc(vsplit_done, 1)
                else:
                    pool.wait_ge(vsplit_done, 2 * q + 1)
                    nc.gpsimd.tensor_tensor(VS[:, q % 2, :, DH:2 * DH], src, VS[:, q % 2, :, 0:DH].bitcast(F32),
                                            ALU.subtract).then_inc(vsplit_done, 1)

            for part in range(2):
                split_values(0, part)
            for part in range(4):
                split_group(1, part)
            for n in range(NS):
                g, i = n // STEPS, n % STEPS
                if i in range(4, 8) and g + 2 < NG:
                    split_group(g + 2, i - 4)
                if i % KT in range(2, 4) and n // KT + 1 < HEADS:
                    split_values(n // KT + 1, i % KT - 2)

        @block.sync
        def _(sp):
            def stack(g, h):
                s_, rows = g % 2, slice(h * DH, (h + 1) * DH)
                sp.wait_ge(split_done, 2 + 4 * g)
                sp.wait_ge(split_low, 2)
                if g >= 2:
                    sp.wait_ge(st_done, STEPS * (g - 2) + KT * (h + 1))
                for place, part in enumerate((0, 0, 1)):
                    sp.dma_start(kS[place * DH:(place + 1) * DH, s_, h, :].bitcast(F32),
                                 k_parts[rows, part, :].bitcast(F32)).then_inc(in_st[s_][h], 16)
                for place, part in enumerate((0, 1, 0)):
                    sp.dma_start(qS[place * DH:(place + 1) * DH, s_, h, :].bitcast(F32),
                                 q_parts[rows, part, :].bitcast(F32)).then_inc(in_st[s_][h], 16)

            def maxima(g):
                s_ = g % 2
                sp.wait_ge(nm_split, 2 * (g + 1))
                for part in range(2):
                    for h in range(4):
                        sp.dma_start(qS[96 + part:97 + part, s_, h, :].bitcast(F32),
                                     nm_parts[h * QT:(h + 1) * QT, s_, part, :].bitcast(F32)).then_inc(in_rows[s_], 16)

            for h in range(4):
                stack(0, h)
            for g in range(NG):
                for h in range(3):
                    if g + 1 < NG:
                        stack(g + 1, h)
                maxima(g)
                if g + 1 < NG:
                    stack(g + 1, 3)

        @block.tensor
        def _(pe):
            def job(j):
                kind, g, u = JOBS[j]
                banks = 2 * (j % 2)
                if j >= 2:
                    pe.wait_ge(job_read, j - 1)
                if kind == "max":
                    h, t, s_ = u // QT, u % QT, g % 2
                    if t == 0:
                        pe.wait_ge(in_st[s_][h], 96 * (g // 2 + 1))
                    for n in range(2):
                        last = nc.tensor.matmul(c.ps[:, banks + n, :], qS[0:96, s_, h, t * P:(t + 1) * P],
                                                kS[0:96, s_, h, n * BANK:(n + 1) * BANK], start=True, stop=True)
                elif kind == "turn":
                    pe.wait_ge(job_read, j)
                    last = nc.tensor.transpose(c.ps[0:16, banks, 0:P], nm[:, g % 2, :], c.ident[:])
                else:
                    pe.wait_ge(o_moved, g + 1)
                    for t in range(QT):
                        last = nc.tensor.matmul(c.ps[:, banks, t * (DH + 1):(t + 1) * (DH + 1)],
                                                oT[:, t * P:(t + 1) * P], fold[:], start=True, stop=True)
                last.then_inc(job_done, 1)

            def scores(n):
                g, h, k = n // STEPS, n % STEPS // KT, n % KT
                if n % STEPS == 0:
                    pe.wait_ge(in_rows[g % 2], 128 * (g // 2 + 1))
                if n >= 2:
                    pe.wait_ge(hi_done, n - 1)
                nc.tensor.matmul(c.ps[:, 4 + n % 2, :], kS[0:98, g % 2, h, k * P:(k + 1) * P], qS[0:98, g % 2, h, :],
                                 start=True, stop=True).then_inc(st_done, 1)

            def weigh(n):
                q, k = n // KT, n % KT
                if k == 0:
                    pe.wait_ge(vsplit_done, 2 * (q + 1))
                    if q >= 2:
                        pe.wait_ge(o_moved, q - 1)
                pe.wait_ge(hi_done, n + 1)
                nc.tensor.matmul(c.ps[0:2 * DH + 1, 6 + q % 2, :], VS[:, q % 2, k, :], pr_hi[:, n % 3, :],
                                 start=k == 0, stop=False)
                pe.wait_ge(lo_done, n + 1)
                nc.tensor.matmul(c.ps[0:2 * DH + 1, 6 + q % 2, :], VS[:, q % 2, k, :], pr_lo[:, n % 3, :],
                                 start=False, stop=k == KT - 1).then_inc(av_done, 1)

            for j in range(FIRST_JOBS):
                job(j)
            pe.wait_ge(ones_set, 1)
            pe.wait_ge(vones_set, 1)
            pe.wait_ge(fold_set, 3)
            for n in range(NS + 8):
                if n < NS:
                    scores(n)
                for j in JOBS_AT[n]:
                    job(j)
                if LAG <= n < NS + LAG:
                    weigh(n - LAG)

        @block.scalar
        def _(act):
            (b, f) = GROUPS[0]
            nc.scalar.activation(k_parts[:, 0, :], KF[:, f, b * KEYS:(b + 1) * KEYS], ACT.Copy).then_inc(split_done, 1)
            nc.scalar.activation(q_parts[:, 0, :], qF[:, f, b * BANK:(b + 1) * BANK], ACT.Copy).then_inc(split_done, 1)

            def move_result(q):
                act.wait_ge(av_done, KT * (q + 1))
                if q >= 1:
                    act.wait_ge(job_done, JOBS.index(("head", q - 1, 0)) + 1)
                nc.scalar.activation(oT[:], c.ps[0:2 * DH + 1, 6 + q % 2, :], ACT.Copy).then_inc(o_moved, 1)

            for n in range(NS + 4):
                if n < NS:
                    act.wait_ge(st_done, n + 1)
                    if n >= 2:
                        act.wait_ge(lo_done, n - 1)
                    nc.scalar.activation(pr[:, n % 2, :], c.ps[:, 4 + n % 2, :], ACT.Exp).then_inc(exp_done, 1)
                    if n >= 3:
                        act.wait_ge(av_done, n - 2)
                    nc.scalar.activation(pr_hi[:, n % 3, :], c.ps[:, 4 + n % 2, :], ACT.Exp).then_inc(hi_done, 1)
                if n >= 11 and (n - 11) % KT == 0:
                    move_result((n - 11) // KT)

        @block.vector
        def _(dve):
            def job(j):
                kind, g, u = JOBS[j]
                banks = 2 * (j % 2)
                dve.wait_ge(job_done, j + 1)
                if kind == "max":
                    nc.vector.tensor_reduce(nm[:, g % 2, u:u + 1], c.ps[:, banks:banks + 2, :], AX.XY, ALU.max,
                                            negate=True).then_inc(job_read, 1)
                elif kind == "turn":
                    turned = c.ps[0:16, banks, 0:P]
                    if g >= 2:
                        dve.wait_ge(in_rows[g % 2], 128 * (g // 2))
                    nc.vector.tensor_copy(nm_parts[:, g % 2, 0, :], turned).then_inc(nm_split, 1)
                    dve.wait_ge(nm_split, 2 * g + 1)
                    nc.vector.tensor_tensor(nm_parts[:, g % 2, 1, :], turned, nm_parts[:, g % 2, 0, :].bitcast(F32),
                                            ALU.subtract).then_inc(nm_split, 1)
                    dve.wait_ge(nm_split, 2 * (g + 1))
                    nc.vector.memset(mark[:], 0.0).then_inc(job_read, 1)
                else:
                    (b, f), h = GROUPS[g // 4], g % 4
                    acc = c.ps[:, banks, 0:QT * (DH + 1)].rearrange("p (t d) -> p t d", t=QT)
                    nc.vector.reciprocal(oinv[:, g % 2, :], acc[:, :, DH]).then_inc(inv_done, 1)
                    dve.wait_ge(inv_done, g + 1)
                    nc.vector.tensor_tensor(o[:, QT * b:QT * (b + 1), (4 * f + h) * DH:(4 * f + h + 1) * DH], acc[:, :, 0:DH],
                                            oinv[:, g % 2, :].unsqueeze(2).to_broadcast([P, QT, DH]), ALU.mult).then_inc(job_read, 1)

            (b, f) = GROUPS[0]
            dve.wait_ge(split_done, 1)
            nc.vector.tensor_tensor(k_parts[:, 1, :], KF[:, f, b * KEYS:(b + 1) * KEYS], k_parts[:, 0, :].bitcast(F32),
                                    ALU.subtract).then_inc(split_low, 1)
            dve.wait_ge(split_done, 2)
            nc.vector.tensor_tensor(q_parts[:, 1, :], qF[:, f, b * BANK:(b + 1) * BANK], q_parts[:, 0, :].bitcast(F32),
                                    ALU.subtract).then_inc(split_low, 1)
            nc.vector.memset(kS[96:98, :, :, :].bitcast(F32), 1.0).then_inc(ones_set, 1)
            nc.vector.memset(VS[:, :, :, 2 * DH:].bitcast(F32), 1.0).then_inc(vones_set, 1)
            nc.vector.tensor_copy(fold[0:DH, :], c.ident[0:DH, 0:DH + 1]).then_inc(fold_set, 1)
            nc.vector.tensor_copy(fold[DH:2 * DH, :], c.ident[DH:2 * DH, DH:2 * DH + 1]).then_inc(fold_set, 1)
            nc.vector.tensor_copy(fold[2 * DH:2 * DH + 1, :], c.ident[2 * DH:2 * DH + 1, DH:2 * DH + 1]).then_inc(fold_set, 1)
            for j in range(FIRST_JOBS):
                job(j)
            for n in range(NS + 8):
                for j in JOBS_AT[n]:
                    job(j)
                if n < NS:
                    dve.wait_ge(exp_done, n + 1)
                    dve.wait_ge(hi_done, n + 1)
                    if n >= 3:
                        dve.wait_ge(av_done, n - 2)
                    nc.vector.tensor_tensor(pr_lo[:, n % 3, :], pr[:, n % 2, :], pr_hi[:, n % 3, :].bitcast(F32),
                                            ALU.subtract).then_inc(lo_done, 1)
            dve.wait_ge(job_read, len(JOBS))
            int8_rows(c, "b_o8", o, oq, so, TT)

    oturned, oturned_moved, out_done, out_scaled = (c.sem(f"b_{n}") for n in ("oturned", "oturned_moved", "out_done", "out_scaled"))
    added = c.sem("b_added")
    tmp = c.at("b_tmp", [P, 2, DM], F32, 139)
    with nc.Block() as block:
        def obank(t):
            return c.ps[:, t % 4, 0:BANK // 2].bitcast(BF16).rearrange("p (k t) -> p k t", k=KD)

        @block.tensor
        def _(pe):
            for t in range(TT + 1):
                if t < TT:
                    if t >= 4:
                        pe.wait_ge(oturned_moved, t - 3)
                    for k in range(KD):
                        last = nc.tensor.transpose(obank(t)[:, k, :], oq[:, t, k * P:(k + 1) * P], c.identb[:])
                    last.then_inc(oturned, 1)
                if t >= 1:
                    t0 = t - 1
                    pe.wait_ge(oturned_moved, t0 + 1)
                    if t0 >= 4:
                        pe.wait_ge(out_scaled, t0 - 3)
                    for k in range(KD):
                        last = nc.tensor.matmul(c.ps[:, 4 + t0 % 4, :], oqF[:, k, t0 * P:(t0 + 1) * P], wpT[:, k, :],
                                                start=k == 0, stop=k == KD - 1)
                    last.then_inc(out_done, 1)

        @block.scalar
        def _(act):
            for t in range(TT):
                act.wait_ge(oturned, t + 1)
                nc.scalar.activation(oqF[:, :, t * P:(t + 1) * P], obank(t), ACT.Copy).then_inc(oturned_moved, 1)

        @block.vector
        def _(dve):
            for t in range(TT):
                dve.wait_ge(out_done, t + 1)
                if t >= 2:
                    dve.wait_ge(added, t - 1)
                nc.vector.scalar_tensor_tensor(tmp[:, t % 2, :], c.ps[:, 4 + t % 4, :], so[:, t:t + 1], swp_row[:],
                                               ALU.mult, ALU.mult).then_inc(out_scaled, 1)

        @block.gpsimd
        def _(pool):
            for t in range(TT):
                pool.wait_ge(out_scaled, t + 1)
                nc.gpsimd.tensor_tensor(c.x[:, t, :], c.x[:, t, :], tmp[:, t % 2, :], ALU.add).then_inc(added, 1)



def experts(c):
    nc = c.nc
    E, LAT, HID, SCALE = 16, 128, 256, 2.5
    KH = HID // P
    s1T = c.at("c_s1T", [P, KD, HID], F32, 52)
    sgT = c.at("c_sgT", [P, KD, HID], F32, 56)
    s2T = c.at("c_s2T", [P, KH, DM], F32, 60)
    wdT = c.at("c_wdT", [P, KD, LAT], F32, 64)
    wupT = c.at("c_wupT", [P, DM], F32, 66)
    wgT = c.at("c_wgT", [P, KD, E], F32, 68)
    bias = c.at("c_bias", [P, E], F32, 68.5)
    r1T = c.at("c_r1T", [P, E, HID], F32, 140)
    rgT = c.at("c_rgT", [P, E, HID], F32, 32)
    r1_parts = [c.at("c_r1_high", [P, E, HID], F32R, 72), c.at("c_r1_low", [P, E, HID], F32R, 168)]
    rg_parts = [c.at("c_rg_high", [P, E, HID], F32R, 88), c.at("c_rg_low", [P, E, HID], F32R, 184)]
    r2T = c.at("c_r2T", [P, E, KH, LAT], F32, 104)
    sF = c.at("c_sF", [P, KH, TOK], F32, 120)
    xl_parts = [c.at("c_xl_high", [P, TOK], F32R, 128), c.at("c_xl_low", [P, TOK], F32R, 200)]
    acc = c.at("c_acc", [P, TT, LAT], F32, 132)
    accF = c.at("c_accF", [P, TOK], F32, 136)
    hF = c.at("c_hF", [P, 2, KH, TOK], F32, 140)
    relu = c.at("c_relu", [P, 2, BANK], F32, 156)
    sq = c.at("c_sq", [P, 2, BANK], F32, 160)
    prob = c.at("c_prob", [P, TT, E], F32, 164)
    sel = c.at("c_sel", [P, TT, E], F32, 164.5)
    rest = c.at("c_rest", [P, TT, E], F32, 165)
    top = c.at("c_top", [P, TT, 8], F32, 165.5)
    w = c.at("c_w", [P, TT, E], F32, 166)
    total = c.at("c_total", [P, TT], F32, 166.5)

    in_s, in_r1, in_rg, in_r2 = c.sem("c_in_s"), c.sem("c_in_r1"), c.sem("c_in_rg"), c.sem("c_in_r2")
    with nc.Block() as block:
        @block.sync
        def _(sp):
            sp.dma_start(wdT[:], tiled(c.dram["c_wdT"])).then_inc(in_s, 16)
            sp.dma_start(wgT[:], tiled(c.dram["c_wgT"])).then_inc(in_s, 16)
            sp.dma_start(s1T[:], tiled(c.dram["c_s1T"])).then_inc(in_s, 16)
            sp.dma_start(sgT[:], tiled(c.dram["c_sgT"])).then_inc(in_s, 16)
            sp.dma_start(s2T[:], tiled(c.dram["c_s2T"])).then_inc(in_s, 16)
            sp.dma_start(wupT[:], c.dram["c_wupT"]).then_inc(in_s, 16)
            sp.dma_start(bias[:], c.dram["c_bias"].partition_broadcast(P)).then_inc(in_s, 16)
            sp.dma_start(r1T[:], c.dram["c_r1T"].rearrange("e p n -> p e n")).then_inc(in_r1, 16)
            sp.dma_start(r2T[:], c.dram["c_r2T"].rearrange("e (k p) n -> p e k n", p=P)).then_inc(in_r2, 16)

    norm_and_transpose(c, "c_ln")

    lat_done, lat_moved, logit_done, prob_done = (c.sem(f"c_{n}") for n in ("lat_done", "lat_moved", "logit_done", "prob_done"))
    sg_done, s1_done, relu_done, sq_done, sh_done = (c.sem(f"c_{n}") for n in ("sg_done", "s1_done", "relu_done", "sq_done", "sh_done"))
    step, lat_low, r_high, r_low = c.sem("c_step"), c.sem("c_lat_low"), c.sem("c_r_high"), c.sem("c_r_low")
    JOBS = [(n, m) for n in range(2) for m in range(KH)]
    HALF = E // 2
    SPLITS = [(loaded, w[:, h * HALF:(h + 1) * HALF], [p_[:, h * HALF:(h + 1) * HALF] for p_ in parts])
              for loaded, w, parts in ((in_r1, r1T, r1_parts), (in_rg, rgT, rg_parts)) for h in range(2)]
    with nc.Block() as block:
        @block.sync
        def _(sp):
            sp.dma_start(rgT[:], c.dram["c_rgT"].rearrange("e p n -> p e n")).then_inc(in_rg, 16)

        @block.tensor
        def _(pe):
            pe.wait_ge(in_s, 112)
            for t in range(TT):
                for k in range(KD):
                    last = nc.tensor.matmul(c.ps[:, 6, t * E:(t + 1) * E], c.xF[:, k, t * P:(t + 1) * P], wgT[:, k, :],
                                            start=k == 0, stop=k == KD - 1)
            last.then_inc(logit_done, 1)
            for n in range(2):
                for k in range(KD):
                    last = nc.tensor.matmul(c.ps[:, 4 + n, :], wdT[:, k, :], c.xF[:, k, n * BANK:(n + 1) * BANK],
                                            start=k == 0, stop=k == KD - 1)
                last.then_inc(lat_done, 1)
            for j, (n, m) in enumerate(JOBS):
                for bank, wT, freed, done in ((j % 2, sgT, relu_done, sg_done), (2 + j % 2, s1T, sh_done, s1_done)):
                    if j >= 2:
                        pe.wait_ge(freed, j - 1)
                    for k in range(KD):
                        last = nc.tensor.matmul(c.ps[:, bank, :], wT[:, k, m * P:(m + 1) * P],
                                                c.xF[:, k, n * BANK:(n + 1) * BANK], start=k == 0, stop=k == KD - 1)
                    last.then_inc(done, 1)

        @block.scalar
        def _(act):
            act.wait_ge(logit_done, 1)
            nc.scalar.activation(prob[:].rearrange("p t e -> p (t e)"), c.ps[:, 6, 0:TT * E], ACT.Sigmoid).then_inc(prob_done, 1)
            for n in range(2):
                act.wait_ge(lat_done, n + 1)
                nc.scalar.activation(xl_parts[0][:, n * BANK:(n + 1) * BANK], c.ps[:, 4 + n, :], ACT.Copy).then_inc(lat_moved, 1)
            for j, (n, m) in enumerate(JOBS):
                loaded, src, dst = SPLITS[j]
                act.wait_ge(loaded, 16)
                nc.scalar.activation(dst[0], src, ACT.Copy).then_inc(r_high, 1)
                act.wait_ge(sg_done, j + 1)
                nc.scalar.activation(relu[:, j % 2, :], c.ps[:, j % 2, :], ACT.Relu).then_inc(relu_done, 1)
                act.wait_ge(relu_done, j + 1)
                if j >= 2:
                    act.wait_ge(sh_done, j - 1)
                nc.scalar.activation(sq[:, j % 2, :], relu[:, j % 2, :], ACT.Square).then_inc(sq_done, 1)

        @block.vector
        def _(dve):
            done = [0]

            def chained(ins):
                done[0] += 1
                ins.then_inc(step, 1)
                dve.wait_ge(step, done[0])

            dve.wait_ge(prob_done, 1)
            chained(nc.vector.tensor_tensor(sel[:], prob[:], bias[:].unsqueeze(1).to_broadcast([P, TT, E]), ALU.add))
            for t in range(TT):
                last = nc.vector.max(top[:, t, :], sel[:, t, :])
            chained(last)
            for t in range(TT):
                last = nc.vector.match_replace(rest[:, t, :], top[:, t, :], sel[:, t, :], -3e38)
            chained(last)
            chained(nc.vector.tensor_tensor(sel[:], sel[:], rest[:], ALU.not_equal))
            chained(nc.vector.tensor_tensor(sel[:], sel[:], prob[:], ALU.mult))
            chained(nc.vector.tensor_reduce(total[:], sel[:], AX.X, ALU.add))
            chained(nc.vector.reciprocal(total[:], total[:]))
            chained(nc.vector.tensor_scalar(total[:], total[:], SCALE, None, ALU.mult))
            chained(nc.vector.tensor_tensor(w[:], sel[:], total[:].unsqueeze(2).to_broadcast([P, TT, E]), ALU.mult))
            for n in range(2):
                dve.wait_ge(lat_moved, n + 1)
                tok = slice(n * BANK, (n + 1) * BANK)
                nc.vector.tensor_tensor(xl_parts[1][:, tok], c.ps[:, 4 + n, :], xl_parts[0][:, tok].bitcast(F32),
                                        ALU.subtract).then_inc(lat_low, 1)
            for j, (n, m) in enumerate(JOBS):
                _, src, dst = SPLITS[j]
                dve.wait_ge(r_high, j + 1)
                nc.vector.tensor_tensor(dst[1], src, dst[0].bitcast(F32), ALU.subtract).then_inc(r_low, 1)
                dve.wait_ge(sq_done, j + 1)
                dve.wait_ge(s1_done, j + 1)
                nc.vector.tensor_tensor(sF[:, m, n * BANK:(n + 1) * BANK], c.ps[:, 2 + j % 2, :], sq[:, j % 2, :],
                                        ALU.mult).then_inc(sh_done, 1)

    UP = [(e, n, m) for e in range(E) for n in range(2) for m in range(KH)]
    g_done, a_done, r_done, q_done, h_done = (c.sem(f"c_e_{n}") for n in ("g_done", "a_done", "r_done", "q_done", "h_done"))
    y_done, y_added = c.sem("c_y_done"), c.sem("c_y_added")
    PER = 2 * KH
    with nc.Block() as block:
        @block.tensor
        def _(pe):
            pe.wait_ge(lat_low, 2)
            pe.wait_ge(r_low, len(SPLITS))
            pe.wait_ge(in_r2, 16)

            def up(e):
                for i in range(PER):
                    j = e * PER + i
                    _, n, m = UP[j]
                    for bank, parts, freed, done in ((j % 2, rg_parts, r_done, g_done), (2 + j % 2, r1_parts, h_done, a_done)):
                        if j >= 2:
                            pe.wait_ge(freed, j - 1)
                        product_of_parts(nc, c.ps[:, bank, :], [w_[:, e, m * P:(m + 1) * P] for w_ in parts],
                                         [x[:, n * BANK:(n + 1) * BANK] for x in xl_parts], True, True).then_inc(done, 1)

            def down(e):
                pe.wait_ge(h_done, (e + 1) * PER)
                for n in range(2):
                    if e >= 1:
                        pe.wait_ge(y_added, 2 * (e - 1) + n + 1)
                    for i in range(4):
                        t = 4 * n + i
                        for k in range(KH):
                            last = nc.tensor.matmul(c.ps[:, 4 + n, i * LAT:(i + 1) * LAT], hF[:, e % 2, k, t * P:(t + 1) * P],
                                                    r2T[:, e, k, :], start=k == 0, stop=k == KH - 1)
                    last.then_inc(y_done, 1)

            up(0)
            for e in range(E):
                if e + 1 < E:
                    up(e + 1)
                down(e)

        @block.scalar
        def _(act):
            for j, (e, n, m) in enumerate(UP):
                act.wait_ge(g_done, j + 1)
                nc.scalar.activation(relu[:, j % 2, :], c.ps[:, j % 2, :], ACT.Relu).then_inc(r_done, 1)
                act.wait_ge(r_done, j + 1)
                if j >= 2:
                    act.wait_ge(h_done, j - 1)
                nc.scalar.activation(sq[:, j % 2, :], relu[:, j % 2, :], ACT.Square).then_inc(q_done, 1)

        @block.vector
        def _(dve):
            def hidden(e):
                if e >= 2:
                    dve.wait_ge(y_done, 2 * (e - 1))
                for i in range(PER):
                    j = e * PER + i
                    _, n, m = UP[j]
                    dve.wait_ge(a_done, j + 1)
                    dve.wait_ge(q_done, j + 1)
                    nc.vector.tensor_tensor(hF[:, e % 2, m, n * BANK:(n + 1) * BANK], c.ps[:, 2 + j % 2, :], sq[:, j % 2, :],
                                            ALU.mult).then_inc(h_done, 1)

            hidden(0)
            for e in range(E):
                if e + 1 < E:
                    hidden(e + 1)
                for n in range(2):
                    dve.wait_ge(y_done, 2 * e + n + 1)
                    if e >= 1:
                        dve.wait_ge(y_added, 2 * (e - 1) + n + 1)
                    for i in range(4):
                        t = 4 * n + i
                        src = c.ps[:, 4 + n, i * LAT:(i + 1) * LAT]
                        if e == 0:
                            last = nc.vector.tensor_scalar(acc[:, t, :], src, w[:, t, e:e + 1], None, ALU.mult)
                        else:
                            last = nc.vector.scalar_tensor_tensor(acc[:, t, :], src, w[:, t, e:e + 1], acc[:, t, :],
                                                                  ALU.mult, ALU.add)
                    last.then_inc(y_added, 1)

    a_turned, a_moved, out_done, added = (c.sem(f"c_{n}") for n in ("a_turned", "a_moved", "out_done", "added"))
    with nc.Block() as block:
        @block.tensor
        def _(pe):
            for n in range(2):
                for i in range(4):
                    last = nc.tensor.transpose(c.ps[:, n, i * P:(i + 1) * P], acc[:, 4 * n + i, :], c.ident[:])
                last.then_inc(a_turned, 1)
            for t in range(TT):
                pe.wait_ge(a_moved, 1 + t // 4)
                if t >= 4:
                    pe.wait_ge(added, t - 3)
                for k in range(KH):
                    nc.tensor.matmul(c.ps[:, 4 + t % 4, :], sF[:, k, t * P:(t + 1) * P], s2T[:, k, :],
                                     start=k == 0, stop=False)
                nc.tensor.matmul(c.ps[:, 4 + t % 4, :], accF[:, t * P:(t + 1) * P], wupT[:], start=False,
                                 stop=True).then_inc(out_done, 1)

        @block.scalar
        def _(act):
            for n in range(2):
                act.wait_ge(a_turned, n + 1)
                nc.scalar.activation(accF[:, n * BANK:(n + 1) * BANK], c.ps[:, n, :], ACT.Copy).then_inc(a_moved, 1)

        @block.vector
        def _(dve):
            for t in range(TT):
                dve.wait_ge(out_done, t + 1)
                nc.vector.tensor_tensor(c.x[:, t, :], c.ps[:, 4 + t % 4, :], c.x[:, t, :], ALU.add).then_inc(added, 1)



def linear_attention(c):
    nc = c.nc
    H, D = 32, 64
    PAIRS, GP = H // 2, 4
    CH = TT // 2
    F = H * D
    at = 52.0

    def take(name, shape, dt, kb):
        nonlocal at
        at += kb
        return c.at(f"d_{name}", shape, dt, at - kb)

    mask = take("mask", [P, 2, 2 * GP, P], F32, 8)
    qdec = take("qdec", [P, 2, GP, P], F32, 4)
    wv = take("wv", [P, KD, DM], F32, 8)
    wv_parts = [take(f"wv_{part}", [P, KD, DM], F32R, 8) for part in ("high", "low")]
    w3 = take("w3", [P, 3, KD, P], F32, 6)
    w3_parts = [take(f"w3_{part}", [P, 3, KD, P], F32R, 6) for part in ("high", "low")]
    wo = take("wo", [P, GP, DM], F32, 8)
    x_parts = [c.at("d_x_high", [P, KD, TOK], F32R, 16), take("x_low", [P, KD, TOK], F32R, 16)]
    v = take("v", [P, TT, DM], F32, 16)
    qF = take("qF", [P, TOK], F32, 4)
    qD = take("qD", [P, TOK], F32, 4)
    kF = take("kF", [P, TOK], F32, 4)
    kT = take("kT", [P, TT, P], F32, 4)
    GA = GP + 2
    ga = take("ga", [P, GA, TOK], F32, 4 * GA)
    A = take("A", [P, 2, 2, CH, P], F32, 8)
    S = take("S", [P, CH - 1, 2, P], F32, 3)
    sq = take("sq", [P, 2, BANK], F32, 4)
    sqsum = take("sqsum", [P, TOK], F32, 4)
    y = c.at("d_y", [P, TT, DM], F32, 32)
    kdec = c.at("d_kdec", [P, H], F32, 50.5)
    bdec = c.at("d_bdec", [P, PAIRS], F32, 50.75)
    nw = c.at("d_nw", [P, PAIRS], F32, 51)
    ones = c.at("d_ones", [P, 1], F32, 51.125)
    ms = c.at("d_ms", [P, TT], F32, 51.25)

    in_c = c.sem("d_in_c")
    in_p, in_v, in_o = c.sem("d_in_p"), c.sem("d_in_v"), c.sem("d_in_o")
    w_high, w_low, wv_high, wv_low = (c.sem(f"d_{n}") for n in ("w_high", "w_low", "wv_high", "wv_low"))
    in_g = [c.sem(f"d_in_g{i}") for i in range(2)]
    a_done, a_moved = c.sem("d_a_done"), c.sem("d_a_moved")
    proj_done, proj_moved = c.sem("d_proj_done"), c.sem("d_proj_moved")
    t_done, t_moved = c.sem("d_t_done"), c.sem("d_t_moved")
    u_done, s_ready = c.sem("d_u_done"), c.sem("d_s_ready")
    o_done, sq_done, ga_done = c.sem("d_o_done"), c.sem("d_sq_done"), c.sem("d_ga_done")
    qd_done, sqsum_done = c.sem("d_qd_done"), c.sem("d_sqsum_done")
    step, zeroed = c.sem("d_step"), c.sem("d_zeroed")

    def first_job(p):
        return 6 * p + (0 if p == 0 else TT * (1 + (p - 1) // GP))

    def a_jobs(p):
        return 4 * p + TT * (p // GP)

    def pair_weights(sp, p):
        for i, name in enumerate(("d_wq", "d_wk", "d_wg")):
            sp.dma_start(w3[:, i, :, :], c.dram[name][p, :, :, :]).then_inc(in_p, 16)

    def group_values(sp, g):
        sp.dma_start(wv[:], tiled(c.dram["d_wvT"])[:, :, g * DM:(g + 1) * DM]).then_inc(in_v, 16)

    with nc.Block() as block:
        @block.sync
        def _(sp):
            sp.dma_start(kdec[:], c.dram["d_kdec"]).then_inc(in_c, 16)
            sp.dma_start(bdec[:], c.dram["d_bdec"]).then_inc(in_c, 16)
            sp.dma_start(nw[:], c.dram["d_nw"]).then_inc(in_c, 16)
            pair_weights(sp, 0)
            group_values(sp, 0)

    norm_and_split(c, "d_ln", *x_parts)

    with nc.Block() as block:
        @block.sync
        def _(sp):
            for p in range(PAIRS):
                if p >= 1:
                    sp.wait_ge(w_low, p)
                    pair_weights(sp, p)
                if p % GP == 0:
                    g = p // GP
                    if g >= 1:
                        sp.wait_ge(wv_low, g)
                        group_values(sp, g)
                    if g >= 2:
                        sp.wait_ge(a_moved, a_jobs(GP * (g - 1)))
                        sp.wait_ge(qd_done, 2 * GP * (g - 1))
                    sp.dma_start(mask[:, g % 2, :, :], c.dram["d_mask"][:, g * 2 * GP:(g + 1) * 2 * GP, :]).then_inc(in_g[g % 2], 16)
                    sp.dma_start(qdec[:, g % 2, :, :], c.dram["d_qdec"][:, g * GP:(g + 1) * GP, :]).then_inc(in_g[g % 2], 16)
                    if g == 0:
                        sp.dma_start(wo[:], tiled(c.dram["d_woT"])[:, 0:GP, :]).then_inc(in_o, 16)
                if p % GP == 1 and p > 1:
                    g = p // GP
                    sp.wait_ge(a_moved, a_jobs(GP * g))
                    sp.dma_start(wo[:], tiled(c.dram["d_woT"])[:, g * GP:(g + 1) * GP, :]).then_inc(in_o, 16)

        @block.tensor
        def _(pe):
            def project(j, i, n):
                if j >= 2:
                    pe.wait_ge(proj_moved, j - 1)
                for k in range(KD):
                    last = product_of_parts(nc, c.ps[:, j % 2, :], [w[:, i, k, :] for w in w3_parts],
                                            [x[:, k, n * BANK:(n + 1) * BANK] for x in x_parts], k == 0, k == KD - 1)
                last.then_inc(proj_done, 1)

            def queries_keys(p):
                pe.wait_ge(w_low, p + 1)
                for i in range(4):
                    project(first_job(p) + i, i // 2, i % 2)

            def gates(p):
                for n in range(2):
                    project(first_job(p) + 4 + n, 2, n)

            def values(g):
                pe.wait_ge(wv_low, g + 1)
                for t in range(TT):
                    j = first_job(GP * g) + 6 + t
                    pe.wait_ge(proj_moved, j - 1)
                    for k in range(KD):
                        last = product_of_parts(nc, c.ps[:, j % 2, :], [x[:, k, t * P:(t + 1) * P] for x in x_parts],
                                                [w[:, k, :] for w in wv_parts], k == 0, k == KD - 1)
                    last.then_inc(proj_done, 1)

            def products(p):
                pe.wait_ge(proj_moved, first_job(p) + 4)
                for i in range(4):
                    b, hh = i // 2, i % 2
                    j, rows = a_jobs(p) + i, slice(hh * D, (hh + 1) * D)
                    if j >= 2:
                        pe.wait_ge(a_moved, j - 1)
                    for ch in range(CH):
                        tok = slice((b * CH + ch) * P, (b * CH + ch + 1) * P)
                        last = nc.tensor.matmul(c.ps[:, 2 + j % 2, ch * P:(ch + 1) * P], kF[rows, tok], qF[rows, tok],
                                                start=True, stop=True)
                    last.then_inc(a_done, 1)

            def turn_keys(p):
                for b in range(2):
                    if p >= 1:
                        pe.wait_ge(s_ready, 3 * p)
                    for ch in range(CH):
                        t = b * CH + ch
                        last = nc.tensor.transpose(c.ps[:, 4 + b, ch * P:(ch + 1) * P], kF[:, t * P:(t + 1) * P], c.ident[:])
                    last.then_inc(t_done, 1)

            def updates(p):
                pe.wait_ge(t_moved, 2 * (p + 1))
                if p % GP == 0:
                    pe.wait_ge(proj_moved, first_job(p) + 6 + TT)
                for b in range(2):
                    for ch in range(CH - 1):
                        t = b * CH + ch
                        last = nc.tensor.matmul(c.ps[:, 4 + b, ch * P:(ch + 1) * P], kT[:, t, :],
                                                v[:, t, p % GP * P:(p % GP + 1) * P], start=True, stop=True)
                last.then_inc(u_done, 1)

            def outputs(p):
                pe.wait_ge(s_ready, 3 * (p + 1))
                pe.wait_ge(qd_done, 2 * (p + 1))
                pe.wait_ge(a_moved, a_jobs(p) + 4)
                for b in range(2):
                    if p >= 1:
                        pe.wait_ge(ga_done, 2 * (p - 1) + b + 1)
                    for ch in range(CH):
                        t = b * CH + ch
                        col = slice(ch * P, (ch + 1) * P)
                        if ch > 0:
                            nc.tensor.matmul(c.ps[:, 6 + b, col], S[:, ch - 1, b, :], qD[:, t * P:(t + 1) * P],
                                             start=True, stop=False, skip_group_check=True)
                        for hh in range(2):
                            h = p % GP * 2 + hh
                            last = nc.tensor.matmul(c.ps[hh * D:(hh + 1) * D, 6 + b, col], v[:, t, h * D:(h + 1) * D],
                                                    A[:, b, hh, ch, :], start=ch == 0, stop=True, skip_group_check=True)
                    last.then_inc(o_done, 1)

            def sum_outputs(g):
                pe.wait_ge(ga_done, 2 * GP * (g + 1))
                pe.wait_ge(in_o, 16 * (g + 1))
                for t in range(TT):
                    j = a_jobs(GP * (g + 1)) - TT + t
                    pe.wait_ge(a_moved, j - 1)
                    for k in range(GP):
                        last = nc.tensor.matmul(c.ps[:, 2 + j % 2, :], ga[:, (g * GP + k) % GA, t * P:(t + 1) * P], wo[:, k, :],
                                                start=k == 0, stop=k == GP - 1)
                    last.then_inc(a_done, 1)

            queries_keys(0)
            gates(0)
            values(0)
            for p in range(PAIRS):
                products(p)
                turn_keys(p)
                if p + 1 < PAIRS:
                    queries_keys(p + 1)
                updates(p)
                if p + 1 < PAIRS:
                    gates(p + 1)
                outputs(p)
                if p + 1 < PAIRS and (p + 1) % GP == 0:
                    values((p + 1) // GP)
                if p % GP == GP - 1:
                    sum_outputs(p // GP)

        @block.scalar
        def _(act):
            def pair(p):
                j = first_job(p)
                for i in range(6):
                    act.wait_ge(proj_done, j + i + 1)
                    tok = slice(i % 2 * BANK, (i % 2 + 1) * BANK)
                    src = c.ps[:, (j + i) % 2, :]
                    if i == 0 and p >= 1:
                        act.wait_ge(a_done, a_jobs(p - 1) + 4)
                        act.wait_ge(qd_done, 2 * p)
                    if i == 2 and p >= 1:
                        act.wait_ge(t_done, 2 * p)
                    if i == 4 and p >= GA:
                        act.wait_ge(a_done, a_jobs(GP * ((p - GA) // GP + 1)))
                    if i < 4:
                        dst = (qF, kF)[i // 2][:, tok]
                        nc.scalar.activation(dst, src, ACT.Silu).then_inc(proj_moved, 1)
                    else:
                        nc.scalar.activation(ga[:, p % GA, tok], src, ACT.Sigmoid).then_inc(proj_moved, 1)

            def values(g):
                j = first_job(GP * g) + 6
                if g >= 1:
                    act.wait_ge(o_done, 2 * GP * g)
                for t in range(TT):
                    act.wait_ge(proj_done, j + t + 1)
                    nc.scalar.activation(v[:, t, :], c.ps[:, (j + t) % 2, :], ACT.Silu).then_inc(proj_moved, 1)

            def squares(p):
                for b in range(2):
                    act.wait_ge(o_done, 2 * p + b + 1)
                    if p >= 1:
                        act.wait_ge(sqsum_done, 2 * (p - 1) + b + 1)
                    nc.scalar.activation(sq[:, b, :], c.ps[:, 6 + b, :], ACT.Square).then_inc(sq_done, 1)

            def high_weights(p):
                act.wait_ge(in_p, 48 * (p + 1))
                if p >= 1:
                    act.wait_ge(w_low, p)
                nc.scalar.activation(w3_parts[0][:], w3[:], ACT.Copy).then_inc(w_high, 1)

            def high_values(g):
                act.wait_ge(in_v, 16 * (g + 1))
                if g >= 1:
                    act.wait_ge(wv_low, g)
                nc.scalar.activation(wv_parts[0][:], wv[:], ACT.Copy).then_inc(wv_high, 1)

            high_weights(0)
            high_values(0)
            pair(0)
            high_weights(1)
            values(0)
            for p in range(PAIRS):
                if p + 1 < PAIRS:
                    pair(p + 1)
                if p + 2 < PAIRS:
                    high_weights(p + 2)
                squares(p)
                if p % GP == GP - 2 and p + 2 < PAIRS:
                    high_values(p // GP + 1)
                if p + 1 < PAIRS and (p + 1) % GP == 0:
                    values((p + 1) // GP)

        @block.gpsimd
        def _(pool):
            nc.gpsimd.memset(sqsum[:], 0.0).then_inc(zeroed, 1)
            pool.wait_ge(zeroed, 1)
            for p in range(PAIRS):
                g = p // GP
                if p % GP == 0:
                    pool.wait_ge(in_g[g % 2], 32 * (g // 2 + 1))
                if p >= 1:
                    pool.wait_ge(o_done, 2 * p)
                for n in range(2):
                    pool.wait_ge(proj_moved, first_job(p) + n + 1)
                    tok = slice(n * BANK, (n + 1) * BANK)
                    nc.gpsimd.tensor_tensor(qD[:, tok].rearrange("p (c i) -> p c i", i=P),
                                            qF[:, tok].rearrange("p (c i) -> p c i", i=P),
                                            qdec[:, g % 2, p % GP, :].unsqueeze(1).to_broadcast([P, CH, P]),
                                            ALU.mult).then_inc(qd_done, 1)
                for b in range(2):
                    pool.wait_ge(sq_done, 2 * p + b + 1)
                    if p >= 1:
                        pool.wait_ge(sqsum_done, 2 * (p - 1) + b + 1)
                    tok = slice(b * BANK, (b + 1) * BANK)
                    nc.gpsimd.tensor_tensor(sqsum[:, tok], sqsum[:, tok], sq[:, b, :], ALU.add).then_inc(sqsum_done, 1)

        @block.vector
        def _(dve):
            nc.vector.memset(S[:], 0.0).then_inc(step, 1)
            nc.vector.memset(ones[:], 1.0)
            dve.wait_ge(step, 1)
            dve.wait_ge(in_c, 48)
            steps = [1]

            def mask_products(p):
                g = p // GP
                if p % GP == 0:
                    dve.wait_ge(in_g[g % 2], 32 * (g // 2 + 1))
                for i in range(4):
                    b, hh = i // 2, i % 2
                    j, h = a_jobs(p) + i, p % GP * 2 + hh
                    dve.wait_ge(a_done, j + 1)
                    if p >= 1:
                        dve.wait_ge(o_done, 2 * (p - 1) + b + 1)
                    nc.vector.tensor_tensor(A[:, b, hh, :, :], c.ps[:, 2 + j % 2, :].rearrange("p (c i) -> p c i", i=P),
                                            mask[:, g % 2, h, :].unsqueeze(1).to_broadcast([P, CH, P]),
                                            ALU.mult).then_inc(a_moved, 1)

            def decay_keys(p):
                if p >= 1:
                    dve.wait_ge(u_done, p)
                for b in range(2):
                    dve.wait_ge(t_done, 2 * p + b + 1)
                    nc.vector.tensor_tensor(kT[:, b * CH:(b + 1) * CH, :].rearrange("p c (h d) -> p c h d", h=2),
                                            c.ps[:, 4 + b, :].rearrange("p (c h d) -> p c h d", c=CH, h=2),
                                            kdec[:, 2 * p:2 * p + 2].unsqueeze(1).unsqueeze(3).to_broadcast([P, CH, 2, D]),
                                            ALU.mult).then_inc(t_moved, 1)

            def states(p):
                dve.wait_ge(u_done, p + 1)
                if p >= 1:
                    dve.wait_ge(o_done, 2 * p)
                for ch in range(CH - 1):
                    for hh in range(2):
                        rows, cols = slice(hh * D, (hh + 1) * D), slice(hh * D, (hh + 1) * D)
                        new = c.ps[rows, 4:6, ch * P + hh * D:ch * P + (hh + 1) * D]
                        if ch == 0:
                            last = nc.vector.tensor_copy(S[rows, 0, :, cols], new)
                        else:
                            last = nc.vector.scalar_tensor_tensor(S[rows, ch, :, cols], S[rows, ch - 1, :, cols],
                                                                  bdec[rows, p:p + 1], new, ALU.mult, ALU.add)
                        if hh == 0:
                            last.then_inc(step, 1)
                            steps[0] += 1
                    last.then_inc(s_ready, 1)
                    dve.wait_ge(step, steps[0])
                    dve.wait_ge(s_ready, 3 * p + ch + 1)

            def gate(p):
                for b in range(2):
                    tok = slice(b * BANK, (b + 1) * BANK)
                    dve.wait_ge(sq_done, 2 * p + b + 1)
                    nc.vector.scalar_tensor_tensor(ga[:, p % GA, tok], c.ps[:, 6 + b, :], nw[:, p:p + 1],
                                                   ga[:, p % GA, tok], ALU.mult, ALU.mult).then_inc(ga_done, 1)

            def add_outputs(g):
                for t in range(TT):
                    j = a_jobs(GP * (g + 1)) - TT + t
                    dve.wait_ge(a_done, j + 1)
                    if g == 0:
                        nc.vector.tensor_copy(y[:, t, :], c.ps[:, 2 + j % 2, :]).then_inc(a_moved, 1)
                    else:
                        nc.vector.tensor_tensor(y[:, t, :], c.ps[:, 2 + j % 2, :], y[:, t, :], ALU.add).then_inc(a_moved, 1)

            def low_weights(p):
                dve.wait_ge(w_high, p + 1)
                nc.vector.tensor_tensor(w3_parts[1][:], w3[:], w3_parts[0][:].bitcast(F32), ALU.subtract).then_inc(w_low, 1)

            def low_values(g):
                dve.wait_ge(wv_high, g + 1)
                nc.vector.tensor_tensor(wv_parts[1][:], wv[:], wv_parts[0][:].bitcast(F32), ALU.subtract).then_inc(wv_low, 1)

            low_weights(0)
            low_values(0)
            low_weights(1)
            for p in range(PAIRS):
                mask_products(p)
                decay_keys(p)
                states(p)
                if p + 2 < PAIRS:
                    low_weights(p + 2)
                if p % GP == GP - 1 and p + 1 < PAIRS:
                    low_values(p // GP + 1)
                gate(p)
                if p % GP == GP - 1:
                    add_outputs(p // GP)

    sum_done, ms_done, rs_done = c.sem("d_sum_done"), c.sem("d_ms_done"), c.sem("d_rs_done")
    with nc.Block() as block:
        @block.tensor
        def _(pe):
            for t in range(TT):
                last = nc.tensor.matmul(c.ps[:, 0, t:t + 1], sqsum[:, t * P:(t + 1) * P], ones[:], start=True, stop=True)
            last.then_inc(sum_done, 1)

        @block.vector
        def _(dve):
            dve.wait_ge(sum_done, 1)
            nc.vector.tensor_scalar(c.var_eps[:], c.ps[:, 0, 0:TT], 1.0 / F, 1e-5, ALU.mult, ALU.add).then_inc(ms_done, 1)
            dve.wait_ge(rs_done, 1)
            for t in range(TT):
                nc.vector.scalar_tensor_tensor(c.x[:, t, :], y[:, t, :], ms[:, t:t + 1], c.x[:, t, :], ALU.mult, ALU.add)

        @block.gpsimd
        def _(pool):
            pool.wait_ge(ms_done, 1)
            nc.gpsimd.tensor_tensor(ms[:], c.var_eps[:], c.neg_half[:], ALU.pow).then_inc(rs_done, 1)



def gated_cross_attention(c):
    nc = c.nc
    H = 16
    ST = CTX // P
    W = P + 1
    CHUNK = 2 * P
    NC, TILES = CTX // CHUNK, CHUNK // P
    wkT = c.at("e_wkT", [P, KD, DM], F32, 52)
    wvT = c.at("e_wvT", [P, KD, DM], F32, 60)
    wk_parts = [c.at("e_wk_high", [P, KD, DM], F32R, 149), c.at("e_wk_low", [P, KD, DM], F32R, 157)]
    wv_parts = [c.at("e_wv_high", [P, KD, DM], F32R, 24), c.at("e_wv_low", [P, KD, DM], F32R, 193)]
    ctxT = c.at("e_ctxT", [P, 2, KD, CHUNK], F32, 68)
    ctx_parts = [c.at("e_ctx_high", [P, 2, KD, CHUNK], F32R, 76), c.at("e_ctx_low", [P, 2, KD, CHUNK], F32R, 16)]
    qF = c.at("e_qF", [P, KD, TOK], F32, 52)
    gF = c.at("e_gF", [P, KD, TOK], F32, 68)
    kf = c.at("e_kf", [P, ST, DM], F32, 84)
    v = c.at("e_v", [P, ST, KD, W], F32, 116)
    wqT = c.at("e_wqT", [P, KD, DM], F32, 165)
    wgT = c.at("e_wgT", [P, KD, DM], F32, 173)
    woT = c.at("e_woT", [P, KD, DM], F32, 181)
    ex = c.at("e_ex", [P, 2, BANK], F32, 189)
    kv = c.at("e_kv", [P, 2, KD, P], F32, 193)
    gz = c.at("e_gz", [P, 2, BANK], F32, 197)
    z = c.at("e_z", [H, TOK], F32, 201)
    ksum = c.at("e_ksum", [P, 2, KD, H], F32, 205)
    blocks = c.at("e_blocks", [P, P], F32, 205.5)
    heads = c.at("e_heads", [P, KD, H], F32, 206)
    headsT = c.at("e_headsT", [H, KD, P], F32, 46)
    bg = c.at("e_bg", [P, KD], F32, 50.5)
    ahead = c.at("e_ahead", [P, 2, KD * DM], F32, 149)
    UNIT = 2 * DM
    aux = c.at("e_aux", [P, UNIT], F32, 32)
    scale = c.at("e_scale", [P, 4, UNIT // MX], F32, 51)
    inv = c.at("e_inv", [P, UNIT // MX], F32, 51.5)
    in_ahead = [c.sem(f"e_in_ahead{j}") for j in range(2)]
    step, rounded, quantised = c.sem("e_step"), c.sem("e_rounded"), c.sem("e_quantised")

    in_k, in_v, in_w, in_b, in_h = (c.sem(f"e_{n}") for n in ("in_k", "in_v", "in_w", "in_b", "in_h"))
    in_ctx = [c.sem(f"e_in_ctx{slot}") for slot in range(2)]
    w_high, w_low, ctx_high, ctx_low = (c.sem(f"e_{n}") for n in ("w_high", "w_low", "ctx_high", "ctx_low"))

    k_done, k_exp, k_min, k_ready = (c.sem(f"e_{n}") for n in ("k_done", "k_exp", "k_min", "k_ready"))
    v_done, v_ready = c.sem("e_v_done"), c.sem("e_v_ready")
    normed, aggr_done, rstd_done = c.sem("e_normed"), c.sem("e_aggr_done"), c.sem("e_rstd_done")
    with nc.Block() as block:
        @block.sync
        def _(sp):
            def context(n):
                if n >= 2:
                    sp.wait_ge(ctx_low, n - 1)
                sp.dma_start(ctxT[:, n % 2], tiled(c.dram["ctxT"])[:, :, n * CHUNK:(n + 1) * CHUNK]).then_inc(in_ctx[n % 2], 16)

            sp.dma_start(wkT[:], tiled(c.dram["e_wkT"])).then_inc(in_k, 16)
            context(0)
            sp.dma_start(wvT[:], tiled(c.dram["e_wvT"])).then_inc(in_v, 16)
            context(1)
            sp.dma_start(bg[:], c.dram["e_bg"]).then_inc(in_b, 16)
            sp.dma_start(blocks[:], c.dram["e_blocks"]).then_inc(in_b, 16)
            sp.dma_start(heads[:], c.dram["e_heads"]).then_inc(in_b, 16)
            for n in range(2, NC):
                context(n)
            for w, name in ((wqT, "e_wqT"), (wgT, "e_wgT"), (woT, "e_woT")):
                sp.dma_start(w[:], tiled(c.dram[name])).then_inc(in_w, 16)

        @block.tensor
        def _(pe):
            for j in range(ST):
                pe.wait_ge(ctx_low, j // TILES + 1)
                for i, bank, parts, freed, done in ((1, j % 4, wk_parts, k_ready, k_done), (2, 4 + j % 4, wv_parts, v_ready, v_done)):
                    pe.wait_ge(w_low, i)
                    if j >= 4:
                        pe.wait_ge(freed, j - 3)
                    for k in range(KD):
                        rows = [x[:, j // TILES % 2, k, j % TILES * P:(j % TILES + 1) * P] for x in ctx_parts]
                        last = product_of_parts(nc, c.ps[:, bank, :], rows, [w[:, k, :] for w in parts], k == 0, k == KD - 1)
                    last.then_inc(done, 1)

        @block.scalar
        def _(act):
            def high_context(n):
                act.wait_ge(in_ctx[n % 2], 16 * (n // 2 + 1))
                if n >= 2:
                    act.wait_ge(v_done, (n - 1) * TILES)
                nc.scalar.activation(ctx_parts[0][:, n % 2], ctxT[:, n % 2], ACT.Copy).then_inc(ctx_high, 1)

            act.wait_ge(in_k, 16)
            nc.scalar.activation(wk_parts[0][:], wkT[:], ACT.Copy).then_inc(w_high, 1)
            high_context(0)
            act.wait_ge(in_v, 16)
            nc.scalar.activation(wv_parts[0][:], wvT[:], ACT.Copy).then_inc(w_high, 1)
            high_context(1)
            for j in range(ST):
                act.wait_ge(k_done, j + 1)
                if j >= 2:
                    act.wait_ge(k_ready, j - 1)
                nc.scalar.activation(ex[:, j % 2, :], c.ps[:, j % 4, :], ACT.Relu, scale=-1.0).then_inc(k_min, 1)
                act.wait_ge(k_min, j + 1)
                nc.scalar.activation(ex[:, j % 2, :], ex[:, j % 2, :], ACT.Exp, scale=-1.0).then_inc(k_exp, 1)
                act.wait_ge(v_done, j + 1)
                if j % TILES == TILES - 1 and j // TILES + 2 < NC:
                    high_context(j // TILES + 2)
                nc.scalar.activation(v[:, j, :, 0:P], c.ps[:, 4 + j % 4, :].rearrange("p (k d) -> p k d", k=KD),
                                     ACT.Copy).then_inc(v_ready, 1)

        @block.gpsimd
        def _(pool):
            nc.gpsimd.memset(v[:, :, :, P:W], 1.0)
            rstd_pool(c, aggr_done, rstd_done)

        @block.vector
        def _(dve):
            def low_weights(i, raw, parts):
                dve.wait_ge(w_high, i + 1)
                nc.vector.tensor_tensor(parts[1][:], raw[:], parts[0][:].bitcast(F32), ALU.subtract).then_inc(w_low, 1)

            def low_context(n):
                dve.wait_ge(ctx_high, n + 1)
                nc.vector.tensor_tensor(ctx_parts[1][:, n % 2], ctxT[:, n % 2], ctx_parts[0][:, n % 2].bitcast(F32),
                                        ALU.subtract).then_inc(ctx_low, 1)

            low_weights(0, wkT, wk_parts)
            low_context(0)
            low_weights(1, wvT, wv_parts)
            low_context(1)
            layernorm_dve(c, "e", aggr_done, rstd_done, normed)
            for j in range(ST):
                if j >= TILES and j % TILES == 0 and j // TILES + 1 < NC:
                    low_context(j // TILES + 1)
                dve.wait_ge(k_exp, j + 1)
                nc.vector.scalar_tensor_tensor(kf[:, j, :], c.ps[:, j % 4, :], 0.0, ex[:, j % 2, :],
                                               ALU.max, ALU.add).then_inc(k_ready, 1)

    turn_normed(c, "e")

    kv_done = c.sem("e_kv_done")
    q_done, q_exp, q_min, q_ready = (c.sem(f"e_{n}") for n in ("q_done", "q_exp", "q_min", "q_ready"))
    g_done, g_ready = c.sem("e_g_done"), c.sem("e_g_ready")
    JOBS = [(n, m) for n in range(2) for m in range(KD)]
    with nc.Block() as block:
        @block.sync
        def _(sp):
            for j, name in enumerate(("f_g", "f_u")):
                sp.dma_start(ahead[:, j, :].rearrange("p (m n) -> p m n", m=KD),
                             tiled(c.dram[name][0:BANK, :])).then_inc(in_ahead[j], 16)
            sp.dma_start(headsT[:], c.dram["e_headsT"]).then_inc(in_h, 16)
            sp.wait_ge(in_h, 16)

        @block.tensor
        def _(pe):
            for b in range(2):
                for m in range(KD):
                    for s in range(ST // 2):
                        t = b * ST // 2 + s
                        last = nc.tensor.matmul(c.ps[:, 2 * b + m // 2, m % 2 * W:(m % 2 + 1) * W],
                                                kf[:, t, m * P:(m + 1) * P], v[:, t, m, :],
                                                start=s == 0, stop=s == ST // 2 - 1)
                last.then_inc(kv_done, 1)
            pe.wait_ge(in_w, 48)
            for j, (n, m) in enumerate(JOBS):
                if j >= 2:
                    pe.wait_ge(q_ready, j - 1)
                for k in range(KD):
                    last = nc.tensor.matmul(c.ps[:, 4 + j % 2, :], wqT[:, k, m * P:(m + 1) * P],
                                            c.xF[:, k, n * BANK:(n + 1) * BANK], start=k == 0, stop=k == KD - 1)
                last.then_inc(q_done, 1)
            for j, (n, m) in enumerate(JOBS):
                if j >= 2:
                    pe.wait_ge(g_ready, j - 1)
                for k in range(KD):
                    last = nc.tensor.matmul(c.ps[:, 6 + j % 2, :], wgT[:, k, m * P:(m + 1) * P],
                                            c.xF[:, k, n * BANK:(n + 1) * BANK], start=k == 0, stop=k == KD - 1)
                last.then_inc(g_done, 1)

        @block.scalar
        def _(act):
            for j, (n, m) in enumerate(JOBS):
                act.wait_ge(q_done, j + 1)
                if j >= 2:
                    act.wait_ge(q_ready, j - 1)
                nc.scalar.activation(ex[:, j % 2, :], c.ps[:, 4 + j % 2, :], ACT.Relu, scale=-1.0).then_inc(q_min, 1)
                act.wait_ge(q_min, j + 1)
                nc.scalar.activation(ex[:, j % 2, :], ex[:, j % 2, :], ACT.Exp, scale=-1.0).then_inc(q_exp, 1)
            act.wait_ge(in_b, 48)
            for j, (n, m) in enumerate(JOBS):
                act.wait_ge(g_done, j + 1)
                nc.scalar.activation(gF[:, m, n * BANK:(n + 1) * BANK], c.ps[:, 6 + j % 2, :], ACT.Sigmoid,
                                     bias=bg[:, m:m + 1]).then_inc(g_ready, 1)

        @block.vector
        def _(dve):
            dve.wait_ge(in_b, 48)
            for b in range(2):
                dve.wait_ge(kv_done, b + 1)
                for m in range(KD):
                    col = m % 2 * W
                    nc.vector.tensor_tensor(kv[:, b, m, :], c.ps[:, 2 * b + m // 2, col:col + P], blocks[:], ALU.mult)
                    nc.vector.tensor_scalar(ksum[:, b, m, :], heads[:, m, :], c.ps[:, 2 * b + m // 2, col + P:col + W],
                                            None, ALU.mult)
            for j, (n, m) in enumerate(JOBS):
                dve.wait_ge(q_exp, j + 1)
                nc.vector.scalar_tensor_tensor(qF[:, m, n * BANK:(n + 1) * BANK], c.ps[:, 4 + j % 2, :], 0.0, ex[:, j % 2, :],
                                               ALU.max, ALU.add).then_inc(q_ready, 1)
            done = [0]
            for i in range(4):
                dve.wait_ge(in_ahead[i // 2], 16)
                if i >= 1:
                    dve.wait_ge(rounded, 2 * i)
                mx_round(c, step, done, rounded, ahead[:, i // 2, i % 2 * UNIT:(i % 2 + 1) * UNIT], aux[:], scale[:, i, :], inv[:])

        @block.gpsimd
        def _(pool):
            for i in range(4):
                pool.wait_ge(rounded, 2 * (i + 1))
                mx_scale(c, ahead[:, i // 2, i % 2 * UNIT:(i % 2 + 1) * UNIT], scale[:, i, :]).then_inc(quantised, 1)

    den_done, z_step, zb_done, gz_done, num_done, ag_done = (
        c.sem(f"e_{n}") for n in ("den_done", "z_step", "zb_done", "gz_done", "num_done", "ag_done"))
    out_done, added = c.sem("e_out_done"), c.sem("e_added")
    with nc.Block() as block:
        @block.tensor
        def _(pe):
            for b in range(2):
                for m in range(KD):
                    last = nc.tensor.matmul(c.ps[0:H, b, :], ksum[:, b, m, :], qF[:, m, b * BANK:(b + 1) * BANK],
                                            start=m == 0, stop=m == KD - 1)
                last.then_inc(den_done, 1)
            for j, (b, m) in enumerate(JOBS):
                if j >= 2:
                    pe.wait_ge(ag_done, j - 1)
                nc.tensor.matmul(c.ps[:, 4 + j % 2, :], kv[:, b, m, :], qF[:, m, b * BANK:(b + 1) * BANK],
                                 start=True, stop=True).then_inc(num_done, 1)
                pe.wait_ge(z_step, 2 * (b + 1))
                nc.tensor.matmul(c.ps[:, 2 + j % 2, :], headsT[:, m, :], z[:, b * BANK:(b + 1) * BANK],
                                 start=True, stop=True).then_inc(zb_done, 1)
            for t in range(TT):
                pe.wait_ge(ag_done, KD * (1 + t // 4))
                if t >= 2:
                    pe.wait_ge(added, t - 1)
                for k in range(KD):
                    last = nc.tensor.matmul(c.ps[:, 6 + t % 2, :], gF[:, k, t * P:(t + 1) * P], woT[:, k, :],
                                            start=k == 0, stop=k == KD - 1)
                last.then_inc(out_done, 1)

        @block.vector
        def _(dve):
            for b in range(2):
                dve.wait_ge(den_done, b + 1)
                nc.vector.tensor_scalar(z[:, b * BANK:(b + 1) * BANK], c.ps[0:H, b, :], 1e-6, None, ALU.add).then_inc(z_step, 1)
                dve.wait_ge(z_step, 2 * b + 1)
                nc.vector.reciprocal(z[:, b * BANK:(b + 1) * BANK], z[:, b * BANK:(b + 1) * BANK]).then_inc(z_step, 1)
            for j, (b, m) in enumerate(JOBS):
                tok = slice(b * BANK, (b + 1) * BANK)
                dve.wait_ge(zb_done, j + 1)
                nc.vector.tensor_tensor(gz[:, j % 2, :], c.ps[:, 2 + j % 2, :], gF[:, m, tok], ALU.mult).then_inc(gz_done, 1)
                dve.wait_ge(gz_done, j + 1)
                nc.vector.tensor_tensor(gF[:, m, tok], c.ps[:, 4 + j % 2, :], gz[:, j % 2, :], ALU.mult).then_inc(ag_done, 1)
            for t in range(TT):
                dve.wait_ge(out_done, t + 1)
                nc.vector.tensor_tensor(c.x[:, t, :], c.ps[:, 6 + t % 2, :], c.x[:, t, :], ALU.add).then_inc(added, 1)



MX = 32
FP8_ROUND = 1.5 * 2.0 ** 20
FP8_SMALL = 2.0 ** -6


def mx_round(c, step, done, rounded, src, aux, scale, inv):
    dve = vector = c.nc.vector
    half = src.shape[-1] // 2

    def halves(ap):
        n = ap.shape[-1] // 2
        return [ap[:, 0:n], ap[:, n:2 * n]]

    srcs, auxs, scales, invs = halves(src), halves(aux), halves(scale), halves(inv)
    blocks = [part.rearrange("p (b m) -> p b m", m=MX) for part in srcs]
    wide = [P, half // MX, MX]
    first = done[0]

    def ready():
        if done[0] >= first + 2:
            dve.wait_ge(step, done[0] - 1)
        done[0] += 1

    for i in range(2):
        ready()
        vector.tensor_reduce(scales[i], blocks[i], AX.X, ALU.max, apply_absolute_value=True).then_inc(step, 1)
    for i in range(2):
        ready()
        vector.tensor_scalar(scales[i], scales[i], 1.0 / 448.0, 1e-30, ALU.mult, ALU.max).then_inc(step, 1)
    for i in range(2):
        ready()
        vector.reciprocal(invs[i], scales[i]).then_inc(step, 1)
    for i in range(2):
        ready()
        vector.tensor_tensor(blocks[i], blocks[i], invs[i].unsqueeze(2).to_broadcast(wide), ALU.mult).then_inc(step, 1)
    for i in range(2):
        ready()
        vector.tensor_scalar(auxs[i].bitcast(U32), srcs[i].bitcast(U32), 0x7F800000, None, ALU.bitwise_and).then_inc(step, 1)
    for i in range(2):
        ready()
        vector.tensor_scalar(auxs[i], auxs[i], FP8_SMALL, FP8_ROUND, ALU.max, ALU.mult).then_inc(step, 1)
    for i in range(2):
        ready()
        vector.tensor_tensor(srcs[i], srcs[i], auxs[i], ALU.add).then_inc(step, 1)
    for i in range(2):
        dve.wait_ge(step, done[0] - 1 + i)
        vector.tensor_tensor(srcs[i], srcs[i], auxs[i], ALU.subtract).then_inc(rounded, 1)


def mx_scale(c, src, scale):
    blocks = src.rearrange("p (b m) -> p b m", m=MX)
    return c.nc.gpsimd.tensor_tensor(blocks, blocks, scale.unsqueeze(2).to_broadcast(list(blocks.shape)), ALU.mult)


def mx_feed_forward(c):
    nc = c.nc
    INTER = 2048
    NCH, UNIT = INTER // BANK, 2 * DM
    gT = c.at("f_gT", [P, 2, KD, BANK], F32, 52)
    uT = c.at("f_uT", [P, 2, KD, BANK], F32, 68)
    dT = c.at("f_dT", [P, 2, KD, DM], F32, 84)
    w = c.at("f_w", [P, 4, KD * DM], F32, 133)
    h = c.at("f_h", [P, 2, TT * BANK], F32, 100)
    hF = c.at("f_hF", [P, 2, KD, P], F32, 165)
    silu = c.at("f_silu", [P, 2, BANK], F32, 169)
    aux = c.at("f_aux", [P, UNIT], F32, 173)
    scale = c.at("f_scale", [P, 4, UNIT // MX], F32, 177)
    inv = c.at("f_inv", [P, UNIT // MX], F32, 177.5)
    xn = c.xn[:].rearrange("p t n -> p (t n)")
    AHEAD = 2

    def w_slot(j):
        return (j + 4 - AHEAD) % 4

    WJOBS = [(name, wT, n) for n in range(NCH) for name, wT in (("f_g", gT), ("f_u", uT), ("f_d", dT))]

    PE_PLAN = [("w", j, r) for j in range(2) for r in range(4)] + [("x", 0), ("x", 1)]
    DVE_PLAN = [("x", 0), ("x", 1)]
    for n in range(NCH):
        next_w = {0: (3 * n + 2, 0), 1: (3 * n + 2, 1)}
        if n + 1 < NCH:
            next_w.update({2: (3 * n + 3, 0), 3: (3 * n + 3, 1), 4: (3 * n + 4, 0), 5: (3 * n + 4, 1)})
        for t in range(TT):
            if n >= 1:
                PE_PLAN.append(("h", n - 1, t))
            if n == 0 and t >= 2 and t % 2 == 0:
                PE_PLAN += [("x", t), ("x", t + 1)]
            PE_PLAN.append(("up", n, t))
            if t - 1 in next_w:
                j, half = next_w[t - 1]
                PE_PLAN += [("w", j, 2 * half), ("w", j, 2 * half + 1)]
            DVE_PLAN.append(("mult", n, t))
            if n == 0 and t < 2:
                DVE_PLAN.append(("x", t + 2))
            if t in next_w:
                DVE_PLAN.append(("w",) + next_w[t])
            if t % 2 == 1:
                DVE_PLAN.append(("h", n, t // 2))
            if n >= 1:
                PE_PLAN.append(("down", n - 1, t))
                DVE_PLAN.append(("add", n - 1, t))
    for t in range(TT):
        PE_PLAN += ([("h", NCH - 1, 0)] if t == 0 else []) + ([("h", NCH - 1, t + 1)] if t + 1 < TT else [])
        PE_PLAN.append(("down", NCH - 1, t))
        DVE_PLAN.append(("add", NCH - 1, t))
    TURNS = [e for e in PE_PLAN if e[0] in "wxh"]
    UNITS = [e for e in DVE_PLAN if e[0] in "wxh"]

    in_w = [c.sem(f"f_in_w{i}") for i in range(4)]
    step, rounded, quantised = c.sem("f_step"), c.sem("f_rounded"), c.sem("f_quantised")
    turned, moved = c.sem("f_turned"), c.sem("f_moved")
    normed, aggr_done, rstd_done = c.sem("f_normed"), c.sem("f_aggr_done"), c.sem("f_rstd_done")
    g_done, u_done, silu_done, h_done, out_done, added = (c.sem(f"f_{n}") for n in (
        "g_done", "u_done", "silu_done", "h_done", "out_done", "added"))

    def unit_rows(e):
        if e[0] == "w":
            return w[:, w_slot(e[1]), e[2] * UNIT:(e[2] + 1) * UNIT]
        if e[0] == "x":
            return xn[:, e[1] * UNIT:(e[1] + 1) * UNIT]
        return h[:, e[1] % 2, e[2] * UNIT:(e[2] + 1) * UNIT]

    def turn_rows(e):
        if e[0] == "w":
            _, j, r = e
            return w[:, w_slot(j), r * DM:(r + 1) * DM], WJOBS[j][1][:, WJOBS[j][2] % 2, :, r * P:(r + 1) * P], ("w", j, r // 2)
        if e[0] == "x":
            t = e[1]
            return c.xn[:, t, :], c.xF[:, :, t * P:(t + 1) * P], ("x", t // 2)
        _, n, t = e
        return h[:, n % 2, t * BANK:(t + 1) * BANK], hF[:, (n * TT + t) % 2, :, :], ("h", n, t // 2)

    with nc.Block() as block:
        @block.sync
        def _(sp):
            for j, (name, _, n) in enumerate(WJOBS):
                if j < AHEAD:
                    continue
                if j >= 4:
                    sp.wait_ge(turned, TURNS.index(("w", j - 4, 3)) + 1)
                rows = tiled(c.dram[name])[:, :, n * BANK:(n + 1) * BANK] if name == "f_d" else tiled(c.dram[name][n * BANK:(n + 1) * BANK, :])
                sp.dma_start(w[:, w_slot(j), :].rearrange("p (m n) -> p m n", m=4), rows).then_inc(in_w[w_slot(j)], 16)

        @block.gpsimd
        def _(pool):
            rstd_pool(c, aggr_done, rstd_done)
            for i, e in enumerate(UNITS):
                pool.wait_ge(rounded, 2 * (i + 1))
                mx_scale(c, unit_rows(e), scale[:, i % 4, :]).then_inc(quantised, 1)

        @block.vector
        def _(dve):
            layernorm_dve(c, "f", aggr_done, rstd_done, normed)
            dve.wait_ge(normed, TT)
            done, i = [0], 0
            for e in DVE_PLAN:
                if e[0] in "wxh":
                    if e[0] == "w":
                        dve.wait_ge(in_w[w_slot(e[1])], 16 * ((e[1] - AHEAD) // 4 + 1))
                    elif e[0] == "h":
                        dve.wait_ge(h_done, TT * e[1] + 2 * e[2] + 2)
                    if i >= 1:
                        dve.wait_ge(rounded, 2 * i)
                    if i >= 4:
                        dve.wait_ge(quantised, i - 3)
                    mx_round(c, step, done, rounded, unit_rows(e), aux[:], scale[:, i % 4, :], inv[:])
                    i += 1
                elif e[0] == "mult":
                    _, n, t = e
                    j = TT * n + t
                    dve.wait_ge(silu_done, j + 1)
                    dve.wait_ge(u_done, j + 1)
                    if n >= 2:
                        dve.wait_ge(turned, TURNS.index(("h", n - 2, t)) + 1)
                    nc.vector.tensor_tensor(h[:, n % 2, t * BANK:(t + 1) * BANK], c.ps[:, 4 + j % 2, :], silu[:, j % 2, :],
                                            ALU.mult).then_inc(h_done, 1)
                else:
                    _, n, t = e
                    j = TT * n + t
                    dve.wait_ge(out_done, j + 1)
                    if n >= 1:
                        dve.wait_ge(added, j - TT + 1)
                    nc.vector.tensor_tensor(c.x[:, t, :], c.ps[:, 6 + j % 2, :], c.x[:, t, :], ALU.add).then_inc(added, 1)

        @block.tensor
        def _(pe):
            for e in PE_PLAN:
                if e[0] in "wxh":
                    i = TURNS.index(e)
                    rows, _, unit = turn_rows(e)
                    if unit in UNITS:
                        pe.wait_ge(quantised, UNITS.index(unit) + 1)
                    if i >= 2:
                        pe.wait_ge(moved, i - 1)
                    for k in range(KD):
                        last = nc.tensor.transpose(c.ps[:, i % 2, k * P:(k + 1) * P], rows[:, k * P:(k + 1) * P], c.ident[:])
                    last.then_inc(turned, 1)
                elif e[0] == "up":
                    _, n, t = e
                    j = TT * n + t
                    pe.wait_ge(moved, TURNS.index(("w", 3 * n + 1, 3)) + 1)
                    pe.wait_ge(moved, TURNS.index(("x", t)) + 1)
                    for bank, wT, freed, done_ in ((2 + j % 2, gT, silu_done, g_done), (4 + j % 2, uT, h_done, u_done)):
                        if j >= 2:
                            pe.wait_ge(freed, j - 1)
                        for k in range(KD):
                            last = nc.tensor.matmul(c.ps[:, bank, :], c.xF[:, k, t * P:(t + 1) * P], wT[:, n % 2, k, :],
                                                    start=k == 0, stop=k == KD - 1)
                        last.then_inc(done_, 1)
                else:
                    _, n, t = e
                    j = TT * n + t
                    pe.wait_ge(moved, TURNS.index(("w", 3 * n + 2, 3)) + 1)
                    pe.wait_ge(moved, TURNS.index(("h", n, t)) + 1)
                    if j >= 2:
                        pe.wait_ge(added, j - 1)
                    for k in range(KD):
                        last = nc.tensor.matmul(c.ps[:, 6 + j % 2, :], hF[:, j % 2, k, :], dT[:, n % 2, k, :],
                                                start=k == 0, stop=k == KD - 1)
                    last.then_inc(out_done, 1)

        @block.scalar
        def _(act):
            for e in PE_PLAN:
                if e[0] in "wxh":
                    i = TURNS.index(e)
                    act.wait_ge(turned, i + 1)
                    if e[0] == "w" and e[2] == 0:
                        name, _, n = WJOBS[e[1]]
                        if name != "f_d" and n >= 2:
                            act.wait_ge(g_done, TT * (n - 1))
                            act.wait_ge(u_done, TT * (n - 1))
                        elif name == "f_d" and n >= 2:
                            act.wait_ge(out_done, TT * (n - 1))
                    elif e[0] == "h" and TT * e[1] + e[2] >= 2:
                        act.wait_ge(out_done, TT * e[1] + e[2] - 1)
                    nc.scalar.activation(turn_rows(e)[1], c.ps[:, i % 2, :].rearrange("p (k o) -> p k o", k=KD),
                                         ACT.Copy).then_inc(moved, 1)
                elif e[0] == "up":
                    j = TT * e[1] + e[2]
                    act.wait_ge(g_done, j + 1)
                    if j >= 2:
                        act.wait_ge(h_done, j - 1)
                    nc.scalar.activation(silu[:, j % 2, :], c.ps[:, 2 + j % 2, :], ACT.Silu).then_inc(silu_done, 1)


def store_result(c):
    nc, stored = c.nc, c.stored
    with nc.Block() as block:
        @block.sync
        def _(sp):
            sp.dma_start(tiled(c.out), c.x[:]).then_inc(stored, 16)
            sp.wait_ge(stored, 16)


STAGES = [mixer, cross_attention, experts, linear_attention, gated_cross_attention, mx_feed_forward]


def build(nc, dram, out):
    c = Core(nc, dram, out)
    for stage in (*STAGES, store_result):
        c.stage_sems = []
        stage(c)
        nc.clear_and_free_semaphores(c.stage_sems)
        nc.all_engine_barrier()


def _layout(i):
    c = np.ascontiguousarray
    a = {}
    a["x"] = c(i["x"].reshape(TOK, DM))
    a["c_ident"] = np.eye(P, dtype=np.float32)
    w = i["L0_attn_W_in"]
    a["winx"] = c(w[:1024])
    a["winzT"] = c(w[1024:].T)
    a["convT"] = c(i["L0_attn_conv_w"].T)
    a["woutT"] = c(i["L0_attn_W_out"].T)
    a["Dv"] = c(i["L0_attn_D"].reshape(8, P).T)
    a["ctxT"] = c(i["ctx_2048"].reshape(CTX, DM).T)
    wkv = i["L0_xattn_wkv"]
    a["b_wkT"], a["b_wvT"] = c(wkv[:512].T), c(wkv[512:].T)
    a["b_wq"], a["b_wp"] = c(i["L0_xattn_wq"]), c(i["L0_xattn_wp"])
    bkv = i["L0_xattn_bkv"]
    a["b_bq"], a["b_bk"] = c(i["L0_xattn_bq"].reshape(4, P).T), c(bkv[:512].reshape(4, P).T)
    a["b_bv"], a["b_bp"] = c(bkv[512:]), c(i["L0_xattn_bp"])
    a["c_s1T"], a["c_sgT"], a["c_s2T"] = (c(i[f"L0_ffn_{n}"].T) for n in ("sw1", "swg", "sw2"))
    a["c_wdT"], a["c_wupT"], a["c_wgT"] = (c(i[f"L0_ffn_{n}"].T) for n in ("Wdown", "Wup", "Wg"))
    a["c_r1T"], a["c_rgT"], a["c_r2T"] = (c(i[f"L0_ffn_{n}"].transpose(0, 2, 1)) for n in ("rw1", "rwg", "rw2"))
    a["c_bias"] = c(i["L0_ffn_biases"])
    qkv = i["L1_attn_qkv_w"].reshape(32, 3, 64, DM)

    def by_pair(w):
        return c(w.reshape(16, P, KD, P).transpose(0, 3, 2, 1))
    a["d_wq"], a["d_wk"], a["d_wg"] = by_pair(qkv[:, 0]), by_pair(qkv[:, 1]), by_pair(i["L1_attn_gate_w"])
    a["d_wvT"] = c(qkv[:, 2].reshape(2048, DM).T)
    a["d_woT"] = c(i["L1_attn_out_w"].T)
    a["d_nw"] = c(i["L1_attn_norm_w"].reshape(16, P).T)
    slope = (2.0 ** (-8.0 / 32)) ** np.arange(1, 33) * (1 + 1e-5)
    r = np.arange(1, P + 1)
    gap = r[None, :] - r[:, None]
    mask = np.where(gap[:, None, :] >= 0, np.exp(-slope[None, :, None] * np.maximum(gap, 0)[:, None, :]), 0.0)
    a["d_mask"] = c(mask.astype(np.float32))
    a["d_qdec"] = c(np.repeat(np.exp(-slope[:, None] * r), 64, 0).reshape(16, P, P).transpose(1, 0, 2).astype(np.float32))
    a["d_kdec"] = c(np.exp(-slope[None, :] * (P - r)[:, None]).astype(np.float32))
    a["d_bdec"] = c(np.repeat(np.exp(-slope * P), 64).reshape(16, P).T.astype(np.float32))
    wkv = i["L1_xattn_Wkv"]
    a["e_wkT"], a["e_wvT"] = c(wkv[:512].T), c(wkv[512:].T)
    a["e_wqT"], a["e_wgT"], a["e_woT"] = (c(i[f"L1_xattn_{n}"].T) for n in ("Wq", "Wg", "Wo"))
    a["e_bg"] = c(i["L1_xattn_bg"].reshape(4, P).T)
    head = np.arange(DM) // 32
    a["e_blocks"] = (head[:P, None] == head[None, :P]).astype(np.float32)
    belongs = (head[:, None] == np.arange(16)).astype(np.float32).reshape(KD, P, 16)
    a["e_heads"], a["e_headsT"] = c(belongs.transpose(1, 0, 2)), c(belongs.transpose(2, 0, 1))
    a["f_g"], a["f_u"], a["f_d"] = (c(i[f"L1_ffn_{n}_w"]) for n in ("gate", "up", "down"))
    return a


def kernel(**inputs):
    import concourse.bacc as _bacc
    from concourse.bass_utils import run_bass_kernel_spmd as _run

    nc = _bacc.Bacc("TRN2", target_bir_lowering=False, num_devices=1)
    arrays = {f"in_{k}": v for k, v in _layout({k: np.asarray(v) for k, v in inputs.items()}).items()}
    dram = {k[3:]: nc.dram_tensor(k, v.shape, mybir.dt.from_np(v.dtype), kind="ExternalInput").ap()
            for k, v in arrays.items()}
    out = nc.dram_tensor("out_0", (TOK, DM), F32, kind="ExternalOutput").ap()
    build(nc, dram, out)
    r = _run(nc, [arrays], core_ids=[0])
    return r.results[0]["out_0"].reshape(2, 512, 512)
```
